# Optimizing a Trainium2 kernel written in Bass

```python
import numpy as np
import jax
import jax.numpy as jnp

def _softmax(x, axis=-1):
    return jax.nn.softmax(x, axis=axis)

def _gelu(x):
    return jax.nn.gelu(x, approximate=True)

def _silu(x):
    return jax.nn.silu(x)

def _sigmoid(x):
    return jax.nn.sigmoid(x)

def _layernorm(x, axis=-1, eps=1e-05):
    m = jnp.mean(x, axis=axis, keepdims=True)
    v = jnp.var(x, axis=axis, keepdims=True)
    return (x - m) / jnp.sqrt(v + eps)

def _scatter_add(tgt, idx, src, axis=0):
    return tgt.at[idx].add(src)

def _segment_sum(src, seg, n):
    return jax.ops.segment_sum(src, seg, n)
kernel_name = 'mk_gnn_preln_d4_gnn_r32_5ff42d'

def setup_inputs(seed: int=0):
    np.random.seed(seed)
    _w = jnp.asarray

    def _rec_inputs():
        import jax
        import jax.numpy as jnp
        _gk = jax.random.key(seed)
        x = -6.415e-05 + 1 * jax.random.normal(jax.random.fold_in(_gk, 1), (625, 512), jnp.float32)
        src = jax.random.randint(jax.random.fold_in(_gk, 2), (10000,), 0, 625, jnp.int32)
        dst = jnp.minimum((625 * jax.random.uniform(jax.random.fold_in(_gk, 3), (10000,)) ** 2.0).astype(jnp.int32), 19999)
        _o = jnp.argsort(dst, stable=True)
        src = src[_o]
        dst = dst[_o]
        edge_attr_20 = 0.000389844 + 1.00025 * jax.random.normal(jax.random.fold_in(_gk, 12), (10000, 20), jnp.float32)
        edge_attr_4 = -0.00185629 + 0.998788 * jax.random.normal(jax.random.fold_in(_gk, 13), (10000, 4), jnp.float32)
        edge_attr_8 = -0.000521468 + 0.999954 * jax.random.normal(jax.random.fold_in(_gk, 14), (10000, 8), jnp.float32)
        edge_attr_8_n2 = -0.000521468 + 0.999954 * jax.random.normal(jax.random.fold_in(_gk, 15), (10000, 8), jnp.float32)
        edge_type_2 = jax.random.randint(jax.random.fold_in(_gk, 17), (10000,), 0, 2, jnp.int32)
        edge_weight = jax.random.uniform(jax.random.fold_in(_gk, 18), (10000,), jnp.float32, 0.0, 0.999993)
        return (x, src, dst, edge_attr_20, edge_attr_4, edge_attr_8, edge_attr_8_n2, edge_type_2, edge_weight)
    x, src, dst, edge_attr_20, edge_attr_4, edge_attr_8, edge_attr_8_n2, edge_type_2, edge_weight = _rec_inputs()

    def _L0_gnn_setup():
        import jax, jax.numpy as jnp
        import numpy as np
        N = 625
        E = 20000
        D = 512
        H = 8
        DH = D // H
        EPS = 1e-05

        def layer_norm(x, g, b):
            mu = x.mean(-1, keepdims=True)
            var = ((x - mu) ** 2).mean(-1, keepdims=True)
            return (x - mu) * jax.lax.rsqrt(var + EPS) * g + b
        key = jax.random.key(seed)
        ks = jax.random.split(key, 12)
        return dict(node_feature=jax.random.normal(ks[0], (N, D), jnp.float32), src=jax.random.randint(ks[1], (E,), 0, N, dtype=jnp.int32), dst=jax.random.randint(ks[2], (E,), 0, N, dtype=jnp.int32), dist_attn=jax.random.normal(ks[3], (E, H), jnp.float32), path_attn=jax.random.normal(ks[4], (E, H), jnp.float32), Wqkv=jax.random.normal(ks[5], (D, 3 * D), jnp.float32) / np.float32(np.sqrt(D)), bqkv=jnp.zeros((3 * D,), jnp.float32), Wo=jax.random.normal(ks[6], (D, D), jnp.float32) / np.float32(np.sqrt(D)), bo=jnp.zeros((D,), jnp.float32), ln1_g=jnp.ones((D,), jnp.float32), ln1_b=jnp.zeros((D,), jnp.float32), W1=jax.random.normal(ks[7], (D, 4 * D), jnp.float32) / np.float32(np.sqrt(D)), b1=jnp.zeros((4 * D,), jnp.float32), W2=jax.random.normal(ks[8], (4 * D, D), jnp.float32) / np.float32(np.sqrt(4 * D)), b2=jnp.zeros((D,), jnp.float32), ln2_g=jnp.ones((D,), jnp.float32), ln2_b=jnp.zeros((D,), jnp.float32))
    _L0_gnn_all = _L0_gnn_setup()
    _L0_gnn_in = {k: v for k, v in _L0_gnn_all.items() if k in ('Wqkv', 'bqkv', 'Wo', 'bo', 'ln1_g', 'ln1_b', 'W1', 'b1', 'W2', 'b2', 'ln2_g', 'ln2_b')}
    del _L0_gnn_all

    def _L1_gnn_setup():
        import jax, jax.numpy as jnp
        import numpy as np
        import math
        B = 128
        F = 32
        R = 20
        N = 512
        E = 8192
        LOG2 = 0.6931471805599453
        IS2 = 1.0 / math.sqrt(2.0)
        IS3 = 1.0 / math.sqrt(3.0)
        IS6 = 1.0 / math.sqrt(6.0)

        def ssp(x):
            return jax.nn.softplus(x) - LOG2
        key = jax.random.key(seed)
        ks = jax.random.split(key, 14)
        return dict(x=jax.random.normal(ks[0], (N, 4 * B), jnp.float32), idx_i=jax.random.randint(ks[1], (E,), 0, N), idx_j=jax.random.randint(ks[2], (E,), 0, N), f_ij=jax.random.normal(ks[3], (E, R), jnp.float32), rcut_ij=jax.random.uniform(ks[4], (E,), jnp.float32), Yr_ij=jax.random.normal(ks[5], (E, 4), jnp.float32), w_in2f_s=jax.random.normal(ks[6], (B, F), jnp.float32), w_in2f_v=jax.random.normal(ks[7], (B, F), jnp.float32), W1=jax.random.normal(ks[8], (R, F), jnp.float32) / math.sqrt(R), b1=jnp.zeros((F,), jnp.float32), W2=jax.random.normal(ks[9], (F, 6 * F), jnp.float32) / math.sqrt(F), b2=jnp.zeros((6 * F,), jnp.float32), w_f2o1_s=jax.random.normal(ks[10], (2 * F, B), jnp.float32), w_f2o1_v=jax.random.normal(ks[11], (2 * F, B), jnp.float32), w_f2o2_s=jax.random.normal(ks[12], (B, B), jnp.float32), w_f2o2_v=jax.random.normal(ks[13], (B, B), jnp.float32))
    _L1_gnn_all = _L1_gnn_setup()
    _L1_gnn_in = {k: v for k, v in _L1_gnn_all.items() if k in ('w_in2f_s', 'w_in2f_v', 'W1', 'b1', 'W2', 'b2', 'w_f2o1_s', 'w_f2o1_v', 'w_f2o2_s', 'w_f2o2_v')}
    del _L1_gnn_all

    def _L2_gnn_setup():
        import jax, jax.numpy as jnp
        import numpy as np

        def _mean_agg(h, src, dst, n):
            s = jax.ops.segment_sum(h[src], dst, num_segments=n)
            deg = jax.ops.segment_sum(jnp.ones((src.shape[0],), h.dtype), dst, num_segments=n)
            return s / jnp.maximum(deg, 1.0)[:, None]
        key = jax.random.key(seed)
        ks = jax.random.split(key, 7)
        N, E, D, H, L = (10000, 5000, 512, 512, 3)
        sc = 1.0 / np.sqrt(D)
        return {'feat': jax.random.normal(ks[0], (N, D), jnp.float32), 'src': jax.random.randint(ks[1], (E,), 0, N, jnp.int32), 'dst': jax.random.randint(ks[2], (E,), 0, N, jnp.int32), 'W_init': jax.random.normal(ks[3], (H, D), jnp.float32) * sc, 'W_fwd': jax.random.normal(ks[4], (L, H, H), jnp.float32) * sc, 'W_bwd': jax.random.normal(ks[5], (L, H, H), jnp.float32) * sc, 'W_self': jax.random.normal(ks[6], (L, H, 3 * H), jnp.float32) * (1.0 / np.sqrt(3 * H))}
    _L2_gnn_all = _L2_gnn_setup()
    _L2_gnn_in = {k: v for k, v in _L2_gnn_all.items() if k in ('W_init', 'W_fwd', 'W_bwd', 'W_self')}
    del _L2_gnn_all

    def _L3_gnn_setup():
        import jax, jax.numpy as jnp
        import numpy as np
        NUM_RELATIONS = 2
        NUM_BASES = 30
        HIDDEN = 512
        N_NODES = 10000
        N_EDGES = 5000

        def rgcn_gate_layer(x, row, col, edge_type, basis, att, gate_w, root, bias):
            H = x.shape[1]
            w = jnp.einsum('rb,bio->rio', att, basis)
            x_j = x[col]
            msgs = []
            for r in range(NUM_RELATIONS):
                gate = jax.nn.sigmoid(x_j @ gate_w[r, :, 0])
                msgs.append(gate[:, None] * x_j @ w[r])
            msg = jnp.where((edge_type == 0)[:, None], msgs[0], msgs[1])
            agg = jax.ops.segment_sum(msg, row, num_segments=x.shape[0])
            return agg + x @ root + bias
        key = jax.random.key(seed)
        ks = jax.random.split(key, 16)
        H, R, B = (HIDDEN, NUM_RELATIONS, NUM_BASES)
        bound = 1.0 / np.sqrt(B * H)
        u = lambda k, shape: jax.random.uniform(k, shape, jnp.float32, -bound, bound)
        inp = {'x': jax.random.normal(ks[0], (N_NODES, H), jnp.float32), 'edge_index': jax.random.randint(ks[1], (2, N_EDGES), 0, N_NODES, jnp.int32), 'edge_type': jax.random.randint(ks[2], (N_EDGES,), 0, R, jnp.int32), 'basis1': u(ks[3], (B, H, H)), 'att1': u(ks[4], (R, B)), 'gate_w1': u(ks[5], (R, H, 1)), 'root1': u(ks[6], (H, H)), 'bias1': u(ks[7], (H,)), 'basis2': u(ks[8], (B, H, H)), 'att2': u(ks[9], (R, B)), 'gate_w2': u(ks[10], (R, H, 1)), 'root2': u(ks[11], (H, H)), 'bias2': u(ks[12], (H,))}
        return inp
    _L3_gnn_all = _L3_gnn_setup()
    _L3_gnn_in = {k: v for k, v in _L3_gnn_all.items() if k in ('basis1', 'att1', 'gate_w1', 'root1', 'bias1', 'basis2', 'att2', 'gate_w2', 'root2', 'bias2')}
    del _L3_gnn_all
    return {'x': x, 'src': src, 'dst': dst, 'edge_attr_20': edge_attr_20, 'edge_attr_4': edge_attr_4, 'edge_attr_8': edge_attr_8, 'edge_attr_8_n2': edge_attr_8_n2, 'edge_type_2': edge_type_2, 'edge_weight': edge_weight, 'L0_gnn_Wqkv': _L0_gnn_in['Wqkv'], 'L0_gnn_bqkv': _L0_gnn_in['bqkv'], 'L0_gnn_Wo': _L0_gnn_in['Wo'], 'L0_gnn_bo': _L0_gnn_in['bo'], 'L0_gnn_ln1_g': _L0_gnn_in['ln1_g'], 'L0_gnn_ln1_b': _L0_gnn_in['ln1_b'], 'L0_gnn_W1': _L0_gnn_in['W1'], 'L0_gnn_b1': _L0_gnn_in['b1'], 'L0_gnn_W2': _L0_gnn_in['W2'], 'L0_gnn_b2': _L0_gnn_in['b2'], 'L0_gnn_ln2_g': _L0_gnn_in['ln2_g'], 'L0_gnn_ln2_b': _L0_gnn_in['ln2_b'], 'L1_gnn_w_in2f_s': _L1_gnn_in['w_in2f_s'], 'L1_gnn_w_in2f_v': _L1_gnn_in['w_in2f_v'], 'L1_gnn_W1': _L1_gnn_in['W1'], 'L1_gnn_b1': _L1_gnn_in['b1'], 'L1_gnn_W2': _L1_gnn_in['W2'], 'L1_gnn_b2': _L1_gnn_in['b2'], 'L1_gnn_w_f2o1_s': _L1_gnn_in['w_f2o1_s'], 'L1_gnn_w_f2o1_v': _L1_gnn_in['w_f2o1_v'], 'L1_gnn_w_f2o2_s': _L1_gnn_in['w_f2o2_s'], 'L1_gnn_w_f2o2_v': _L1_gnn_in['w_f2o2_v'], 'L2_gnn_W_init': _L2_gnn_in['W_init'], 'L2_gnn_W_fwd': _L2_gnn_in['W_fwd'], 'L2_gnn_W_bwd': _L2_gnn_in['W_bwd'], 'L2_gnn_W_self': _L2_gnn_in['W_self'], 'L3_gnn_basis1': _L3_gnn_in['basis1'], 'L3_gnn_att1': _L3_gnn_in['att1'], 'L3_gnn_gate_w1': _L3_gnn_in['gate_w1'], 'L3_gnn_root1': _L3_gnn_in['root1'], 'L3_gnn_bias1': _L3_gnn_in['bias1'], 'L3_gnn_basis2': _L3_gnn_in['basis2'], 'L3_gnn_att2': _L3_gnn_in['att2'], 'L3_gnn_gate_w2': _L3_gnn_in['gate_w2'], 'L3_gnn_root2': _L3_gnn_in['root2'], 'L3_gnn_bias2': _L3_gnn_in['bias2']}

def reference(x, src, dst, edge_attr_20, edge_attr_4, edge_attr_8, edge_attr_8_n2, edge_type_2, edge_weight, L0_gnn_Wqkv, L0_gnn_bqkv, L0_gnn_Wo, L0_gnn_bo, L0_gnn_ln1_g, L0_gnn_ln1_b, L0_gnn_W1, L0_gnn_b1, L0_gnn_W2, L0_gnn_b2, L0_gnn_ln2_g, L0_gnn_ln2_b, L1_gnn_w_in2f_s, L1_gnn_w_in2f_v, L1_gnn_W1, L1_gnn_b1, L1_gnn_W2, L1_gnn_b2, L1_gnn_w_f2o1_s, L1_gnn_w_f2o1_v, L1_gnn_w_f2o2_s, L1_gnn_w_f2o2_v, L2_gnn_W_init, L2_gnn_W_fwd, L2_gnn_W_bwd, L2_gnn_W_self, L3_gnn_basis1, L3_gnn_att1, L3_gnn_gate_w1, L3_gnn_root1, L3_gnn_bias1, L3_gnn_basis2, L3_gnn_att2, L3_gnn_gate_w2, L3_gnn_root2, L3_gnn_bias2):
    import jax
    import jax.numpy as jnp

    def _L0_gnn_ref(node_feature, src, dst, dist_attn, path_attn, Wqkv, bqkv, Wo, bo, ln1_g, ln1_b, W1, b1, W2, b2, ln2_g, ln2_b):
        import jax, jax.numpy as jnp
        import numpy as np
        N = 625
        E = 20000
        D = 512
        H = 8
        DH = D // H
        EPS = 1e-05

        def layer_norm(x, g, b):
            mu = x.mean(-1, keepdims=True)
            var = ((x - mu) ** 2).mean(-1, keepdims=True)
            return (x - mu) * jax.lax.rsqrt(var + EPS) * g + b
        h = layer_norm(node_feature, ln1_g, ln1_b)
        qkv = (h @ Wqkv + bqkv).reshape(N, 3, H, DH)
        q = qkv[:, 0] * D ** (-0.5)
        k = qkv[:, 1]
        v = qkv[:, 2]
        logits = jnp.einsum('ehd,ehd->eh', q[src], k[dst])
        a = logits + dist_attn + path_attn
        mx = jax.ops.segment_max(a, dst, num_segments=N)
        e = jnp.exp(a - mx[dst])
        s = jax.ops.segment_sum(e, dst, num_segments=N)
        sa = e / s[dst]
        msg = v[src] * sa[:, :, None]
        agg = jax.ops.segment_sum(msg, dst, num_segments=N).reshape(N, D)
        x = agg @ Wo + bo
        h1 = node_feature + x
        h2 = layer_norm(h1, ln2_g, ln2_b)
        h2 = jax.nn.gelu(h2 @ W1 + b1, approximate=False) @ W2 + b2
        return h1 + h2

    def _L1_gnn_ref(x, idx_i, idx_j, f_ij, rcut_ij, Yr_ij, w_in2f_s, w_in2f_v, W1, b1, W2, b2, w_f2o1_s, w_f2o1_v, w_f2o2_s, w_f2o2_v):
        import jax, jax.numpy as jnp
        import numpy as np
        import math
        B = 128
        F = 32
        R = 20
        N = 512
        E = 8192
        LOG2 = 0.6931471805599453
        IS2 = 1.0 / math.sqrt(2.0)
        IS3 = 1.0 / math.sqrt(3.0)
        IS6 = 1.0 / math.sqrt(6.0)

        def ssp(x):
            return jax.nn.softplus(x) - LOG2
        n = x.shape[0]
        xs = x[:, :B]
        xv = x[:, B:].reshape(n, B, 3)
        hs = xs @ w_in2f_s / math.sqrt(B)
        hv = jnp.einsum('nbc,bf->nfc', xv, w_in2f_v) / math.sqrt(B)
        s = hs[idx_j]
        v = hv[idx_j]
        ys = Yr_ij[:, 0]
        yv = Yr_ij[:, 1:4]
        t_s1 = s * ys[:, None]
        t_s2 = jnp.einsum('efc,ec->ef', v, yv) * IS3
        t_v1 = s[:, :, None] * yv[:, None, :]
        t_v2 = v * ys[:, None, None]
        t_pv = jnp.cross(v, yv[:, None, :]) * IS2
        ax, ay, az = (v[..., 0], v[..., 1], v[..., 2])
        bx, by, bz = (yv[:, None, 0:1], yv[:, None, 1:2], yv[:, None, 2:3])
        bx, by, bz = (bx[..., 0], by[..., 0], bz[..., 0])
        t_q = jnp.stack([(ax * by + ay * bx) * IS2, (ay * bz + az * by) * IS2, (2.0 * az * bz - ax * bx - ay * by) * IS6, (ax * bz + az * bx) * IS2, (ax * bx - ay * by) * IS2], axis=-1)
        h = ssp(f_ij @ W1 + b1)
        Wij = (h @ W2 + b2) * rcut_ij[:, None]
        Wf = Wij.reshape(-1, F, 6)
        edge = jnp.concatenate([(t_s1 * Wf[..., 0])[..., None], (t_s2 * Wf[..., 1])[..., None], t_v1 * Wf[..., 2:3], t_v2 * Wf[..., 3:4], t_pv * Wf[..., 4:5], t_q * Wf[..., 5:6]], axis=-1)
        agg = jax.ops.segment_sum(edge.reshape(edge.shape[0], -1), idx_i, num_segments=n).reshape(n, F, 16)
        s_in = jnp.concatenate([agg[..., 0], agg[..., 1]], axis=1)
        v_in = jnp.concatenate([agg[..., 2:5], agg[..., 5:8]], axis=1)
        os1 = s_in @ w_f2o1_s / math.sqrt(2 * F)
        ov1 = jnp.einsum('nmc,mb->nbc', v_in, w_f2o1_v) / math.sqrt(2 * F)
        os1 = ssp(os1)
        os2 = os1 @ w_f2o2_s / math.sqrt(B)
        ov2 = jnp.einsum('nbc,bd->ndc', ov1, w_f2o2_v) / math.sqrt(B)
        return jnp.concatenate([os2, ov2.reshape(n, -1)], axis=-1)

    def _L2_gnn_ref(feat, src, dst, W_init, W_fwd, W_bwd, W_self):
        import jax, jax.numpy as jnp
        import numpy as np

        def _mean_agg(h, src, dst, n):
            s = jax.ops.segment_sum(h[src], dst, num_segments=n)
            deg = jax.ops.segment_sum(jnp.ones((src.shape[0],), h.dtype), dst, num_segments=n)
            return s / jnp.maximum(deg, 1.0)[:, None]
        n = feat.shape[0]
        h = jax.nn.relu(feat @ W_init.T)
        num_layers = W_fwd.shape[0]
        for l in range(num_layers):
            h_self = h
            fwd_neigh = _mean_agg(h, src, dst, n) @ W_fwd[l].T
            bwd_neigh = _mean_agg(h, dst, src, n) @ W_bwd[l].T
            cat = jnp.concatenate((h_self, fwd_neigh, bwd_neigh), axis=1)
            h = jax.nn.relu(cat @ W_self[l].T)
        return h

    def _L3_gnn_ref(x, edge_index, edge_type, basis1, att1, gate_w1, root1, bias1, basis2, att2, gate_w2, root2, bias2):
        import jax, jax.numpy as jnp
        import numpy as np
        NUM_RELATIONS = 2
        NUM_BASES = 30
        HIDDEN = 512
        N_NODES = 10000
        N_EDGES = 5000

        def rgcn_gate_layer(x, row, col, edge_type, basis, att, gate_w, root, bias):
            H = x.shape[1]
            w = jnp.einsum('rb,bio->rio', att, basis)
            x_j = x[col]
            msgs = []
            for r in range(NUM_RELATIONS):
                gate = jax.nn.sigmoid(x_j @ gate_w[r, :, 0])
                msgs.append(gate[:, None] * x_j @ w[r])
            msg = jnp.where((edge_type == 0)[:, None], msgs[0], msgs[1])
            agg = jax.ops.segment_sum(msg, row, num_segments=x.shape[0])
            return agg + x @ root + bias
        row, col = (edge_index[0], edge_index[1])
        h = jax.nn.relu(rgcn_gate_layer(x, row, col, edge_type, basis1, att1, gate_w1, root1, bias1))
        out = rgcn_gate_layer(h, row, col, edge_type, basis2, att2, gate_w2, root2, bias2)
        return out
    edge_index = jnp.stack([src, dst])
    h = jnp.maximum(_layernorm(x, axis=-1), 0.0)
    x = x + _L0_gnn_ref(h, src, dst, edge_attr_8, edge_attr_8_n2, L0_gnn_Wqkv, L0_gnn_bqkv, L0_gnn_Wo, L0_gnn_bo, L0_gnn_ln1_g, L0_gnn_ln1_b, L0_gnn_W1, L0_gnn_b1, L0_gnn_W2, L0_gnn_b2, L0_gnn_ln2_g, L0_gnn_ln2_b)
    h = jnp.maximum(_layernorm(x, axis=-1), 0.0)
    x = x + _L1_gnn_ref(h, src, dst, edge_attr_20, edge_weight, edge_attr_4, L1_gnn_w_in2f_s, L1_gnn_w_in2f_v, L1_gnn_W1, L1_gnn_b1, L1_gnn_W2, L1_gnn_b2, L1_gnn_w_f2o1_s, L1_gnn_w_f2o1_v, L1_gnn_w_f2o2_s, L1_gnn_w_f2o2_v)
    h = jnp.maximum(_layernorm(x, axis=-1), 0.0)
    x = x + _L2_gnn_ref(h, src, dst, L2_gnn_W_init, L2_gnn_W_fwd, L2_gnn_W_bwd, L2_gnn_W_self)
    h = jnp.maximum(_layernorm(x, axis=-1), 0.0)
    x = x + _L3_gnn_ref(h, edge_index, edge_type_2, L3_gnn_basis1, L3_gnn_att1, L3_gnn_gate_w1, L3_gnn_root1, L3_gnn_bias1, L3_gnn_basis2, L3_gnn_att2, L3_gnn_gate_w2, L3_gnn_root2, L3_gnn_bias2)
    return x

_drawn_inputs = setup_inputs


def setup_inputs(seed=0):
    import zlib

    import numpy as np

    out = dict(_drawn_inputs(seed))
    spreads = {'L0_gnn_bqkv': (0.0, 0.1),
     'L0_gnn_bo': (0.0, 0.1),
     'L0_gnn_ln1_g': (1.0, 0.2),
     'L0_gnn_ln1_b': (0.0, 0.1),
     'L0_gnn_b1': (0.0, 0.1),
     'L0_gnn_b2': (0.0, 0.1),
     'L0_gnn_ln2_g': (1.0, 0.2),
     'L0_gnn_ln2_b': (0.0, 0.1),
     'L1_gnn_b1': (0.0, 0.1),
     'L1_gnn_b2': (0.0, 0.1)}
    factors = {'L3_gnn_basis1': 8.0,
     'L3_gnn_att1': 8.0,
     'L3_gnn_gate_w1': 8.0,
     'L3_gnn_root1': 8.0,
     'L3_gnn_bias1': 26.682,
     'L3_gnn_basis2': 8.0,
     'L3_gnn_att2': 8.0,
     'L3_gnn_gate_w2': 22.281,
     'L3_gnn_root2': 8.0,
     'L3_gnn_bias2': 25.777}
    for name, (base, spread) in spreads.items():
        noise = np.random.default_rng([zlib.crc32(name.encode()), seed]).standard_normal(out[name].shape)
        drawn = base * np.exp(spread * noise) if base else spread * noise
        out[name] = jnp.asarray(drawn.astype(out[name].dtype))
    for name, factor in factors.items():
        out[name] = (out[name] * factor).astype(out[name].dtype)
    return out
```

```python
import concourse.bass as bass
from concourse import mybir
from contextlib import ExitStack

F32 = mybir.dt.float32
BF16 = mybir.dt.bfloat16
I32 = mybir.dt.int32
ALU = mybir.AluOpType
ACT = mybir.ActivationFunctionType
AX = mybir.AxisListType

P = 128
N = 625
E = 10000
D = 512
H = 8
DH = D // H
NC = (N + P - 1) // P
NP = NC * P
LAST = N - (NC - 1) * P
ER = (E + P - 1) // P
ETAIL = E - (ER - 1) * P
NT = (E + NC * (P - 1)) // P + 1
LO_BINS = 32
HI_BINS = 24
BIG = 1.0e30
FEAT = 36
K4 = D // P


class Chain:

    def __init__(self, eng, sem):
        self.eng, self.sem, self.n, self.turn, self.per = eng, sem, 0, None, 0

    def __call__(self, ins):
        self.n += 1
        ins.then_inc(self.sem, 1)
        self.eng.wait_ge(self.sem, self.n if self.turn is None else self.turn * self.per + self.n)

    def enter(self, turn, per):
        self.turn, self.per, self.at = turn, per, self.n

    def leave(self, turns):
        assert self.n - self.at == self.per
        self.n = self.at + turns * self.per
        self.turn = None


class Plan:

    def __init__(self, stages, taken):
        self.taken, self.first, self.by = taken, {}, []
        for name, count, engine in stages:
            self.first[name] = len(self.by)
            self.by += [engine] * count

    def slot(self, ps, name, i):
        j = self.first[name] + i
        return ps[:, 1024 * (j % 4):1024 * (j % 4) + 1024]

    def wait_taken(self, pe, j):
        engine = self.by[j]
        pe.wait_ge(self.taken[engine], self.by[:j + 1].count(engine))

    def open(self, pe, name, i):
        j = self.first[name] + i
        if j >= 4:
            self.wait_taken(pe, j - 4)

    def number(self, name, i):
        return self.first[name] + i + 1


LATER = [("h1T", K4, "act"), ("in2f", NC, "act"), ("attT", NT // 4, "act"), ("hid", 7, "act"), ("filt", NT // 4, "dve"),
         ("f2T", 2, "act"), ("o1", 4, "act"), ("o2", NC, "dve"),
         ("adjT", 2 * NC, "act"), ("deg", 1, "dve"), ("meanT", NC, "act"),
         ("wi", K4, "act"), ("h2T", K4, "act"), ("h0", NC, "act"), ("hT", K4, "act")]
for _l in range(3):
    LATER += [(f"{_n}{_l}", K4, "act") for _n in ("ws", "sf", "cf", "sb", "cb", "F", "B")] + [(f"L{_l}", NC, "act")]
    if _l < 2:
        LATER.append((f"hT{_l}", K4, "act"))
for _l in range(2):
    LATER += [(f"T{_l}", K4, "act"), (f"gate{_l}", NC, "act"), (f"P{_l}0", K4, "act"), (f"P{_l}1", K4, "act"), (f"O{_l}", NC, "dve")]


def build(nc, a, out):
    with ExitStack() as ctx:
        def sb(name, shape, dt=F32):
            return ctx.enter_context(nc.sbuf_tensor(name, shape, dt))

        def sem(name):
            return ctx.enter_context(nc.semaphore(name))

        iota = sb("iota", [P, NP])
        ident = sb("ident", [P, P])
        identb = sb("identb", [P, P], BF16)
        ones = sb("ones", [P, P])
        below = sb("below", [P, P])
        zeros = sb("zeros", [P, 2 * P])
        work = sb("work", [P, 12288])
        fT = sb("fT", [P, K4 * NP])
        sort = fT[0:ER, :].rearrange("p (j t) -> p j t", t=P)
        dsti = sort[:, 0].bitcast(I32)
        srci = sort[:, 1].bitcast(I32)
        enum = sort[:, 2]
        w1 = sort[:, 3]
        w2 = sort[:, 4]
        w2i = sort[:, 5].bitcast(I32)
        key = sort[:, 6]
        keyi = sort[:, 7].bitcast(I32)
        pos = sort[:, 8]
        posi = sort[:, 9].bitcast(I32)
        digi = sort[:, 10:12].bitcast(I32)
        dig = sort[:, 12:14]
        small = sb("small", [ER, 8, LO_BINS])
        chi = sb("chi", [ER, 8], I32)
        onehot = work[0:ER, 0:2048].bitcast(BF16)
        prefix = work[0:ER, 2048:2048 + LO_BINS * P]
        OHW = P + 2 * P
        oneh = work[0:ER, 6144:6144 + 8 * OHW].rearrange("p (s w) -> p s w", w=OHW)
        eidx = sb("eidx", [P, NT], I32)
        srcx = sb("srcx", [P, NT], I32)
        dstx = sb("dstx", [P, NT], I32)
        pay = sb("pay", [P, 2, NT])
        payi = sb("payi", [P, 2, NT], I32)
        real = sb("real", [P, NT])
        rel = sb("rel", [P, NT])
        segk = sb("segk", [P, NT])
        tchunk = sb("tchunk", [ER, NT], I32)
        tch = sb("tch", [ER, 4, NT])
        ps = ctx.enter_context(nc.psum_tensor("ps", [P, 4096], F32))

        s_fill = sem("s_fill")
        s_const = sem("s_const")
        s_edges_in = sem("s_edges_in")
        s_dve = sem("s_dve")
        s_pool = sem("s_pool")
        s_count = sem("s_count")
        s_prefix = sem("s_prefix")
        s_half = [[sem(f"s_half{k}{h}") for h in range(2)] for k in range(2)]
        s_halfused = [[sem(f"s_halfused{k}{h}") for h in range(2)] for k in range(2)]
        s_zeroed = sem("s_zeroed")
        s_permuted = sem("s_permuted")
        s_sorted = sem("s_sorted")

        xs = sb("xs", [P, NC, D])
        hn = sb("hn", [P, NC, D])
        hT = sb("hT", [P, K4, NP])
        bT = sb("bT", [P, K4 * NP])
        aux = sb("aux", [P, 10752])
        wA = sb("wA", [P, 4 * 4 * D])
        att = sb("att", [P, NT * FEAT])
        attr = att[:, :].rearrange("p (t f) -> p t f", f=FEAT)
        nrm = aux[:, 8192:8192 + NC * D].rearrange("p (m n) -> p m n", n=D)
        bst = sb("bst", [P, NC, 6])
        mv = sb("mv", [P, NC, 2])
        var = sb("var", [P, NC])
        std = sb("std", [P, NC])
        rstd = sb("rstd", [P, NC])
        nmr = sb("nmr", [P, NC])
        lng = sb("lng", [P, 2, 2, K4])
        b1c = sb("b1c", [P, 16])
        rows = sb("rows", [P, 2, D])
        bqkv = wA[:, 6144:6144 + 3 * D]
        wqkv = wA[:, 0:K4 * 3 * D].rearrange("p (k n) -> p k n", k=K4)
        ETP, ETJ = 125, E // 125
        etab = aux[0:ETP, 0:ETJ * FEAT].rearrange("p (j f) -> p j f", f=FEAT)
        raw20 = aux[0:ETP, 2880:2880 + 1600].rearrange("p (j f) -> p j f", f=20)
        raw4 = aux[0:ETP, 4480:4480 + 320].rearrange("p (j f) -> p j f", f=4)
        raw8 = aux[0:ETP, 4800:4800 + 640].rearrange("p (j f) -> p j f", f=8)
        raw8b = aux[0:ETP, 5440:5440 + 640].rearrange("p (j f) -> p j f", f=8)
        rawt = aux[0:ETP, 6080:6160].bitcast(I32)
        raww = aux[0:ETP, 6160:6240]
        wo = aux[:, 4096:4096 + K4 * D].rearrange("p (k n) -> p k n", k=K4)
        etab_d = nc.dram_tensor("etab_d", (E, FEAT), F32).ap()
        q_d = nc.dram_tensor("q_d", (NP, D), F32).ap()
        v_d = nc.dram_tensor("v_d", (NP, D), F32).ap()
        ends_d = nc.dram_tensor("ends_d", (112, 5), F32).ap()
        carry_d = nc.dram_tensor("carry_d", (112, 2), F32).ap()
        kS = bT[:, :].rearrange("p (m n) -> p m n", n=D)
        qv = work[:, 0:2 * NC * D].rearrange("p (w m n) -> p w m n", w=2, m=NC)
        NB4 = NT // 4
        hot = work[:, 0:NT * P // 2].bitcast(BF16).rearrange("p (t d) -> p t d", d=P)
        hTf = hT[:, :, :].rearrange("p k n -> p (k n)")
        hot4 = hTf[:, 0:3 * 4 * P].rearrange("p (k n) -> p k n", k=3)
        hotT = hot4[:, 0, :]
        ring = fT[:, 0:4 * D].rearrange("p (s n) -> p s n", n=D)
        msg = work[:, 5888:5888 + 4 * D].rearrange("p (s n) -> p s n", n=D)
        lg = sb("lg", [P, NT, H])
        lga = hTf[:, 1536:1536 + NT * H].rearrange("p (t h) -> p t h", h=H)
        TT, TG = 14, 6
        lgp, kp = (work[:, 5888 + 672 * j:5888 + 672 * (j + 1)].rearrange("p (g t h) -> p g t h", g=TG, t=TT) for j in range(2))
        aT = work[0:112, 7936:7936 + 768]
        kT = work[0:112, 8704:8704 + 768]
        pen = work[0:112, 9472:9472 + 769]
        fwd = work[0:112, 10496:10496 + 768]
        bwd = work[0:112, 11264:11264 + 768]
        ends = sb("ends", [112, 5])
        endh = sb("endh", [H, TT, 5])
        carh = sb("carh", [H, TT, 2])
        chd = sb("chd", [H, 4, TT])
        carry = sb("carry", [112, 2])
        agg = nrm
        sums = sb("sums", [P, NC, H])
        g1T = aux[:, 0:16 * NP].rearrange("p (j n) -> p j n", n=NP)
        w1s = wA[:, :].rearrange("p (k n) -> p k n", k=K4)
        w2s = work[:, 0:16 * D].rearrange("p (k n) -> p k n", k=16)

        s_x = sem("s_x")
        s_xpad = sem("s_xpad")
        s_raw = sem("s_raw")
        s_table = sem("s_table")
        s_etab = sem("s_etab")
        s_par = sem("s_par")
        s_wqkv = sem("s_wqkv")
        s_var = sem("s_var")
        s_std = sem("s_std")
        s_stat = sem("s_stat")
        s_norm = sem("s_norm")
        s_job = sem("s_job")
        s_act = sem("s_act")
        s_by_act = sem("s_by_act")
        s_by_dve = sem("s_by_dve")
        s_q_out = sem("s_q_out")
        s_v_out = sem("s_v_out")
        s_att = sem("s_att")
        s_hot = sem("s_hot")
        s_q_in = [sem(f"s_q_in{j}") for j in range(4)]
        s_q_used = [sem(f"s_q_used{j}") for j in range(4)]
        s_hot4 = sem("s_hot4")
        s_hot4_used = [sem(f"s_hot4_used{k}") for k in range(3)]
        s_soft = sem("s_soft")
        s_h1b = sem("s_h1b")
        s_turned = sem("s_turned")
        s_hotT = sem("s_hotT")
        s_kg = sem("s_kg")
        s_logits = sem("s_logits")
        s_ak = sem("s_ak")
        s_akT = sem("s_akT")
        s_ends = sem("s_ends")
        s_ends_out = sem("s_ends_out")
        s_ends_in = sem("s_ends_in")
        s_carry = sem("s_carry")
        s_carry_out = sem("s_carry_out")
        s_carry_in = sem("s_carry_in")
        s_max = sem("s_max")
        s_maxT = sem("s_maxT")
        s_shift = sem("s_shift")
        s_prob = sem("s_prob")
        s_v_in = [sem(f"s_v_in{j}") for j in range(4)]
        s_msg = [sem(f"s_msg{j}") for j in range(4)]
        s_msg_used = [sem(f"s_msg_used{j}") for j in range(4)]
        s_agg = sem("s_agg")
        s_aggn = sem("s_aggn")
        s_wo = sem("s_wo")
        s_w1 = sem("s_w1")
        s_w2 = sem("s_w2")
        s_resid = sem("s_resid")
        s_pre = sem("s_pre")
        plan = Plan([("ln1T", K4, "act"), ("qkv", 3 * NC, "dve"), ("aggT", K4, "act"), ("wo", NC, "dve"),
                     ("ln2T", K4, "act"), ("ffn1", 16, "act"), ("ffn2", NC, "dve")] + LATER,
                    {"act": s_by_act, "dve": s_by_dve})
        B1, F1, NF = 128, 32, 8 * 32
        half = sb("half", [P, 1])
        zf = wA[:, 0:21 * P]
        tf = wA[:, 21 * P:42 * P]
        small_w = wA[:, 5376:8192]
        w_in = small_w[:, 0:64].rearrange("p (w f) -> p w f", w=2)
        w_f1 = small_w[0:FEAT, 64:96]
        w_f2 = small_w[:, 96:288]
        b_f2 = small_w[:, 288:480]
        w_bd = small_w[:, 1152:1664].rearrange("p (j n) -> p j n", n=P)
        b_fc = small_w[:, 1024:1152]
        w_o1s = small_w[0:64, 480:608]
        w_o1v = small_w[:, 608:736]
        w_o2 = small_w[:, 736:992].rearrange("p (w n) -> p w n", w=2)
        attT = work[0:FEAT, 0:NB4 * 4 * P].rearrange("p (g n) -> p g n", n=4 * P)
        filt = aux[:, :].rearrange("p (t n) -> p t n", n=P)
        uS = bT[:, 0:NC * P].rearrange("p (m n) -> p m n", n=P)
        u_d = nc.dram_tensor("u_d", (NP, P), F32).ap()
        ringu = fT[:, 0:12 * P].rearrange("p (s n) -> p s n", n=P)
        feat = work[:, 5376:5376 + 12 * NF].rearrange("p (s n) -> p s n", n=NF)
        t1, t2, t3 = (work[:, 8448 + 128 * j:8448 + 128 * (j + 1)].rearrange("p (s f) -> p s f", f=F1) for j in range(3))
        t4 = work[:, 8832:8832 + 384].rearrange("p (s c f) -> p s c f", c=3, f=F1)
        t5 = work[:, 9216:9216 + 128].rearrange("p (s f) -> p s f", f=F1)
        agg1 = bT[:, 0:NC * NF].rearrange("p (m n) -> p m n", n=NF)
        oT = bT[:, :].rearrange("p (k n) -> p k n", n=NP)
        tz = fT[:, 0:NP]
        tmask = bT[:, 0:2 * NT].rearrange("p (r t) -> p r t", r=2)
        srcf = sb("srcf", [P, NT])
        hotL = [work[:, 0:2560], work[:, 2560:5120], hTf[:, 0:2560]]
        hotL = [h.rearrange("p (j n) -> p j n", n=NP) for h in hotL]
        hotS = fT[:, 0:4 * NP // 2].bitcast(BF16).rearrange("p (s n) -> p s n", n=NP)
        hotD = fT[:, 2 * NP:2 * NP + 4 * P // 2].bitcast(BF16).rearrange("p (s n) -> p s n", n=P)
        adj = [work[:, 3200 * r:3200 * (r + 1)].rearrange("p (i n) -> p i n", n=NP) for r in range(2)]
        adjT = [aux[:, 3200 * r:3200 * (r + 1)].rearrange("p (i n) -> p i n", n=NP) for r in range(2)]
        deg = sb("deg", [P, NC])
        degd = fT[:, 0:NP]
        meanf = wA[:, 0:3200].rearrange("p (i n) -> p i n", n=NP)
        meanb = wA[:, 3200:6400].rearrange("p (i n) -> p i n", n=NP)
        LAYERS = 3

        def square(at):
            return work[:, at:at + K4 * D].rearrange("p (k n) -> p k n", n=D)
        wn, cf, cb, sfT, wsT, raw = (square(2048 * j) for j in range(6))
        fTv = fT[:, :].rearrange("p (k n) -> p k n", n=NP)
        bTv = bT[:, :].rearrange("p (k n) -> p k n", n=NP)
        NBASE = 30
        attb = sb("attb", [P, 2, 2 * NBASE])
        gw = sb("gw", [P, 2, 2, K4])
        gate = sb("gate", [P, NC, 2])
        root = [square(0), square(2048)]
        acc = [aux[:, 6400:6400 + 4096].rearrange("p (r n) -> p r n", r=2),
               work[:, 4096:8192].rearrange("p (r n) -> p r n", r=2)]
        bas = [att[:, 0:1024], att[:, 1024:2048], wA[:, 6400:7424]]
        gx = wA[:, 0:2 * NC * D].rearrange("p (r m n) -> p r m n", r=2, m=NC)

        s_f1zero = sem("s_f1zero")
        s_l1w = sem("s_l1w")
        s_is3 = sem("s_is3")
        s_z = sem("s_z")
        s_ssp = sem("s_ssp")
        s_u_out = sem("s_u_out")
        s_u_in = [sem(f"s_u_in{j}") for j in range(12)]
        s_u_used = [sem(f"s_u_used{k}") for k in range(3)]
        s_feat = sem("s_feat")
        s_feat_used = [sem(f"s_feat_used{k}") for k in range(3)]
        s_agg1 = sem("s_agg1")
        s_tz = sem("s_tz")
        s_hs = [sem(f"s_hs{j}") for j in range(4)]
        s_hs_used = [sem(f"s_hs_used{j}") for j in range(4)]
        s_counts = sem("s_counts")
        s_adj = sem("s_adj")
        s_mean = sem("s_mean")
        s_rawin = sem("s_rawin")
        s_wnin = sem("s_wnin")
        s_free = sem("s_free")
        s_bas_in = [sem(f"s_bas_in{j}") for j in range(3)]
        s_bas_used = [sem(f"s_bas_used{j}") for j in range(3)]
        s_rel = sem("s_rel")
        s_l3par = sem("s_l3par")
        s_root = sem("s_root")
        s_gate = sem("s_gate")
        s_gx = sem("s_gx")
        s_h3 = sem("s_h3")
        s_x3 = sem("s_x3")
        s_xb = sem("s_xb")
        s_out = sem("s_out")

        block = ctx.enter_context(nc.Block())

        @block.sync
        def _(sp):
            sp.wait_ge(s_fill, 2)
            for dst_tile, name in ((dsti, "dst"), (srci, "src")):
                full = a[name][0:(ER - 1) * P].rearrange("(p t) -> p t", t=P)
                tail = a[name][(ER - 1) * P:E].rearrange("(p t) -> p t", p=1)
                sp.dma_start(dst_tile[0:ER - 1, :], full).then_inc(s_edges_in, 16)
                sp.dma_start(dst_tile[ER - 1:ER, 0:ETAIL], tail).then_inc(s_edges_in, 16)

            sp.wait_ge(s_xpad, 1)
            sp.dma_start(xs[:, 0:NC - 1, :], a["x"][0:(NC - 1) * P].rearrange("(m p) n -> p m n", p=P)).then_inc(s_x, 16)
            sp.dma_start(xs[0:LAST, NC - 1, :], a["x"][(NC - 1) * P:N]).then_inc(s_x, 16)
            for t, name in ((raw20, "edge_attr_20"), (raw4, "edge_attr_4"), (raw8, "edge_attr_8"), (raw8b, "edge_attr_8_n2")):
                sp.dma_start(t, a[name].rearrange("(p j) f -> p j f", p=ETP)).then_inc(s_raw, 16)
            sp.dma_start(rawt, a["edge_type_2"].rearrange("(p j) -> p j", p=ETP)).then_inc(s_raw, 16)
            sp.dma_start(raww, a["edge_weight"].rearrange("(p j) -> p j", p=ETP)).then_inc(s_raw, 16)
            sp.dma_start(wqkv, a["L0_gnn_Wqkv"].rearrange("(k p) n -> p k n", p=P)).then_inc(s_wqkv, 16)
            sp.dma_start(bqkv, a["L0_gnn_bqkv"].rearrange("(o n) -> o n", o=1).to_broadcast([P, 3 * D])).then_inc(s_wqkv, 16)
            with nc.allow_non_contiguous_dma(reason="a few columns of parameters"):
                for j, name in enumerate(("L0_gnn_ln1_g", "L0_gnn_ln1_b", "L0_gnn_ln2_g", "L0_gnn_ln2_b")):
                    sp.dma_start(lng[:, j // 2, j % 2, :], a[name].rearrange("(k p) -> p k", p=P)).then_inc(s_par, 16)
                sp.dma_start(b1c[:, :], a["L0_gnn_b1"].rearrange("(k p) -> p k", p=P)).then_inc(s_par, 16)
            for j, name in enumerate(("L0_gnn_bo", "L0_gnn_b2")):
                sp.dma_start(rows[:, j, :], a[name].rearrange("(o n) -> o n", o=1).to_broadcast([P, D])).then_inc(s_par, 16)
            sp.wait_ge(s_table, 1)
            sp.dma_start(etab_d.rearrange("(p j) f -> p j f", p=ETP), etab).then_inc(s_etab, 16)
            sp.wait_ge(s_by_dve, NC)
            sp.dma_start(q_d.rearrange("(m p) n -> p m n", p=P), qv[:, 0]).then_inc(s_q_out, 16)
            sp.wait_ge(s_by_dve, 3 * NC)
            sp.dma_start(v_d.rearrange("(m p) n -> p m n", p=P), qv[:, 1]).then_inc(s_v_out, 16)
            sp.wait_ge(s_etab, 16)
            sp.dma_start(wo, a["L0_gnn_Wo"].rearrange("(k p) n -> p k n", p=P)).then_inc(s_wo, 16)
            sp.dma_start(w1s, a["L0_gnn_W1"].rearrange("(k p) n -> p k n", p=P)).then_inc(s_w1, 16)
            with nc.allow_non_contiguous_dma(reason="a few numbers a block"):
                sp.wait_ge(s_ends, 1)
                sp.dma_start(ends_d, ends[:, :]).then_inc(s_ends_out, 16)
                sp.wait_ge(s_ends_out, 16)
                sp.dma_start(endh[:, :, :], ends_d.rearrange("(t h) v -> h t v", h=H)).then_inc(s_ends_in, 16)
                sp.wait_ge(s_carry, 1)
                sp.dma_start(carry_d.rearrange("(t h) v -> h t v", h=H), carh[:, :, :]).then_inc(s_carry_out, 16)
                sp.wait_ge(s_carry_out, 16)
                sp.dma_start(carry[:, :], carry_d).then_inc(s_carry_in, 16)
            sp.wait_ge(s_agg, 1)
            sp.dma_start(w2s, a["L0_gnn_W2"].rearrange("(k p) n -> p k n", p=P)).then_inc(s_w2, 16)
            sp.wait_ge(s_f1zero, 1)
            for w, name in ((w_in[:, 0], "w_in2f_s"), (w_in[:, 1], "w_in2f_v"), (w_f1[0:20], "W1"), (w_o1s, "w_f2o1_s"),
                            (w_o1v[0:64], "w_f2o1_v"), (w_o1v[64:128], "w_f2o1_v"), (w_o2[:, 0], "w_f2o2_s"), (w_o2[:, 1], "w_f2o2_v")):
                sp.dma_start(w, a["L1_gnn_" + name]).then_inc(s_l1w, 16)
            sp.dma_start(w_f1[33:34], a["L1_gnn_b1"].rearrange("(o n) -> o n", o=1)).then_inc(s_l1w, 16)
            for j in range(4):
                sp.dma_start(w_f2[F1 * j:F1 * (j + 1)], a["L1_gnn_W2"]).then_inc(s_l1w, 16)
            sp.dma_start(b_f2, a["L1_gnn_b2"].rearrange("(o n) -> o n", o=1).to_broadcast([P, 192])).then_inc(s_l1w, 16)
            sp.wait_ge(s_by_act, plan.by[:plan.number("in2f", NC - 1)].count("act"))
            sp.dma_start(u_d.rearrange("(m p) n -> p m n", p=P), uS).then_inc(s_u_out, 16)
            for l in range(2):
                sp.dma_start(attb[:, l, :], a[f"L3_gnn_att{l + 1}"].rearrange("r b -> (r b)").rearrange("(o n) -> o n", o=1).to_broadcast([P, 2 * NBASE])).then_inc(s_l3par, 16)
                sp.dma_start(rows[:, l, :], a[f"L3_gnn_bias{l + 1}"].rearrange("(o n) -> o n", o=1).to_broadcast([P, D])).then_inc(s_l3par, 16)
                with nc.allow_non_contiguous_dma(reason="a few columns of parameters"):
                    for r in range(2):
                        sp.dma_start(gw[:, l, r, :], a[f"L3_gnn_gate_w{l + 1}"][r, :, 0].rearrange("(k p) -> p k", p=P)).then_inc(s_l3par, 16)
            sp.wait_ge(s_job, plan.number("o2", NC - 1))
            sp.dma_start(raw, a["L2_gnn_W_init"].rearrange("(k p) n -> p k n", p=P)).then_inc(s_rawin, 16)
            sp.wait_ge(s_mean, 2)
            for l in range(LAYERS):
                before = ("wi", f"sb{l - 1}")[l > 0]
                for part, now in enumerate(("ws", "sf", "sb")):
                    sp.wait_ge(s_job, plan.number(before, K4 - 1))
                    sp.dma_start(raw, a["L2_gnn_W_self"][l, :, part * D:(part + 1) * D].rearrange("(k p) n -> p k n", p=P)).then_inc(s_rawin, 16)
                    before = f"{now}{l}"
                    if part:
                        if part == 2:
                            sp.wait_ge(s_job, plan.number(f"cf{l}", K4 - 1))
                        elif l:
                            sp.wait_ge(s_job, plan.number(f"cb{l - 1}", K4 - 1))
                        sp.dma_start(wn, a["L2_gnn_W_" + ("fwd", "bwd")[part - 1]][l].rearrange("(k p) n -> p k n", p=P)).then_inc(s_wnin, 16)
            sp.wait_ge(s_job, plan.number(f"L{LAYERS - 1}", NC - 1))
            for l in range(2):
                sp.dma_start(root[l], a[f"L3_gnn_root{l + 1}"].rearrange("(k p) n -> p k n", p=P)).then_inc(s_root, 16)
            sp.wait_ge(s_by_dve, plan.by.count("dve"))
            sp.dma_start(out[0:(NC - 1) * P].rearrange("(m p) n -> p m n", p=P), xs[:, 0:NC - 1, :]).then_inc(s_out, 16)
            sp.dma_start(out[(NC - 1) * P:N], xs[0:LAST, NC - 1, :]).then_inc(s_out, 16)
            sp.wait_ge(s_out, 32)

        @block.gpsimd
        def _(pool):
            step = Chain(pool, s_pool)
            pool.memset(dsti[:, :], NP).then_inc(s_fill, 1)
            pool.memset(srci[:, :], 0).then_inc(s_fill, 1)
            step(pool.iota(iota[:, :], pattern=[[1, NP]], base=0, channel_multiplier=0,
                           allow_small_or_imprecise_dtypes=True))
            step(pool.iota(enum[:, :], pattern=[[1, P]], base=1, channel_multiplier=P,
                           allow_small_or_imprecise_dtypes=True))
            step(pool.memset(ones[:, :], 1.0))
            step(pool.memset(zeros[:, :], 0.0))
            for m in (ident, identb):
                step(pool.memset(m[:, :], 0.0))
                step(pool.affine_select(out=m[:, :], in_=m[:, :], compare_op=ALU.not_equal, fill=1.0,
                                        base=0, pattern=[[-1, P]], channel_multiplier=1))
            pool.affine_select(out=below[:, :], in_=ones[:, :], compare_op=ALU.is_gt, fill=0.0,
                               base=0, pattern=[[1, P]], channel_multiplier=-1).then_inc(s_const, 1)

            pool.memset(xs[:, NC - 1, :], 0.0).then_inc(s_xpad, 1)
            pool.wait_ge(s_raw, 96)
            pool.tensor_copy(etab[:, :, 0:20], raw20)
            pool.tensor_tensor(etab[:, :, 20:24], raw4, raww.unsqueeze(2).to_broadcast([ETP, ETJ, 4]), ALU.mult)
            pool.tensor_tensor(etab[:, :, 24:32], raw8, raw8b, ALU.add)
            pool.tensor_copy(etab[:, :, 32], rawt)
            step(pool.memset(etab[:, :, 33:34], 1.0))
            pool.memset(etab[:, :, 34:36], 0.0).then_inc(s_table, 1)
            pool.wait_ge(s_sorted, 1)
            pool.wait_ge(s_etab, 16)
            for t in range(NT):
                pool.indirect_dma_start(out=attr[:, t, :], out_offset=None, in_=etab_d,
                                        in_offset=bass.IndirectOffsetOnAxis(ap=eidx[:, t:t + 1], axis=0)).then_inc(s_att, 16)
            pool.wait_ge(s_norm, 2)
            pool.wait_ge(s_par, 7 * 16)
            pool.tensor_tensor(hn[:, :, :], hn[:, :, :], rows[:, 0, :].unsqueeze(1).to_broadcast([P, NC, D]), ALU.add).then_inc(s_h1b, 1)
            pool.wait_ge(s_q_out, 16)
            for t in range(NT):
                if t >= 4:
                    pool.wait_ge(s_q_used[t % 4], t // 4)
                pool.indirect_dma_start(out=ring[:, t % 4, :], out_offset=None, in_=q_d,
                                        in_offset=bass.IndirectOffsetOnAxis(ap=srcx[:, t:t + 1], axis=0)).then_inc(s_q_in[t % 4], 16)
            pool.wait_ge(s_v_out, 16)
            for t in range(NT):
                if t >= 4:
                    pool.wait_ge(s_msg[t % 4], t // 4)
                else:
                    pool.wait_ge(s_q_used[t % 4], NT // 4)
                pool.indirect_dma_start(out=ring[:, t % 4, :], out_offset=None, in_=v_d,
                                        in_offset=bass.IndirectOffsetOnAxis(ap=srcx[:, t:t + 1], axis=0)).then_inc(s_v_in[t % 4], 16)
            pool.wait_ge(s_norm, 3)
            step(pool.tensor_tensor(xs[:, :, :], xs[:, :, :], hn[:, :, :], ALU.add))
            pool.tensor_tensor(xs[:, :, :], xs[:, :, :], rows[:, 1, :].unsqueeze(1).to_broadcast([P, NC, D]), ALU.add).then_inc(s_resid, 1)
            pool.memset(half[:, :], 0.5)
            pool.wait_ge(s_job, plan.number("ffn1", 15))
            pool.memset(w_f1, 0.0).then_inc(s_f1zero, 1)
            pool.wait_ge(s_l1w, 14 * 16)
            pool.tensor_scalar(w_o1s[32:64], w_o1s[32:64], 3.0 ** -0.5, None, ALU.mult).then_inc(s_is3, 1)
            pool.wait_ge(s_u_out, 16)
            for t in range(NT):
                if t >= 12:
                    pool.wait_ge(s_u_used[t // 4 % 3], t // 12)
                pool.indirect_dma_start(out=ringu[:, t % 12, :], out_offset=None, in_=u_d,
                                        in_offset=bass.IndirectOffsetOnAxis(ap=dstx[:, t:t + 1], axis=0)).then_inc(s_u_in[t % 12], 16)
            for l in range(2):
                if l == 0:
                    pool.wait_ge(s_free, 1)
                    pool.wait_ge(s_mean, 2)
                halves = a[f"L3_gnn_basis{l + 1}"].rearrange("b (c k p) n -> b c p k n", c=2, p=P)
                with pool.Fori(0, NBASE // 3) as i:
                    for u in range(6):
                        pool.wait_ge(s_bas_used[u % 3], i * 2 + (l * 2 * NBASE // 3 + u // 3))
                        pool.dma_start(bas[u % 3].rearrange("p (o k n) -> p o k n", o=1, k=2),
                                       halves[bass.ds(i * 3 + u // 2, 1), u % 2].rearrange("o p k n -> p o k n")).then_inc(s_bas_in[u % 3], 16)
            pool.wait_ge(s_norm, 6)
            pool.wait_ge(s_l3par, 8 * 16)
            pool.tensor_tensor(xs[:, :, :], xs[:, :, :], rows[:, 1, :].unsqueeze(1).to_broadcast([P, NC, D]), ALU.add).then_inc(s_xb, 1)

        @block.scalar
        def _(act):
            step = Chain(act, s_act)

            def norm(turn, dst, src, func):
                act.wait_ge(s_var, turn + 1)
                act.activation(std[:, :], var[:, :], ACT.Sqrt).then_inc(s_std, 1)
                act.wait_ge(s_stat, turn + 1)
                for m in range(NC):
                    last = act.activation(dst[:, m, :], src[:, m, :], func, bias=nmr[:, m:m + 1], scale=rstd[:, m:m + 1])
                last.then_inc(s_norm, 1)

            def take_turned(name, dst, count=K4, scale=None, shift=None):
                for k in range(count):
                    act.wait_ge(s_job, plan.number(name, k))
                    o = plan.slot(ps, name, k)[:, 0:NP]
                    if scale is None:
                        act.activation(dst[:, k, :], o, ACT.Copy).then_inc(s_by_act, 1)
                    else:
                        act.activation(dst[:, k, :], o, ACT.Identity, bias=shift[:, k:k + 1], scale=scale[:, k:k + 1]).then_inc(s_by_act, 1)

            norm(0, hn, xs, ACT.Relu)
            norm(1, nrm, hn, ACT.Identity)
            act.wait_ge(s_par, 7 * 16)
            take_turned("ln1T", hT, scale=lng[:, 0, 0, :], shift=lng[:, 0, 1, :])
            with act.Fori(0, NB4) as i:
                act.wait_ge(s_turned, i + 1)
                act.activation(hotT, ps[:, 0:4 * P], ACT.Copy).then_inc(s_hotT, 1)
            act.wait_ge(s_akT, 1)
            act.activation(aT, ps[0:112, 0:768], ACT.Copy).then_inc(s_ak, 1)
            act.wait_ge(s_akT, 2)
            act.activation(kT, ps[0:112, 1024:1024 + 768], ACT.Copy).then_inc(s_ak, 1)
            act.wait_ge(s_shift, 1)
            act.activation(lg[:, :, :], lga[:, :, :], ACT.Exp).then_inc(s_prob, 1)

            def widen(base):
                with act.Fori(0, NB4 // 3) as i:
                    for k in range(3):
                        act.wait_ge(s_hot4_used[k], i + base)
                        act.activation(hot4[:, k, :].rearrange("p (t d) -> p t d", d=P),
                                       hot[:, bass.ds(i * 12 + 4 * k, 4), :], ACT.Copy).then_inc(s_hot4, 1)

            widen(0)
            take_turned("aggT", hT)
            norm(2, nrm, hn, ACT.Identity)
            take_turned("ln2T", hT, scale=lng[:, 1, 0, :], shift=lng[:, 1, 1, :])
            for j in range(16):
                act.wait_ge(s_job, plan.number("ffn1", j))
                act.activation(g1T[:, j, :], plan.slot(ps, "ffn1", j)[:, 0:NP], ACT.Gelu, bias=b1c[:, j:j + 1]).then_inc(s_by_act, 1)

            def take(name, j, dst, width=D, func=ACT.Copy, **how):
                act.wait_ge(s_job, plan.number(name, j))
                act.activation(dst, plan.slot(ps, name, j)[:, 0:width], func, **how).then_inc(s_by_act, 1)

            def softplus(z, t):
                step(act.activation(t, z, ACT.Abs))
                step(act.activation(t, t, ACT.Exp, scale=-1.0))
                act.activation(t, t, ACT.Ln, scale=0.5, bias=half[:, :]).then_inc(s_z, 1)

            norm(3, hn, xs, ACT.Relu)
            take_turned("h1T", hT)
            for m in range(NC):
                take("in2f", m, uS[:, m, :], P, scale=float(B1) ** -0.5)
            for g in range(NB4):
                act.wait_ge(s_job, plan.number("attT", g))
                act.activation(attT[:, g, :], plan.slot(ps, "attT", g)[0:FEAT, 0:4 * P], ACT.Copy).then_inc(s_by_act, 1)
            for g in range(7):
                take("hid", g, zf[:, 3 * P * g:3 * P * (g + 1)], 3 * P)
            act.wait_ge(s_by_act, plan.by[:plan.number("hid", 6)].count("act"))
            act.wait_ge(s_is3, 1)
            softplus(zf, tf)
            act.wait_ge(s_agg, 2)
            act.activation(agg1, ps[:, 0:NC * 512].rearrange("p (m n) -> p m n", n=512)[:, :, 0:NF], ACT.Copy).then_inc(s_agg1, 1)
            take_turned("f2T", hT, 2)
            for k in range(4):
                take("o1", k, oT[:, k, :], NP, scale=0.125)
            act.wait_ge(s_by_act, plan.by[:plan.number("o1", 3)].count("act"))
            softplus(oT[:, 0, :], tz)
            for r in range(2):
                act.wait_ge(s_counts, r + 1)
                act.activation(adj[r][:, 0:4, :].rearrange("p i (c q) -> p i c q", q=P),
                               ps[:, 0:2560].rearrange("p (c i q) -> p i c q", i=4, q=P), ACT.Copy)
                act.activation(adj[r][:, 4, :], ps[:, 2560:2560 + NP], ACT.Copy).then_inc(s_adj, 1)
            for r in range(2):
                for c in range(NC):
                    take("adjT", r * NC + c, adjT[r][:, c, :], NP)
            for c in range(NC):
                take("meanT", c, meanb[:, c, :], NP)
            norm(4, hn, xs, ACT.Relu)
            for k in range(K4):
                take("wi", k, wsT[:, k, :])
            take_turned("h2T", hT)
            for m in range(NC):
                take("h0", m, hn[:, m, :], func=ACT.Relu)
            take_turned("hT", hT)
            act.wait_ge(s_mean, 2)
            for l in range(LAYERS):
                for name, dst in (("ws", wsT), ("sf", sfT), ("cf", cf), ("sb", sfT), ("cb", cb)):
                    for k in range(K4):
                        take(f"{name}{l}", k, dst[:, k, :])
                take_turned(f"F{l}", fTv)
                take_turned(f"B{l}", bTv)
                for m in range(NC):
                    take(f"L{l}", m, hn[:, m, :], func=ACT.Relu)
                if l < LAYERS - 1:
                    take_turned(f"hT{l}", hT)
            norm(5, hn, xs, ACT.Relu)
            for l in range(2):
                take_turned(f"T{l}", hT)
                for m in range(NC):
                    take(f"gate{l}", m, gate[:, m, :], 2, ACT.Sigmoid)
                act.wait_ge(s_by_act, plan.by[:plan.number(f"gate{l}", NC - 1)].count("act"))
                for r in range(2):
                    for m in range(NC):
                        last = act.activation(gx[:, r, m, :], hn[:, m, :], ACT.Copy, scale=gate[:, m, r:r + 1])
                    last.then_inc(s_gx, 1)
                take_turned(f"P{l}0", fTv)
                take_turned(f"P{l}1", bTv)

        @block.vector
        def _(dve):
            step = Chain(dve, s_dve)

            def rank(turn, bins):
                oh = onehot[:, 0:bins * P].rearrange("p (b t) -> p b t", t=P)
                pre = prefix[:, 0:bins * P].rearrange("p (b t) -> p b t", t=P)
                end, cnt, tot, excl, off, incl = (small[:, j, 0:bins] for j in range(6))
                step(dve.tensor_tensor(oh, key[:, :].unsqueeze(1).to_broadcast([ER, bins, P]),
                                       iota[0:ER, 0:bins].unsqueeze(2).to_broadcast([ER, bins, P]), ALU.is_equal))
                step(dve.tensor_tensor_scan(prefix[:, 0:bins * P], onehot[:, 0:bins * P], onehot[:, 0:bins * P],
                                            0.0, ALU.add, ALU.max))
                step(dve.tensor_copy(end, pre[:, :, P - 1]))
                step(dve.tensor_copy(cnt, end))
                dve.tensor_tensor(cnt[:, 1:bins], end[:, 1:bins], end[:, 0:bins - 1], ALU.subtract).then_inc(s_count, 1)
                dve.wait_ge(s_count, turn + 1)
                dve.wait_ge(s_prefix, turn + 1)
                above, every = ps[0:ER, 0:bins], ps[0:ER, 64:64 + bins]
                step(dve.tensor_copy(tot, every))
                step(dve.tensor_tensor_scan(incl, tot, tot, 0.0, ALU.add, ALU.max))
                step(dve.tensor_tensor(excl, incl, tot, ALU.subtract))
                step(dve.scalar_tensor_tensor(off, above, -1.0, cnt, ALU.add, ALU.add))
                step(dve.tensor_tensor(off, off, end, ALU.subtract))
                step(dve.tensor_tensor(off, off, excl, ALU.add))
                if turn == 1:
                    nch = bins // 4
                    ctot, cincl, cexcl = (small[:, 6, 8 * j:8 * j + nch] for j in range(3))
                    step(dve.tensor_reduce(ctot, tot.rearrange("p (c b) -> p c b", b=4), AX.X, ALU.add))
                    ci = chi[:, 0:nch]
                    step(dve.tensor_scalar(ci, ctot, float(P - 1), None, ALU.add))
                    step(dve.tensor_scalar(ci, ci, 7, 7, ALU.arith_shift_right, ALU.arith_shift_left))
                    step(dve.tensor_copy(ctot, ci))
                    step(dve.tensor_tensor_scan(cincl, ctot, ctot, 0.0, ALU.add, ALU.max))
                    step(dve.tensor_tensor(cexcl, cincl, ctot, ALU.subtract))
                    off4 = off.rearrange("p (c b) -> p c b", b=4)
                    first = excl.rearrange("p (c b) -> p c b", b=4)[:, :, 0]
                    step(dve.tensor_tensor(cincl, cexcl, first, ALU.subtract))
                    step(dve.tensor_tensor(off4, off4, cincl.unsqueeze(2).to_broadcast([ER, nch, 4]), ALU.add))
                    step(dve.tensor_scalar(cexcl, cexcl, 1.0 / P, None, ALU.mult))
                    step(dve.tensor_tensor(tch[:, :, :], iota[0:ER, 0:NT].unsqueeze(1).to_broadcast([ER, 4, NT]),
                                           cexcl[:, 1:NC].unsqueeze(2).to_broadcast([ER, NC - 1, NT]), ALU.is_ge))
                    step(dve.tensor_reduce(key[:, 0:NT], tch[:, :, :].rearrange("p c t -> p t c"), AX.X, ALU.add))
                    step(dve.tensor_copy(tchunk[:, :], key[:, 0:NT]))
                step(dve.tensor_tensor(pre, pre, off.unsqueeze(2).to_broadcast([ER, bins, P]), ALU.add))
                step(dve.tensor_tensor(pre, pre, oh, ALU.mult))
                step(dve.tensor_reduce(pos[:, :], pre.rearrange("p b t -> p t b"), AX.X, ALU.add))
                step(dve.tensor_copy(posi[:, :], pos[:, :]))
                step(dve.tensor_scalar(digi[:, 0, :], posi[:, :], 7, None, ALU.arith_shift_right))
                step(dve.tensor_scalar(digi[:, 1, :], posi[:, :], P - 1, None, ALU.bitwise_and))
                step(dve.tensor_copy(dig[:, :, :], digi[:, :, :]))

            def move(turn, by, rows, cols):
                with dve.Fori(0, P // 8) as i:
                    for half in range(2):
                        dve.wait_ge(s_halfused[turn][half], i)
                        for j in range(4):
                            at = bass.ds(i * 8 + (4 * half + j), 1)
                            o = oneh[:, 4 * half + j, :]
                            dve.tensor_scalar(o[:, 0:rows], iota[0:ER, 0:rows], dig[:, by, at], None, ALU.is_equal)
                            dve.tensor_scalar(o[:, P:P + cols], iota[0:ER, 0:cols], dig[:, 1 - by, at],
                                              w1[:, at], ALU.is_equal, ALU.mult)
                            last = dve.tensor_scalar(o[:, 2 * P:2 * P + cols], iota[0:ER, 0:cols], dig[:, 1 - by, at],
                                                     w2[:, at], ALU.is_equal, ALU.mult)
                        last.then_inc(s_half[turn][half], 1)

            dve.wait_ge(s_edges_in, 64)
            dve.wait_ge(s_const, 1)
            step(dve.scalar_tensor_tensor(w2[:, :], srci[:, :], 1024.0, dsti[:, :], ALU.mult, ALU.add))
            step(dve.scalar_tensor_tensor(w1[:, :], dsti[:, :], float(NP), enum[:, :], ALU.is_lt, ALU.mult))
            step(dve.tensor_scalar(keyi[:, :], dsti[:, :], LO_BINS - 1, None, ALU.bitwise_and))
            step(dve.tensor_copy(key[:, :], keyi[:, :]))
            rank(0, LO_BINS)
            move(0, 0, ER, P)
            dve.wait_ge(s_permuted, 1)
            step(dve.tensor_copy(w1[:, :], ps[0:ER, 512:512 + P]))
            step(dve.tensor_copy(w2i[:, :], ps[0:ER, 512 + P:512 + 2 * P]))
            step(dve.tensor_scalar(keyi[:, :], w2i[:, :], 5, 31, ALU.arith_shift_right, ALU.bitwise_and))
            step(dve.tensor_copy(key[:, :], keyi[:, :]))
            step(dve.scalar_tensor_tensor(w2[:, :], w1[:, :], 0.0, w2i[:, :], ALU.is_gt, ALU.mult))
            rank(1, HI_BINS)
            move(1, 1, P, NT)
            dve.wait_ge(s_permuted, 2)
            step(dve.tensor_copy(pay[:, 0, :], ps[:, 1024:1024 + NT]))
            step(dve.tensor_copy(payi[:, 1, :], ps[:, 1024 + NT:1024 + 2 * NT]))
            step(dve.tensor_scalar(eidx[:, :], pay[:, 0, :], -1.0, 0.0, ALU.add, ALU.max))
            step(dve.tensor_scalar(real[:, :], pay[:, 0, :], 0.0, None, ALU.is_gt))
            step(dve.tensor_scalar(srcx[:, :], payi[:, 1, :], 10, None, ALU.arith_shift_right))
            step(dve.tensor_scalar(dstx[:, :], payi[:, 1, :], 1023, None, ALU.bitwise_and))
            step(dve.scalar_tensor_tensor(segk[:, :], dstx[:, :], 1.0, real[:, :], ALU.add, ALU.mult))
            step(dve.tensor_scalar(payi[:, 0, :], dstx[:, :], P - 1, None, ALU.bitwise_and))
            step(dve.scalar_tensor_tensor(rel[:, :], payi[:, 0, :], 1.0, real[:, :], ALU.add, ALU.mult))
            dve.tensor_scalar(rel[:, :], rel[:, :], -1.0, None, ALU.add).then_inc(s_sorted, 1)


            def stats(turn, src):
                for m in range(NC):
                    last = dve.bn_stats(bst[:, m, :], src[:, m, :])
                step(last)
                for m in range(NC):
                    last = dve.bn_aggr(mv[:, m, :], bst[:, m, :])
                step(last)
                dve.tensor_scalar(var[:, :], mv[:, :, 1], 1e-5, None, ALU.add).then_inc(s_var, 1)
                dve.wait_ge(s_std, turn + 1)
                step(dve.reciprocal(rstd[:, :], std[:, :]))
                dve.scalar_tensor_tensor(nmr[:, :], mv[:, :, 0], -1.0, rstd[:, :], ALU.mult, ALU.mult).then_inc(s_stat, 1)

            dve.wait_ge(s_x, 32)
            stats(0, xs)
            dve.wait_ge(s_norm, 1)
            stats(1, hn)
            dve.wait_ge(s_wqkv, 32)
            for n, dst in enumerate((qv[:, 0], kS, qv[:, 1])):
                for m in range(NC):
                    dve.wait_ge(s_job, plan.number("qkv", n * NC + m))
                    dve.tensor_tensor(dst[:, m, :], plan.slot(ps, "qkv", n * NC + m)[:, 0:D], bqkv[:, n * D:(n + 1) * D],
                                      ALU.add).then_inc(s_by_dve, 1)
            dve.wait_ge(s_q_out, 16)
            dve.wait_ge(s_v_out, 16)

            def make_hot():
                dve.tensor_tensor(hot, iota[:, 0:P].unsqueeze(1).to_broadcast([P, NT, P]),
                                  rel[:, :].unsqueeze(2).to_broadcast([P, NT, P]), ALU.is_equal).then_inc(s_hot, 1)

            make_hot()
            with dve.Fori(0, NB4) as i:
                step.enter(i, 1)
                for j in range(4):
                    dve.wait_ge(s_q_in[j], i * 16 + 16)
                    dve.wait_ge(s_kg, i * 4 + (j + 1))
                    last = dve.tensor_tensor(msg[:, j, :], ring[:, j, :], ps[:, 512 * (4 + j):512 * (5 + j)], ALU.mult)
                    last.then_inc(s_q_used[j], 1)
                dve.wait_ge(s_q_used[3], i + 1)
                step(dve.tensor_reduce(lg[:, bass.ds(i * 4, 4), :], msg.rearrange("p s (h d) -> p (s h) d", d=DH), AX.X, ALU.add))
            step.leave(NB4)
            dve.wait_ge(s_att, 16 * NT)
            step(dve.scalar_tensor_tensor(lg[:, :, :], lg[:, :, :], float(D) ** -0.5, attr[:, :, 24:32], ALU.mult, ALU.add))
            dve.tensor_copy(lgp.rearrange("p g t h -> p t g h"), lg[:, :, :].rearrange("p (t g) h -> p t g h", g=TG))
            dve.tensor_copy(kp.rearrange("p g t h -> p t g h"),
                            segk[:, :].rearrange("p (t g) -> p t g", g=TG).unsqueeze(3).to_broadcast([P, TT, TG, H])).then_inc(s_soft, 1)
            dve.wait_ge(s_ak, 2)
            step(dve.memset(pen[:, :], 0.0))
            step(dve.tensor_tensor(pen[:, 1:768], kT[:, 1:768], kT[:, 0:767], ALU.not_equal))
            step(dve.tensor_scalar(pen[:, 1:768], pen[:, 1:768], -BIG, None, ALU.mult))

            def scans(start_f, start_b):
                dve.tensor_tensor_scan(fwd[:, :], pen[:, 0:768], aT[:, :], start_f, ALU.add, ALU.max)
                step(dve.tensor_tensor_scan(bwd[:, ::-1], pen[:, 768:0:-1], aT[:, ::-1], start_b, ALU.add, ALU.max))

            scans(-BIG, -BIG)
            dve.tensor_copy(ends[:, 0:1], fwd[:, 767:768])
            dve.tensor_copy(ends[:, 1:2], bwd[:, 0:1])
            dve.tensor_copy(ends[:, 2:3], kT[:, 0:1])
            dve.tensor_copy(ends[:, 3:4], kT[:, 767:768])
            dve.tensor_reduce(ends[:, 4:5], pen[:, 0:768], AX.X, ALU.min).then_inc(s_ends, 1)
            dve.wait_ge(s_ends_in, 16)
            seam, hop, run_f, run_b = (chd[:, j, :] for j in range(4))
            step(dve.memset(chd[:, :, :], 0.0))
            step(dve.memset(carh[:, :, :], -BIG))
            step(dve.tensor_tensor(seam[:, 1:TT], endh[:, 1:TT, 2], endh[:, 0:TT - 1, 3], ALU.not_equal))
            step(dve.tensor_scalar(seam, seam, -BIG, None, ALU.mult))
            step(dve.tensor_tensor(hop, seam, endh[:, :, 4], ALU.add))
            step(dve.tensor_tensor_scan(run_f, hop, endh[:, :, 0], -BIG, ALU.add, ALU.max))
            step(dve.tensor_tensor(carh[:, 1:TT, 0], run_f[:, 0:TT - 1], seam[:, 1:TT], ALU.add))
            step(dve.tensor_copy(hop, endh[:, :, 4]))
            step(dve.tensor_tensor(hop[:, 0:TT - 1], hop[:, 0:TT - 1], seam[:, 1:TT], ALU.add))
            step(dve.tensor_tensor_scan(run_b[:, ::-1], hop[:, ::-1], endh[:, ::-1, 1], -BIG, ALU.add, ALU.max))
            step(dve.tensor_tensor(carh[:, 0:TT - 1, 1], run_b[:, 1:TT], seam[:, 1:TT], ALU.add))
            step(dve.tensor_scalar(carh[:, :, :], carh[:, :, :], -BIG, None, ALU.max))
            dve.nop().then_inc(s_carry, 1)
            dve.wait_ge(s_carry_in, 16)
            scans(carry[:, 0:1], carry[:, 1:2])
            dve.tensor_tensor(aT[:, :], fwd[:, :], bwd[:, :], ALU.max).then_inc(s_max, 1)
            dve.wait_ge(s_maxT, 1)
            top = ps[:, 2048:2048 + TG * P].rearrange("p (g q) -> p g q", q=P)[:, :, 0:112]
            dve.tensor_tensor(lga[:, :, :].rearrange("p (t g) h -> p t g h", g=TG), lg[:, :, :].rearrange("p (t g) h -> p t g h", g=TG),
                              top.rearrange("p g (t h) -> p t g h", h=H), ALU.subtract).then_inc(s_shift, 1)
            dve.wait_ge(s_prob, 1)
            with dve.Fori(0, NB4) as i:
                for j in range(4):
                    dve.wait_ge(s_v_in[j], i * 16 + 16)
                    dve.wait_ge(s_msg_used[j], i)
                    dve.tensor_tensor(msg[:, j, :].rearrange("p (h d) -> p h d", d=DH), ring[:, j, :].rearrange("p (h d) -> p h d", d=DH),
                                      lg[:, bass.ds(i * 4 + j, 1), :].rearrange("p o h -> p (o h)").unsqueeze(2).to_broadcast([P, H, DH]), ALU.mult).then_inc(s_msg[j], 1)
            dve.wait_ge(s_agg, 1)
            step(dve.tensor_scalar(sums[:, :, :], ps[:, 2560:2560 + NC * H].rearrange("p (m h) -> p m h", h=H), 0.5, None, ALU.max))
            step(dve.reciprocal(sums[:, :, :], sums[:, :, :]))
            for m in range(NC):
                last = dve.tensor_tensor(agg[:, m, :].rearrange("p (h d) -> p h d", d=DH), ps[:, 512 * m:512 * (m + 1)].rearrange("p (h d) -> p h d", d=DH),
                                         sums[:, m, :].unsqueeze(2).to_broadcast([P, H, DH]), ALU.mult)
            last.then_inc(s_aggn, 1)
            dve.wait_ge(s_h1b, 1)
            for m in range(NC):
                dve.wait_ge(s_job, plan.number("wo", m))
                dve.tensor_tensor(hn[:, m, :], plan.slot(ps, "wo", m)[:, 0:D], hn[:, m, :], ALU.add).then_inc(s_by_dve, 1)
            dve.wait_ge(s_by_dve, plan.by[:plan.number("wo", NC - 1)].count("dve"))
            stats(2, hn)
            dve.wait_ge(s_resid, 1)
            for m in range(NC):
                dve.wait_ge(s_job, plan.number("ffn2", m))
                dve.tensor_tensor(xs[:, m, :], plan.slot(ps, "ffn2", m)[:, 0:D], xs[:, m, :], ALU.add).then_inc(s_by_dve, 1)
            dve.wait_ge(s_by_dve, plan.by[:plan.number("ffn2", NC - 1)].count("dve"))
            stats(3, xs)
            dve.wait_ge(s_is3, 1)
            step(dve.memset(small_w[:, 1152:1664], 0.0))
            for j in range(4):
                lanes = slice(F1 * j, F1 * (j + 1))
                step(dve.tensor_copy(w_bd[lanes, j, :].rearrange("p (c f) -> p c f", f=F1),
                                     w_f2[lanes].rearrange("p (f c) -> p c f", c=6)[:, 0:4, :]))
            dve.wait_ge(s_z, 1)
            dve.scalar_tensor_tensor(zf, zf, 0.0, tf, ALU.max, ALU.add).then_inc(s_ssp, 1)
            step(dve.tensor_copy(b_fc.rearrange("p (c f) -> p c f", f=F1), b_f2.rearrange("p (f c) -> p c f", c=6)[:, 0:4, :]))
            for g in range(NB4):
                dve.wait_ge(s_job, plan.number("filt", g))
                dve.tensor_tensor(filt[:, g:g + 63 + 1:21, :], plan.slot(ps, "filt", g)[:, 0:4 * P].rearrange("p (j n) -> p j n", n=P),
                                  b_fc.unsqueeze(1).to_broadcast([P, 4, P]), ALU.add).then_inc(s_by_dve, 1)
            dve.wait_ge(s_by_dve, plan.by[:plan.number("filt", NB4 - 1)].count("dve"))
            step(dve.scalar_tensor_tensor(srcf[:, :], srcx[:, :], 1.0, real[:, :], ALU.add, ALU.mult))
            step(dve.tensor_scalar(srcf[:, :], srcf[:, :], -1.0, None, ALU.add))
            with dve.Fori(0, NB4 // 3) as i:
                step.enter(i, 6)
                for k in range(3):
                    for j in range(4):
                        dve.wait_ge(s_u_in[4 * k + j], i * 16 + 16)
                    dve.wait_ge(s_feat_used[k], i)
                    for j in range(4):
                        dve.tensor_scalar(hotL[k][:, j, :], iota[:, :], srcf[:, bass.ds(i * 12 + (4 * k + j), 1)], None, ALU.is_equal)
                    u = ringu[:, 4 * k:4 * k + 4, :]
                    s = u[:, :, 0:F1]
                    v = u[:, :, F1:P].rearrange("p s (c f) -> p s c f", c=3)
                    w = filt[:, bass.ds(i * 12 + 4 * k, 4), :]
                    y = attr[:, bass.ds(i * 12 + 4 * k, 4), 20:24]
                    ys = y[:, :, 0:1].to_broadcast([P, 4, F1])
                    yv = y[:, :, 1:4].unsqueeze(3).to_broadcast([P, 4, 3, F1])
                    f = feat[:, 4 * k:4 * k + 4, :]
                    fv = f[:, :, 2 * F1:NF].rearrange("p s (c w f) -> p s c w f", c=3, w=2)
                    dve.tensor_tensor(t1, w[:, :, 0:F1], ys, ALU.mult)
                    dve.tensor_tensor(t2, w[:, :, 2 * F1:3 * F1], s, ALU.mult)
                    dve.tensor_tensor(t3, w[:, :, 3 * F1:4 * F1], ys, ALU.mult)
                    step(dve.tensor_tensor(t4, v, yv, ALU.mult))
                    dve.tensor_tensor(f[:, :, 0:F1], t1, s, ALU.mult)
                    dve.tensor_tensor(fv[:, :, :, 0, :], t2.unsqueeze(2).to_broadcast([P, 4, 3, F1]), yv, ALU.mult)
                    dve.tensor_tensor(fv[:, :, :, 1, :], t3.unsqueeze(2).to_broadcast([P, 4, 3, F1]), v, ALU.mult).then_inc(s_u_used[k], 1)
                    step(dve.tensor_reduce(t5, t4.rearrange("p s c f -> p s f c"), AX.X, ALU.add))
                    dve.tensor_tensor(f[:, :, F1:2 * F1], t5, w[:, :, F1:2 * F1], ALU.mult).then_inc(s_feat, 1)
            step.leave(NB4 // 3)
            dve.wait_ge(s_z, 2)
            dve.scalar_tensor_tensor(oT[:, 0, :], oT[:, 0, :], 0.0, tz, ALU.max, ALU.add).then_inc(s_ssp, 1)
            for m in range(NC):
                dve.wait_ge(s_job, plan.number("o2", m))
                o = plan.slot(ps, "o2", m)
                dve.scalar_tensor_tensor(xs[:, m, 0:B1], o[:, 0:B1], float(B1) ** -0.5, xs[:, m, 0:B1], ALU.mult, ALU.add)
                xv = xs[:, m, B1:D].rearrange("p (d c) -> p c d", c=3)
                dve.scalar_tensor_tensor(xv, o[:, B1:D].rearrange("p (c d) -> p c d", c=3), float(B1) ** -0.5, xv, ALU.mult, ALU.add).then_inc(s_by_dve, 1)
            step(dve.tensor_scalar(tmask[:, 0, :], attr[:, :, 32], 0.0, None, ALU.is_equal))
            step(dve.tensor_scalar(tmask[:, 1, :], attr[:, :, 32], 0.0, None, ALU.not_equal))
            dve.nop().then_inc(s_free, 1)
            for r in range(2):
                with dve.Fori(0, NB4) as i:
                    for j in range(4):
                        dve.wait_ge(s_hs_used[j], i + r * NB4)
                        at = bass.ds(i * 4 + j, 1)
                        dve.tensor_scalar(hotS[:, j, :], iota[:, :], srcf[:, at], None, ALU.is_equal)
                        dve.tensor_scalar(hotD[:, j, :], iota[:, 0:P], rel[:, at], tmask[:, r, at], ALU.is_equal, ALU.mult).then_inc(s_hs[j], 1)
            dve.wait_ge(s_job, plan.number("adjT", 2 * NC - 1))
            dve.wait_ge(s_adj, 2)
            step(dve.tensor_tensor(adj[0][:, :, :], adj[0][:, :, :], adj[1][:, :, :], ALU.add))
            step(dve.tensor_reduce(deg[:, :], adj[0][:, :, :], AX.X, ALU.add))
            step(dve.tensor_scalar(deg[:, :], deg[:, :], 1.0, None, ALU.max))
            step(dve.reciprocal(deg[:, :], deg[:, :]))
            dve.tensor_tensor(adj[1][:, :, :], adj[0][:, :, :], deg[:, :].unsqueeze(2).to_broadcast([P, NC, NP]), ALU.mult).then_inc(s_mean, 1)
            dve.wait_ge(s_job, plan.number("deg", 0))
            dve.tensor_scalar(degd, plan.slot(ps, "deg", 0)[:, 0:NP], 1.0, None, ALU.max).then_inc(s_by_dve, 1)
            dve.wait_ge(s_by_dve, plan.by[:plan.number("deg", 0)].count("dve"))
            step(dve.reciprocal(degd, degd))
            dve.tensor_tensor(meanf[:, :, :], adj[0][:, :, :], degd.unsqueeze(1).to_broadcast([P, NC, NP]), ALU.mult).then_inc(s_mean, 1)
            stats(4, xs)

            def combine(l):
                step(dve.memset(acc[l], 0.0))
                with dve.Fori(0, NBASE // 3) as i:
                    step.enter(i, 6)
                    for u in range(6):
                        dve.wait_ge(s_bas_in[u % 3], i * 32 + (16 * (l * 2 * NBASE // 3 + u // 3) + 16))
                        part = slice(u % 2 * 1024, u % 2 * 1024 + 1024)
                        for r in range(2):
                            last = dve.scalar_tensor_tensor(acc[l][:, r, part], bas[u % 3], attb[:, l, bass.ds(i * 3 + (u // 2 + r * NBASE), 1)],
                                                            acc[l][:, r, part], ALU.mult, ALU.add)
                            if r == 0:
                                step(last)
                        last.then_inc(s_bas_used[u % 3], 1)
                        dve.wait_ge(s_bas_used[u % 3], i * 2 + (l * 2 * NBASE // 3 + u // 3 + 1))
                step.leave(NBASE // 3)
                dve.nop().then_inc(s_rel, 1)

            dve.wait_ge(s_l3par, 8 * 16)
            combine(0)
            dve.wait_ge(s_by_act, plan.by[:plan.number(f"L{LAYERS - 1}", NC - 1)].count("act"))
            step(dve.tensor_tensor(xs[:, :, :], xs[:, :, :], hn[:, :, :], ALU.add))
            stats(5, xs)
            combine(1)
            for m in range(NC):
                dve.wait_ge(s_job, plan.number("O0", m))
                dve.tensor_tensor(hn[:, m, :], plan.slot(ps, "O0", m)[:, 0:D], rows[:, 0, :], ALU.add).then_inc(s_by_dve, 1)
            dve.wait_ge(s_by_dve, plan.by[:plan.number("O0", NC - 1)].count("dve"))
            dve.tensor_scalar(hn[:, :, :], hn[:, :, :], 0.0, None, ALU.max).then_inc(s_h3, 1)
            dve.wait_ge(s_xb, 1)
            for m in range(NC):
                dve.wait_ge(s_job, plan.number("O1", m))
                dve.tensor_tensor(xs[:, m, :], plan.slot(ps, "O1", m)[:, 0:D], xs[:, m, :], ALU.add).then_inc(s_by_dve, 1)

        @block.tensor
        def _(pe):
            def counts(turn, bins):
                pe.wait_ge(s_count, turn + 1)
                cnt = small[:, 1, 0:bins]
                pe.matmul(ps[0:ER, 0:bins], below[0:ER, 0:ER], cnt, start=True, stop=True)
                pe.matmul(ps[0:ER, 64:64 + bins], ones[0:ER, 0:ER], cnt, start=True, stop=True).then_inc(s_prefix, 1)

            def permute(turn, rows, cols):
                bank = ps[0:rows, 512 * (turn + 1):512 * (turn + 1) + 2 * cols]
                pe.matmul(bank, zeros[0:ER, 0:rows], zeros[0:ER, 0:2 * cols], start=True, stop=False)
                with pe.Fori(0, P // 8) as i:
                    for half in range(2):
                        pe.wait_ge(s_half[turn][half], i + 1)
                        for j in range(4):
                            o = oneh[:, 4 * half + j, :]
                            mv = o[:, P:3 * P].rearrange("p (k w) -> p k w", k=2)[:, :, 0:cols]
                            last = pe.matmul(bank.rearrange("p (k w) -> p k w", k=2), o[:, 0:rows], mv,
                                             start=False, stop=False)
                        last.then_inc(s_halfused[turn][half], 1)
                pe.matmul(bank, zeros[0:ER, 0:rows], zeros[0:ER, 0:2 * cols], start=False, stop=True)\
                  .then_inc(s_permuted, 1)

            pe.wait_ge(s_const, 1)
            counts(0, LO_BINS)
            permute(0, ER, P)
            counts(1, HI_BINS)
            permute(1, P, NT)

            def turn_nodes(name, src, count=K4, cols=lambda k: slice(k * P, (k + 1) * P)):
                for k in range(count):
                    plan.open(pe, name, k)
                    o = plan.slot(ps, name, k)
                    for m in range(NC):
                        last = pe.transpose(o[:, m * P:(m + 1) * P], src[:, m, cols(k)], ident[:, :])
                    last.then_inc(s_job, 1)

            def product(name, j, width, pairs):
                plan.open(pe, name, j)
                o = plan.slot(ps, name, j)
                for at in range(0, width, D):
                    to = min(at + D, width)
                    for n, (lhsT, rhs) in enumerate(pairs):
                        last = pe.matmul(o[:, at:to], lhsT, rhs[:, at:to], start=n == 0, stop=n == len(pairs) - 1)
                last.then_inc(s_job, 1)

            def node(t, k, m):
                return t[:, k, m * P:(m + 1) * P]

            pe.wait_ge(s_norm, 2)
            turn_nodes("ln1T", nrm)
            pe.wait_ge(s_wqkv, 32)
            for n in range(3):
                for m in range(NC):
                    if m == 0 and n == 0:
                        plan.wait_taken(pe, plan.number("ln1T", K4 - 1) - 1)
                    product("qkv", n * NC + m, D, [(node(hT, k, m), wqkv[:, k, n * D:(n + 1) * D]) for k in range(K4)])
            plan.wait_taken(pe, plan.number("qkv", 3 * NC - 1) - 1)
            pe.wait_ge(s_hot, 1)

            def tile_chunk(t):
                return pe.value_load(tchunk[0:1, bass.ds(t, 1)], min_val=0, max_val=NC - 1)

            with pe.Fori(0, NB4) as i:
                pe.wait_ge(s_hotT, i)
                for j in range(4):
                    last = pe.matmul(ps[:, j * P:(j + 1) * P], hot[:, bass.ds(i * 4 + j, 1), :].rearrange("p o d -> p (o d)"), identb[:, :], start=True, stop=True)
                last.then_inc(s_turned, 1)
                pe.wait_ge(s_hotT, i + 1)
                for j in range(4):
                    pe.wait_ge(s_q_used[j], i)
                    c = tile_chunk(i * 4 + j)
                    pe.matmul(ps[:, 512 * (4 + j):512 * (5 + j)], hotT[:, j * P:(j + 1) * P],
                              kS[:, bass.ds(c, 1), :].rearrange("p o n -> p (o n)"), start=True, stop=True).then_inc(s_kg, 1)
            pe.wait_ge(s_soft, 1)
            for n, src in enumerate((lgp, kp)):
                for g in range(TG):
                    last = pe.transpose(ps[0:112, 1024 * n + g * P:1024 * n + (g + 1) * P], src[:, g].rearrange("p t h -> p (t h)"), ident[:, :])
                last.then_inc(s_akT, 1)
            pe.wait_ge(s_max, 1)
            for g in range(TG):
                last = pe.transpose(ps[:, 2048 + g * P:2048 + g * P + 112], aT[:, g * P:(g + 1) * P], ident[0:112, 0:112])
            last.then_inc(s_maxT, 1)

            def open_sums(width, banks=NC):
                for m in range(banks):
                    pe.matmul(ps[:, 512 * m:512 * m + width], zeros[:, 0:P], iota[:, 0:width], start=True, stop=False)

            def close_sums(width, banks=NC):
                for m in range(banks):
                    last = pe.matmul(ps[:, 512 * m:512 * m + width], zeros[:, 0:P], iota[:, 0:width], start=False, stop=True)
                return last

            pe.wait_ge(s_prob, 1)
            pe.wait_ge(s_const, 1)
            open_sums(D)
            pe.matmul(ps[:, 2560:2560 + NC * H], zeros[:, 0:P], iota[:, 0:NC * H], start=True, stop=False)
            with pe.Fori(0, NB4 // 3) as i:
                for k in range(3):
                    pe.wait_ge(s_hot4, i * 3 + (k + 1))
                    for j in range(4):
                        pe.wait_ge(s_msg[j], i * 3 + (k + 1))
                        c = tile_chunk(i * 12 + (4 * k + j))
                        one = hot4[:, k, j * P:(j + 1) * P]
                        pe.matmul(ps[:, bass.ds(c * 512, D)], one, msg[:, j, :], start=False, stop=False, skip_group_check=True)\
                          .then_inc(s_msg_used[j], 1)
                        last = pe.matmul(ps[:, bass.ds(c * H + 2560, H)], one, lg[:, bass.ds(i * 12 + (4 * k + j), 1), :].rearrange("p o h -> p (o h)"),
                                         start=False, stop=False, skip_group_check=True)
                    last.then_inc(s_hot4_used[k], 1)
            close_sums(D)
            pe.matmul(ps[:, 2560:2560 + NC * H], zeros[:, 0:P], iota[:, 0:NC * H], start=False, stop=True).then_inc(s_agg, 1)
            pe.wait_ge(s_aggn, 1)
            turn_nodes("aggT", agg)
            pe.wait_ge(s_wo, 16)
            plan.wait_taken(pe, plan.number("aggT", K4 - 1) - 1)
            for m in range(NC):
                product("wo", m, D, [(node(hT, k, m), wo[:, k, :]) for k in range(K4)])
            pe.wait_ge(s_norm, 3)
            turn_nodes("ln2T", nrm)
            pe.wait_ge(s_w1, 16)
            plan.wait_taken(pe, plan.number("ln2T", K4 - 1) - 1)
            for j in range(16):
                product("ffn1", j, NP, [(w1s[:, k, j * P:(j + 1) * P], hT[:, k, :]) for k in range(K4)])
            pe.wait_ge(s_w2, 16)
            plan.wait_taken(pe, plan.number("ffn1", 15) - 1)
            for m in range(NC):
                product("ffn2", m, D, [(node(g1T, j, m), w2s[:, j, :]) for j in range(16)])

            def taken(name, j):
                plan.wait_taken(pe, plan.number(name, j) - 1)

            pe.wait_ge(s_norm, 4)
            turn_nodes("h1T", hn, cols=lambda k: slice(0, P) if k == 0 else slice(P + k - 1, D, 3))
            pe.wait_ge(s_is3, 1)
            taken("h1T", K4 - 1)
            for m in range(NC):
                plan.open(pe, "in2f", m)
                for k in range(K4):
                    last = pe.matmul(plan.slot(ps, "in2f", m)[:, F1 * k:F1 * (k + 1)], node(hT, k, m), w_in[:, min(k, 1)], start=True, stop=True)
                last.then_inc(s_job, 1)
            for g in range(NB4):
                plan.open(pe, "attT", g)
                for j in range(4):
                    last = pe.transpose(plan.slot(ps, "attT", g)[0:FEAT, j * P:(j + 1) * P], attr[:, j * NB4 + g, :], ident[:, :])
                last.then_inc(s_job, 1)
            taken("attT", NB4 - 1)
            for g3 in range(7):
                plan.open(pe, "hid", g3)
                for g in range(3):
                    for j in range(4):
                        last = pe.matmul(plan.slot(ps, "hid", g3)[F1 * j:F1 * (j + 1), g * P:(g + 1) * P], w_f1,
                                         attT[:, 3 * g3 + g, j * P:(j + 1) * P], start=True, stop=True)
                last.then_inc(s_job, 1)
            pe.wait_ge(s_ssp, 1)
            for g in range(NB4):
                plan.open(pe, "filt", g)
                pe.matmul(plan.slot(ps, "filt", g)[:, 0:4 * P], zf[:, g * P:(g + 1) * P], small_w[:, 1152:1664], start=True, stop=True).then_inc(s_job, 1)
            for j in range(4):
                taken("filt", NB4 - 1 - j)
            open_sums(NF)
            with pe.Fori(0, NB4 // 3) as i:
                for k in range(3):
                    pe.wait_ge(s_feat, i * 3 + (k + 1))
                    for j in range(4):
                        for m in range(NC):
                            last = pe.matmul(ps[:, 512 * m:512 * m + NF], hotL[k][:, j, m * P:(m + 1) * P], feat[:, 4 * k + j, :],
                                             start=False, stop=False)
                    last.then_inc(s_feat_used[k], 1)
            close_sums(NF).then_inc(s_agg, 1)
            pe.wait_ge(s_agg1, 1)
            turn_nodes("f2T", agg1, 2)
            taken("f2T", 1)
            product("o1", 0, NP, [(w_o1s, hT[0:64, 0, :])])
            for c in range(3):
                lanes = slice(64, 128) if c % 2 == 0 else slice(0, 64)
                product("o1", 1 + c, NP, [(w_o1v[lanes], hT[lanes, (c + 1) // 2, :])])
            pe.wait_ge(s_ssp, 2)
            taken("o1", 3)
            for m in range(NC):
                plan.open(pe, "o2", m)
                for k in range(4):
                    last = pe.matmul(plan.slot(ps, "o2", m)[:, k * P:(k + 1) * P], node(oT, k, m), w_o2[:, min(k, 1)], start=True, stop=True)
                last.then_inc(s_job, 1)
            for j in range(4):
                taken("o2", NC - 1 - j)
            for r in range(2):
                if r:
                    pe.wait_ge(s_adj, 1)
                open_sums(D, 7)
                with pe.Fori(0, NB4) as i:
                    for j in range(4):
                        pe.wait_ge(s_hs[j], i + (r * NB4 + 1))
                        c = tile_chunk(i * 4 + j)
                        for n in range(NC):
                            to = c * 512 + n * P if n < NC - 1 else c * P + 2560
                            last = pe.matmul(ps[:, bass.ds(to, P)], hotS[:, j, n * P:(n + 1) * P], hotD[:, j, :],
                                             start=False, stop=False, skip_group_check=True)
                        last.then_inc(s_hs_used[j], 1)
                close_sums(D, 7).then_inc(s_counts, 1)
            pe.wait_ge(s_adj, 2)

            def turn_square(name, n, src, c):
                plan.open(pe, name, n)
                for i in range(NC):
                    last = pe.transpose(plan.slot(ps, name, n)[:, i * P:(i + 1) * P], src[:, i, c * P:(c + 1) * P], ident[:, :])
                last.then_inc(s_job, 1)

            for r in range(2):
                for c in range(NC):
                    turn_square("adjT", r * NC + c, adj[r], c)
            pe.wait_ge(s_mean, 1)
            product("deg", 0, NP, [(ones[:, :], adj[0][:, i, :]) for i in range(NC)])
            for c in range(NC):
                turn_square("meanT", c, adj[1], c)

            def turn_weights(name, n):
                pe.wait_ge(s_rawin, 16 * n)
                for k in range(K4):
                    plan.open(pe, name, k)
                    for o in range(K4):
                        last = pe.transpose(plan.slot(ps, name, k)[:, o * P:(o + 1) * P], raw[:, o, k * P:(k + 1) * P], ident[:, :])
                    last.then_inc(s_job, 1)

            pe.wait_ge(s_norm, 5)
            turn_weights("wi", 1)
            turn_nodes("h2T", hn)
            taken("h2T", K4 - 1)
            for m in range(NC):
                product("h0", m, D, [(node(hT, k, m), wsT[:, k, :]) for k in range(K4)])
            taken("h0", NC - 1)
            turn_nodes("hT", hn)
            for l in range(LAYERS):
                turn_weights(f"ws{l}", 3 * l + 2)
                for p, (s, c) in enumerate((("sf", "cf"), ("sb", "cb"))):
                    turn_weights(f"{s}{l}", 3 * l + 3 + p)
                    pe.wait_ge(s_wnin, 16 * (2 * l + p + 1))
                    taken(f"{s}{l}", K4 - 1)
                    for k in range(K4):
                        product(f"{c}{l}", k, D, [(wn[:, o, k * P:(k + 1) * P], sfT[:, o, :]) for o in range(K4)])
                for name, mean in (("F", meanf), ("B", meanb)):
                    for k in range(K4):
                        product(f"{name}{l}", k, NP, [(hn[:, i, k * P:(k + 1) * P], mean[:, i, :]) for i in range(NC)])
                taken(f"B{l}", K4 - 1)
                for m in range(NC):
                    product(f"L{l}", m, D, [(node(t, k, m), w[:, k, :]) for t, w in ((hT, wsT), (fTv, cf), (bTv, cb)) for k in range(K4)])
                if l < LAYERS - 1:
                    taken(f"L{l}", NC - 1)
                    turn_nodes(f"hT{l}", hn)
            for l in range(2):
                if l == 0:
                    pe.wait_ge(s_norm, 6)
                    pe.wait_ge(s_root, 32)
                    pe.wait_ge(s_l3par, 8 * 16)
                else:
                    pe.wait_ge(s_h3, 1)
                turn_nodes(f"T{l}", hn)
                taken(f"T{l}", K4 - 1)
                for m in range(NC):
                    product(f"gate{l}", m, 2, [(node(hT, k, m), gw[:, l, :, k]) for k in range(K4)])
                for r in range(2):
                    pe.wait_ge(s_gx, 2 * l + r + 1)
                    for k in range(K4):
                        product(f"P{l}{r}", k, NP, [(gx[:, r, i, k * P:(k + 1) * P], adjT[r][:, i, :]) for i in range(NC)])
                taken(f"P{l}1", K4 - 1)
                pe.wait_ge(s_rel, l + 1)
                wr = [acc[l][:, r].rearrange("p (k n) -> p k n", n=D) for r in range(2)]
                for m in range(NC):
                    product(f"O{l}", m, D, [(node(t, k, m), w[:, k, :]) for t, w in ((hT, root[l]), (fTv, wr[0]), (bTv, wr[1])) for k in range(K4)])


_INS = ['x', 'src', 'dst', 'edge_attr_20', 'edge_attr_4', 'edge_attr_8', 'edge_attr_8_n2', 'edge_type_2',
        'edge_weight', 'L0_gnn_Wqkv', 'L0_gnn_bqkv', 'L0_gnn_Wo', 'L0_gnn_bo', 'L0_gnn_ln1_g', 'L0_gnn_ln1_b',
        'L0_gnn_W1', 'L0_gnn_b1', 'L0_gnn_W2', 'L0_gnn_b2', 'L0_gnn_ln2_g', 'L0_gnn_ln2_b', 'L1_gnn_w_in2f_s',
        'L1_gnn_w_in2f_v', 'L1_gnn_W1', 'L1_gnn_b1', 'L1_gnn_W2', 'L1_gnn_b2', 'L1_gnn_w_f2o1_s',
        'L1_gnn_w_f2o1_v', 'L1_gnn_w_f2o2_s', 'L1_gnn_w_f2o2_v', 'L2_gnn_W_init', 'L2_gnn_W_fwd', 'L2_gnn_W_bwd',
        'L2_gnn_W_self', 'L3_gnn_basis1', 'L3_gnn_att1', 'L3_gnn_gate_w1', 'L3_gnn_root1', 'L3_gnn_bias1',
        'L3_gnn_basis2', 'L3_gnn_att2', 'L3_gnn_gate_w2', 'L3_gnn_root2', 'L3_gnn_bias2']


def kernel(**inputs):
    import numpy as _np
    import concourse.bacc as _bacc
    from concourse import mybir as _mybir
    from concourse.bass_utils import run_bass_kernel_spmd as _run

    nc = _bacc.Bacc("TRN2", target_bir_lowering=False, num_devices=1)
    arrays, args = {}, {}
    for name in _INS:
        a = _np.ascontiguousarray(inputs[name])
        arrays[f"in_{name}"] = a
        args[name] = nc.dram_tensor(f"in_{name}", a.shape, _mybir.dt.from_np(a.dtype), kind="ExternalInput").ap()
    out = nc.dram_tensor("out_x", (N, D), F32, kind="ExternalOutput").ap()
    build(nc, args, out)
    r = _run(nc, [arrays], core_ids=[0])
    return r.results[0]["out_x"]
```

```python
import concourse.bass as bass
from concourse import mybir
from contextlib import ExitStack

F32 = mybir.dt.float32
F32R = mybir.dt.float32r
BF16 = mybir.dt.bfloat16
F16 = mybir.dt.float16
I32 = mybir.dt.int32
ALU = mybir.AluOpType
ACT = mybir.ActivationFunctionType
AX = mybir.AxisListType

P = 128
N = 625
E = 10000
D = 512
H = 8
DH = D // H
NC = (N + P - 1) // P
NP = NC * P
LAST = N - (NC - 1) * P
ER = (E + P - 1) // P
ETAIL = E - (ER - 1) * P
NT = (E + NC * (P - 1)) // P + 1
LO_BINS = 32
HI_BINS = 24
BIG = 1.0e30
FEAT = 36
K4 = D // P


class Chain:

    def __init__(self, eng, sem):
        self.eng, self.sem, self.n, self.turn, self.per = eng, sem, 0, None, 0

    def __call__(self, ins):
        self.n += 1
        ins.then_inc(self.sem, 1)
        self.eng.wait_ge(self.sem, self.n if self.turn is None else self.turn * self.per + self.n)

    def enter(self, turn, per):
        self.turn, self.per, self.at = turn, per, self.n

    def leave(self, turns):
        assert self.n - self.at == self.per
        self.n = self.at + turns * self.per
        self.turn = None


class Plan:

    def __init__(self, stages, taken):
        self.taken, self.first, self.by = taken, {}, []
        for name, count, engine in stages:
            self.first[name] = len(self.by)
            self.by += [engine] * count

    def slot(self, ps, name, i):
        j = self.first[name] + i
        return ps[:, 1024 * (j % 4):1024 * (j % 4) + 1024]

    def wait_taken(self, pe, j):
        engine = self.by[j]
        pe.wait_ge(self.taken[engine], self.by[:j + 1].count(engine))

    def open(self, pe, name, i):
        j = self.first[name] + i
        if j >= 4:
            self.wait_taken(pe, j - 4)

    def number(self, name, i):
        return self.first[name] + i + 1


LATER = [("h1T", K4, "act"), ("in2f", NC, "act"), ("attT", NT // 4, "act"), ("hid", 7, "act"), ("filt", NT // 4, "dve"),
         ("f2T", 2, "act"), ("o1", 4, "act"), ("o2", NC, "dve"),
         ("deg", 1, "dve"), ("meanT", NC, "act"),
         ("wi", K4, "act"), ("h2T", K4, "act"), ("h0", NC, "act"), ("hT", K4, "act")]
for _l in range(3):
    LATER += [(f"{_n}{_l}", K4, "act") for _n in ("ws", "sf", "cf", "sb", "cb", "F", "B")] + [(f"L{_l}", NC, "act")]
    if _l < 2:
        LATER.append((f"hT{_l}", K4, "act"))
for _l in range(2):
    LATER += [(f"T{_l}", K4, "act"), (f"gate{_l}", NC, "act"), (f"P{_l}0", K4, "act"), (f"P{_l}1", K4, "act"), (f"O{_l}", NC, "dve")]


def build(nc, a, out):
    with ExitStack() as ctx:
        def sb(name, shape, dt=F32):
            return ctx.enter_context(nc.sbuf_tensor(name, shape, dt))

        def sb_twice(name, shape):
            with nc.sbuf_tensor(name + "_r", shape, F32R) as rounded:
                pass
            return sb(name, shape), rounded

        def sem(name):
            return ctx.enter_context(nc.semaphore(name))

        iota = sb("iota", [P, NP])
        iota16 = sb("iota16", [P, NP], F16)
        ident = sb("ident", [P, P])
        identb = sb("identb", [P, P], BF16)
        ones = sb("ones", [P, P])
        below = sb("below", [P, P])
        zeros = sb("zeros", [P, 2 * P])
        work, work_r = sb_twice("work", [P, 12288])
        fT = sb("fT", [P, K4 * NP])
        sort = fT[0:ER, :].rearrange("p (j t) -> p j t", t=P)
        dsti = sort[:, 0].bitcast(I32)
        enum = sort[:, 2]
        load = sort[:, 3]
        loadi = sort[:, 4].bitcast(I32)
        key = sort[:, 6]
        keyi = sort[:, 7].bitcast(I32)
        pos = sort[:, 8]
        posi = sort[:, 9].bitcast(I32)
        digi = sort[:, 10:12].bitcast(I32)
        dig = sort[:, 12:14]
        small = sb("small", [ER, 8, LO_BINS])
        chi = sb("chi", [ER, 8], I32)
        onehot = work[0:ER, 0:2048].bitcast(BF16)
        prefix = work[0:ER, 2048:2048 + LO_BINS * P]
        rowhot, colhot = (work[0:ER, 6144 + 1024 * j:7168 + 1024 * j].rearrange("p (s w) -> p s w", w=P) for j in range(2))
        eidx = sb("eidx", [P, NT], I32)
        srcx = sb("srcx", [P, NT], I32)
        dstx = sb("dstx", [P, NT], I32)
        reli = sb("reli", [P, NT], I32)
        real = sb("real", [P, NT])
        rel = sb("rel", [P, NT])
        segk = sb("segk", [P, NT])
        tchunk = sb("tchunk", [ER, NT // 4], I32)
        tch = sb("tch", [ER, 4, NT])
        ps = ctx.enter_context(nc.psum_tensor("ps", [P, 4096], F32))

        s_fill = sem("s_fill")
        s_const = sem("s_const")
        s_edges_in = sem("s_edges_in")
        s_dve = sem("s_dve")
        s_pool = sem("s_pool")
        s_count = sem("s_count")
        s_prefix = sem("s_prefix")
        s_ranked = sem("s_ranked")
        s_hots = [sem(f"s_hots{h}") for h in range(2)]
        s_hot_read = [sem(f"s_hot_read{h}") for h in range(2)]
        s_zeroed = sem("s_zeroed")
        s_permuted = sem("s_permuted")
        s_sorted = sem("s_sorted")

        xs = sb("xs", [P, NC, D])
        hn = sb("hn", [P, NC, D])
        hT, hT_r = sb_twice("hT", [P, K4, NP])
        bT, bT_r = sb_twice("bT", [P, K4 * NP])
        aux = sb("aux", [P, 10752])
        wA, wA_r = sb_twice("wA", [P, 4 * 4 * D])
        att = sb("att", [P, NT * FEAT])
        attr = att[:, :].rearrange("p (t f) -> p t f", f=FEAT)
        nrm = aux[:, 8192:8192 + NC * D].rearrange("p (m n) -> p m n", n=D)
        bst = sb("bst", [P, NC, 6])
        mv = sb("mv", [P, NC, 2])
        var = sb("var", [P, NC])
        std = sb("std", [P, NC])
        rstd = sb("rstd", [P, NC])
        nmr = sb("nmr", [P, NC])
        lng = sb("lng", [P, 2, 2, K4])
        b1c = sb("b1c", [P, 16])
        rows = sb("rows", [P, 2, D])
        bqkv = wA[:, 6144:6144 + 3 * D]
        wqkv = wA[:, 0:K4 * 3 * D].rearrange("p (k n) -> p k n", k=K4)
        ETP, ETJ = 125, E // 125
        etab = aux[0:ETP, 0:ETJ * FEAT].rearrange("p (j f) -> p j f", f=FEAT)
        raw20 = aux[0:ETP, 2880:2880 + 1600].rearrange("p (j f) -> p j f", f=20)
        raw4 = aux[0:ETP, 4480:4480 + 320].rearrange("p (j f) -> p j f", f=4)
        raw8 = aux[0:ETP, 4800:4800 + 640].rearrange("p (j f) -> p j f", f=8)
        raw8b = aux[0:ETP, 5440:5440 + 640].rearrange("p (j f) -> p j f", f=8)
        rawt = aux[0:ETP, 6080:6160].bitcast(I32)
        raww = aux[0:ETP, 6160:6240]
        rawsd = aux[0:ETP, 6240:6400].bitcast(I32).rearrange("p (c j) -> p c j", c=2)
        wo = aux[:, 4096:4096 + K4 * D].rearrange("p (k n) -> p k n", k=K4)
        etab_d = nc.dram_tensor("etab_d", (E, FEAT), F32).ap()
        q_d = nc.dram_tensor("q_d", (NP, D), F32).ap()
        v_d = nc.dram_tensor("v_d", (NP, D), F32).ap()
        ends_d = nc.dram_tensor("ends_d", (112, 5), F32).ap()
        carry_d = nc.dram_tensor("carry_d", (112, 2), F32).ap()
        kH = bT_r[:, :].rearrange("p (m n) -> p m n", n=D)
        kf = work[:, 8192:8192 + NC * D].rearrange("p (m n) -> p m n", n=D)
        kL = work_r[:, 8192:8192 + NC * D].rearrange("p (m n) -> p m n", n=D)
        qv = work[:, 0:2 * NC * D].rearrange("p (w m n) -> p w m n", w=2, m=NC)
        NB4 = NT // 4
        hot = work[:, 0:NT * P // 2].bitcast(BF16).rearrange("p (t d) -> p t d", d=P)
        hTf = hT[:, :, :].rearrange("p k n -> p (k n)")
        hot4 = hTf[:, 0:3 * 4 * P].rearrange("p (k n) -> p k n", k=3)
        hotT = hT_r[:, 0, 0:4 * P]
        ring = fT[:, 0:4 * D].rearrange("p (s n) -> p s n", n=D)
        msg = work[:, 5888:5888 + 4 * D].rearrange("p (s n) -> p s n", n=D)
        lg = sb("lg", [P, NT, H])
        lga = hTf[:, 1536:1536 + NT * H].rearrange("p (t h) -> p t h", h=H)
        TT, TG = 14, 6
        lgp, kp = (work[:, 5888 + 672 * j:5888 + 672 * (j + 1)].rearrange("p (g t h) -> p g t h", g=TG, t=TT) for j in range(2))
        aT = work[0:112, 7936:7936 + 768]
        kT = work[0:112, 8704:8704 + 768]
        pen = work[0:112, 9472:9472 + 769]
        fwd = work[0:112, 10496:10496 + 768]
        bwd = work[0:112, 11264:11264 + 768]
        ends = sb("ends", [112, 5])
        endh = sb("endh", [H, TT, 5])
        carh = sb("carh", [H, TT, 2])
        chd = sb("chd", [H, 4, TT])
        carry = sb("carry", [112, 2])
        agg = nrm
        sums = sb("sums", [P, NC, H])
        g1T = aux[:, 0:16 * NP].rearrange("p (j n) -> p j n", n=NP)
        w1s = wA[:, :].rearrange("p (k n) -> p k n", k=K4)
        w2s = work[:, 0:16 * D].rearrange("p (k n) -> p k n", k=16)

        s_x = sem("s_x")
        s_xpad = sem("s_xpad")
        s_raw = sem("s_raw")
        s_table = sem("s_table")
        s_etab = sem("s_etab")
        s_par = sem("s_par")
        s_wqkv = sem("s_wqkv")
        s_var = sem("s_var")
        s_std = sem("s_std")
        s_stat = sem("s_stat")
        s_norm = sem("s_norm")
        s_job = sem("s_job")
        s_act = sem("s_act")
        s_by_act = sem("s_by_act")
        s_by_dve = sem("s_by_dve")
        s_q_out = sem("s_q_out")
        s_v_out = sem("s_v_out")
        PIECE = NT // 3
        s_att = [sem(f"s_att{j}") for j in range(3)]
        s_ids = sem("s_ids")
        s_hot = sem("s_hot")
        s_q_in = [sem(f"s_q_in{j}") for j in range(4)]
        s_q_used = [sem(f"s_q_used{j}") for j in range(4)]
        s_hot4 = sem("s_hot4")
        s_hot4_used = [sem(f"s_hot4_used{k}") for k in range(3)]
        s_soft = sem("s_soft")
        s_h1b = sem("s_h1b")
        s_turned = sem("s_turned")
        s_hotT = sem("s_hotT")
        s_kg = sem("s_kg")
        s_kH = sem("s_kH")
        s_kL = sem("s_kL")
        s_logits = sem("s_logits")
        s_ak = sem("s_ak")
        s_akT = sem("s_akT")
        s_ends = sem("s_ends")
        s_ends_out = sem("s_ends_out")
        s_ends_in = sem("s_ends_in")
        s_carry = sem("s_carry")
        s_carry_out = sem("s_carry_out")
        s_carry_in = sem("s_carry_in")
        s_max = sem("s_max")
        s_maxT = sem("s_maxT")
        s_shift = sem("s_shift")
        s_prob = sem("s_prob")
        s_v_in = [sem(f"s_v_in{j}") for j in range(4)]
        s_msg = [sem(f"s_msg{j}") for j in range(4)]
        s_msg_used = [sem(f"s_msg_used{j}") for j in range(4)]
        s_agg = sem("s_agg")
        s_aggn = sem("s_aggn")
        s_wo = sem("s_wo")
        s_w1 = sem("s_w1")
        s_w2 = sem("s_w2")
        s_resid = sem("s_resid")
        s_pre = sem("s_pre")
        plan = Plan([("ln1T", K4, "act"), ("qkv", 3 * NC, "dve"), ("aggT", K4, "act"), ("wo", NC, "dve"),
                     ("ln2T", K4, "act"), ("ffn1", 16, "act"), ("ffn2", NC, "dve")] + LATER,
                    {"act": s_by_act, "dve": s_by_dve})
        B1, F1, NF = 128, 32, 8 * 32
        half = sb("half", [P, 1])
        zf = wA[:, 0:21 * P]
        tf = wA[:, 21 * P:42 * P]
        small_w = wA[:, 5376:8192]
        w_in = small_w[:, 0:64].rearrange("p (w f) -> p w f", w=2)
        w_f1 = small_w[0:FEAT, 64:96]
        w_f2 = small_w[:, 96:288]
        b_f2 = small_w[:, 288:480]
        w_bd = small_w[:, 1152:1664].rearrange("p (j n) -> p j n", n=P)
        b_fc = small_w[:, 1024:1152]
        w_o1s = small_w[0:64, 480:608]
        w_o1v = small_w[:, 608:736]
        w_o2 = small_w[:, 736:992].rearrange("p (w n) -> p w n", w=2)
        attT = work[0:FEAT, 0:NB4 * 4 * P].rearrange("p (g n) -> p g n", n=4 * P)
        filt = aux[:, :].rearrange("p (t n) -> p t n", n=P)
        uS = bT[:, 0:NC * P].rearrange("p (m n) -> p m n", n=P)
        u_d = nc.dram_tensor("u_d", (NP, P), F32).ap()
        ringu = fT[:, 0:12 * P].rearrange("p (s n) -> p s n", n=P)
        feat = work[:, 5120:5120 + 12 * NF].rearrange("p (s n) -> p s n", n=NF)
        featH = work_r[:, 9088:9088 + 12 * NF].rearrange("p (s n) -> p s n", n=NF)
        featL = wA_r[:, 0:12 * NF].rearrange("p (s n) -> p s n", n=NF)
        t1, t2, t3 = (work[:, 8192 + 128 * j:8192 + 128 * (j + 1)].rearrange("p (s f) -> p s f", f=F1) for j in range(3))
        t4 = work[:, 8576:8576 + 384].rearrange("p (s c f) -> p s c f", c=3, f=F1)
        t5 = work[:, 8960:8960 + 128].rearrange("p (s f) -> p s f", f=F1)
        agg1 = bT[:, 0:NC * NF].rearrange("p (m n) -> p m n", n=NF)
        oT = bT[:, :].rearrange("p (k n) -> p k n", n=NP)
        tz = fT[:, 0:NP]
        tmask = bT[:, 0:2 * NT].rearrange("p (r t) -> p r t", r=2)
        srcf = sb("srcf", [P, NT])
        hotL = [work_r[:, 0:2560], work_r[:, 2560:5120], hT_r[:, :, :].rearrange("p k n -> p (k n)")]
        hotL = [h.rearrange("p (j n) -> p j n", n=NP) for h in hotL]
        hotS = fT[:, 0:4 * NP // 2].bitcast(BF16).rearrange("p (s n) -> p s n", n=NP)
        hotD = fT[:, 2 * NP:2 * NP + 4 * P // 2].bitcast(BF16).rearrange("p (s n) -> p s n", n=P)
        both, bymean = (work[:, 3200 * r:3200 * (r + 1)].rearrange("p (i n) -> p i n", n=NP) for r in range(2))
        adj = [aux[:, 3200 * r:3200 * (r + 1)].rearrange("p (i n) -> p i n", n=NP) for r in range(2)]
        deg = sb("deg", [P, NC])
        degd = fT[:, 0:NP]
        meanf = wA[:, 0:3200].rearrange("p (i n) -> p i n", n=NP)
        meanb = wA[:, 3200:6400].rearrange("p (i n) -> p i n", n=NP)
        LAYERS = 3

        def square(at):
            return work[:, at:at + K4 * D].rearrange("p (k n) -> p k n", n=D)
        wn, cf, cb, sfT, wsT, raw = (square(2048 * j) for j in range(6))
        fTv = fT[:, :].rearrange("p (k n) -> p k n", n=NP)
        bTv = bT[:, :].rearrange("p (k n) -> p k n", n=NP)
        NBASE = 30
        attb = sb("attb", [P, 2, 2 * NBASE])
        gw = sb("gw", [P, 2, 2, K4])
        gate = sb("gate", [P, NC, 2])
        root = [square(0), square(2048)]
        acc = aux[:, 6400:6400 + 4096].rearrange("p (r n) -> p r n", r=2)
        rel_w = [work[:, 4096:8192].rearrange("p (r n) -> p r n", r=2), acc]
        rel_d = nc.dram_tensor("rel_d", (P, 2, 4 * D), F32).ap()
        bas = [att[:, 0:1024], att[:, 1024:2048], wA[:, 6400:7424]]
        gx = wA[:, 0:2 * NC * D].rearrange("p (r m n) -> p r m n", r=2, m=NC)

        s_f1zero = sem("s_f1zero")
        s_l1w = sem("s_l1w")
        s_is3 = sem("s_is3")
        s_z = sem("s_z")
        s_ssp = sem("s_ssp")
        s_u_out = sem("s_u_out")
        s_u_in = [sem(f"s_u_in{j}") for j in range(12)]
        s_u_used = [sem(f"s_u_used{k}") for k in range(3)]
        s_feat = sem("s_feat")
        s_feat_full = sem("s_feat_full")
        s_featH = sem("s_featH")
        s_feat_used = [sem(f"s_feat_used{k}") for k in range(3)]
        s_agg1 = sem("s_agg1")
        s_tz = sem("s_tz")
        s_hs = [sem(f"s_hs{j}") for j in range(4)]
        s_hs_used = [sem(f"s_hs_used{j}") for j in range(4)]
        s_counts = sem("s_counts")
        s_adj = sem("s_adj")
        s_mean = sem("s_mean")
        s_rawin = sem("s_rawin")
        s_wnin = sem("s_wnin")
        s_free = sem("s_free")
        s_bas_in = [sem(f"s_bas_in{j}") for j in range(3)]
        s_bas_used = [sem(f"s_bas_used{j}") for j in range(3)]
        s_rel = sem("s_rel")
        s_rel_out = sem("s_rel_out")
        s_rel_in = sem("s_rel_in")
        s_l3par = sem("s_l3par")
        s_root = sem("s_root")
        s_gate = sem("s_gate")
        s_gx = sem("s_gx")
        s_h3 = sem("s_h3")
        s_x3 = sem("s_x3")
        s_xb = sem("s_xb")
        s_out = sem("s_out")

        block = ctx.enter_context(nc.Block())

        @block.sync
        def _(sp):
            sp.wait_ge(s_fill, 1)
            sp.dma_start(dsti[0:ER - 1, :], a["dst"][0:(ER - 1) * P].rearrange("(p t) -> p t", t=P)).then_inc(s_edges_in, 16)
            sp.dma_start(dsti[ER - 1:ER, 0:ETAIL], a["dst"][(ER - 1) * P:E].rearrange("(p t) -> p t", p=1)).then_inc(s_edges_in, 16)

            sp.wait_ge(s_xpad, 1)
            sp.dma_start(xs[:, 0:NC - 1, :], a["x"][0:(NC - 1) * P].rearrange("(m p) n -> p m n", p=P)).then_inc(s_x, 16)
            sp.dma_start(xs[0:LAST, NC - 1, :], a["x"][(NC - 1) * P:N]).then_inc(s_x, 16)
            for t, name in ((raw20, "edge_attr_20"), (raw4, "edge_attr_4"), (raw8, "edge_attr_8"), (raw8b, "edge_attr_8_n2")):
                sp.dma_start(t, a[name].rearrange("(p j) f -> p j f", p=ETP)).then_inc(s_raw, 16)
            sp.dma_start(rawt, a["edge_type_2"].rearrange("(p j) -> p j", p=ETP)).then_inc(s_raw, 16)
            sp.dma_start(raww, a["edge_weight"].rearrange("(p j) -> p j", p=ETP)).then_inc(s_raw, 16)
            sp.dma_start(rawsd[:, 0], a["src"].rearrange("(p j) -> p j", p=ETP)).then_inc(s_raw, 16)
            sp.dma_start(rawsd[:, 1], a["dst"].rearrange("(p j) -> p j", p=ETP)).then_inc(s_raw, 16)
            sp.dma_start(wqkv, a["L0_gnn_Wqkv"].rearrange("(k p) n -> p k n", p=P)).then_inc(s_wqkv, 16)
            sp.dma_start(bqkv, a["L0_gnn_bqkv"].rearrange("(o n) -> o n", o=1).to_broadcast([P, 3 * D])).then_inc(s_wqkv, 16)
            with nc.allow_non_contiguous_dma(reason="a few columns of parameters"):
                for j, name in enumerate(("L0_gnn_ln1_g", "L0_gnn_ln1_b", "L0_gnn_ln2_g", "L0_gnn_ln2_b")):
                    sp.dma_start(lng[:, j // 2, j % 2, :], a[name].rearrange("(k p) -> p k", p=P)).then_inc(s_par, 16)
                sp.dma_start(b1c[:, :], a["L0_gnn_b1"].rearrange("(k p) -> p k", p=P)).then_inc(s_par, 16)
            for j, name in enumerate(("L0_gnn_bo", "L0_gnn_b2")):
                sp.dma_start(rows[:, j, :], a[name].rearrange("(o n) -> o n", o=1).to_broadcast([P, D])).then_inc(s_par, 16)
            sp.wait_ge(s_table, 1)
            sp.dma_start(etab_d.rearrange("(p j) f -> p j f", p=ETP), etab).then_inc(s_etab, 16)
            sp.wait_ge(s_by_dve, NC)
            sp.dma_start(q_d.rearrange("(m p) n -> p m n", p=P), qv[:, 0]).then_inc(s_q_out, 16)
            sp.wait_ge(s_by_dve, 3 * NC)
            sp.dma_start(v_d.rearrange("(m p) n -> p m n", p=P), qv[:, 1]).then_inc(s_v_out, 16)
            sp.wait_ge(s_etab, 16)
            sp.dma_start(wo, a["L0_gnn_Wo"].rearrange("(k p) n -> p k n", p=P)).then_inc(s_wo, 16)
            sp.dma_start(w1s, a["L0_gnn_W1"].rearrange("(k p) n -> p k n", p=P)).then_inc(s_w1, 16)
            with nc.allow_non_contiguous_dma(reason="a few numbers a block"):
                sp.wait_ge(s_ends, 1)
                sp.dma_start(ends_d, ends[:, :]).then_inc(s_ends_out, 16)
                sp.wait_ge(s_ends_out, 16)
                sp.dma_start(endh[:, :, :], ends_d.rearrange("(t h) v -> h t v", h=H)).then_inc(s_ends_in, 16)
                sp.wait_ge(s_carry, 1)
                sp.dma_start(carry_d.rearrange("(t h) v -> h t v", h=H), carh[:, :, :]).then_inc(s_carry_out, 16)
                sp.wait_ge(s_carry_out, 16)
                sp.dma_start(carry[:, :], carry_d).then_inc(s_carry_in, 16)
            sp.wait_ge(s_agg, 1)
            sp.dma_start(w2s, a["L0_gnn_W2"].rearrange("(k p) n -> p k n", p=P)).then_inc(s_w2, 16)
            sp.wait_ge(s_f1zero, 1)
            for w, name in ((w_in[:, 0], "w_in2f_s"), (w_in[:, 1], "w_in2f_v"), (w_f1[0:20], "W1"), (w_o1s, "w_f2o1_s"),
                            (w_o1v[0:64], "w_f2o1_v"), (w_o1v[64:128], "w_f2o1_v"), (w_o2[:, 0], "w_f2o2_s"), (w_o2[:, 1], "w_f2o2_v")):
                sp.dma_start(w, a["L1_gnn_" + name]).then_inc(s_l1w, 16)
            sp.dma_start(w_f1[33:34], a["L1_gnn_b1"].rearrange("(o n) -> o n", o=1)).then_inc(s_l1w, 16)
            for j in range(4):
                sp.dma_start(w_f2[F1 * j:F1 * (j + 1)], a["L1_gnn_W2"]).then_inc(s_l1w, 16)
            sp.dma_start(b_f2, a["L1_gnn_b2"].rearrange("(o n) -> o n", o=1).to_broadcast([P, 192])).then_inc(s_l1w, 16)
            sp.wait_ge(s_by_act, plan.by[:plan.number("in2f", NC - 1)].count("act"))
            sp.dma_start(u_d.rearrange("(m p) n -> p m n", p=P), uS).then_inc(s_u_out, 16)
            for l in range(2):
                sp.dma_start(attb[:, l, :], a[f"L3_gnn_att{l + 1}"].rearrange("r b -> (r b)").rearrange("(o n) -> o n", o=1).to_broadcast([P, 2 * NBASE])).then_inc(s_l3par, 16)
                sp.dma_start(rows[:, l, :], a[f"L3_gnn_bias{l + 1}"].rearrange("(o n) -> o n", o=1).to_broadcast([P, D])).then_inc(s_l3par, 16)
                with nc.allow_non_contiguous_dma(reason="a few columns of parameters"):
                    for r in range(2):
                        sp.dma_start(gw[:, l, r, :], a[f"L3_gnn_gate_w{l + 1}"][r, :, 0].rearrange("(k p) -> p k", p=P)).then_inc(s_l3par, 16)
            sp.wait_ge(s_job, plan.number("o2", NC - 1))
            sp.dma_start(raw, a["L2_gnn_W_init"].rearrange("(k p) n -> p k n", p=P)).then_inc(s_rawin, 16)
            sp.wait_ge(s_mean, 2)
            for l in range(LAYERS):
                before = ("wi", f"sb{l - 1}")[l > 0]
                for part, now in enumerate(("ws", "sf", "sb")):
                    sp.wait_ge(s_job, plan.number(before, K4 - 1))
                    sp.dma_start(raw, a["L2_gnn_W_self"][l, :, part * D:(part + 1) * D].rearrange("(k p) n -> p k n", p=P)).then_inc(s_rawin, 16)
                    before = f"{now}{l}"
                    if part:
                        if part == 2:
                            sp.wait_ge(s_job, plan.number(f"cf{l}", K4 - 1))
                        elif l:
                            sp.wait_ge(s_job, plan.number(f"cb{l - 1}", K4 - 1))
                        sp.dma_start(wn, a["L2_gnn_W_" + ("fwd", "bwd")[part - 1]][l].rearrange("(k p) n -> p k n", p=P)).then_inc(s_wnin, 16)
            sp.wait_ge(s_job, plan.number(f"L{LAYERS - 1}", NC - 1))
            for l in range(2):
                sp.dma_start(root[l], a[f"L3_gnn_root{l + 1}"].rearrange("(k p) n -> p k n", p=P)).then_inc(s_root, 16)
            sp.wait_ge(s_rel_out, 16)
            sp.dma_start(rel_w[0], rel_d).then_inc(s_rel_in, 16)
            sp.wait_ge(s_by_dve, plan.by.count("dve"))
            sp.dma_start(out[0:(NC - 1) * P].rearrange("(m p) n -> p m n", p=P), xs[:, 0:NC - 1, :]).then_inc(s_out, 16)
            sp.dma_start(out[(NC - 1) * P:N], xs[0:LAST, NC - 1, :]).then_inc(s_out, 16)
            sp.wait_ge(s_out, 32)

        @block.gpsimd
        def _(pool):
            step = Chain(pool, s_pool)
            pool.memset(dsti[:, :], NP).then_inc(s_fill, 1)
            step(pool.iota(iota[:, :], pattern=[[1, NP]], base=0, channel_multiplier=0,
                           allow_small_or_imprecise_dtypes=True))
            step(pool.tensor_copy(iota16[:, :], iota[:, :]))
            step(pool.iota(enum[:, :], pattern=[[1, P]], base=1, channel_multiplier=P,
                           allow_small_or_imprecise_dtypes=True))
            step(pool.memset(ones[:, :], 1.0))
            step(pool.memset(zeros[:, :], 0.0))
            for m in (ident, identb):
                step(pool.memset(m[:, :], 0.0))
                step(pool.affine_select(out=m[:, :], in_=m[:, :], compare_op=ALU.not_equal, fill=1.0,
                                        base=0, pattern=[[-1, P]], channel_multiplier=1))
            pool.affine_select(out=below[:, :], in_=ones[:, :], compare_op=ALU.is_gt, fill=0.0,
                               base=0, pattern=[[1, P]], channel_multiplier=-1).then_inc(s_const, 1)

            pool.memset(xs[:, NC - 1, :], 0.0).then_inc(s_xpad, 1)
            pool.wait_ge(s_raw, 128)
            pool.tensor_copy(etab[:, :, 0:20], raw20)
            pool.tensor_tensor(etab[:, :, 20:24], raw4, raww.unsqueeze(2).to_broadcast([ETP, ETJ, 4]), ALU.mult)
            pool.tensor_tensor(etab[:, :, 24:32], raw8, raw8b, ALU.add)
            pool.tensor_copy(etab[:, :, 32], rawt)
            pool.memset(etab[:, :, 33:34], 1.0)
            pool.tensor_copy(etab[:, :, 34], rawsd[:, 0])
            pool.tensor_copy(etab[:, :, 35], rawsd[:, 1]).then_inc(s_table, 1)
            pool.wait_ge(s_sorted, 1)
            pool.wait_ge(s_etab, 16)
            for t in range(NT):
                pool.indirect_dma_start(out=attr[:, t, :], out_offset=None, in_=etab_d,
                                        in_offset=bass.IndirectOffsetOnAxis(ap=eidx[:, t:t + 1], axis=0)).then_inc(s_att[t // PIECE], 16)
            pool.wait_ge(s_norm, 2)
            pool.wait_ge(s_par, 7 * 16)
            pool.tensor_tensor(hn[:, :, :], hn[:, :, :], rows[:, 0, :].unsqueeze(1).to_broadcast([P, NC, D]), ALU.add).then_inc(s_h1b, 1)
            pool.wait_ge(s_q_out, 16)
            for t in range(NT):
                if t % PIECE == 0:
                    pool.wait_ge(s_ids, t // PIECE + 1)
                pool.wait_ge(s_q_used[t % 4], t // 4 + 1)
                pool.indirect_dma_start(out=ring[:, t % 4, :], out_offset=None, in_=q_d,
                                        in_offset=bass.IndirectOffsetOnAxis(ap=srcx[:, t:t + 1], axis=0)).then_inc(s_q_in[t % 4], 16)
            pool.wait_ge(s_v_out, 16)
            for t in range(NT):
                if t >= 4:
                    pool.wait_ge(s_msg[t % 4], t // 4)
                else:
                    pool.wait_ge(s_q_used[t % 4], NT // 4 + 1)
                pool.indirect_dma_start(out=ring[:, t % 4, :], out_offset=None, in_=v_d,
                                        in_offset=bass.IndirectOffsetOnAxis(ap=srcx[:, t:t + 1], axis=0)).then_inc(s_v_in[t % 4], 16)
            pool.wait_ge(s_norm, 3)
            step(pool.tensor_tensor(xs[:, :, :], xs[:, :, :], hn[:, :, :], ALU.add))
            pool.tensor_tensor(xs[:, :, :], xs[:, :, :], rows[:, 1, :].unsqueeze(1).to_broadcast([P, NC, D]), ALU.add).then_inc(s_resid, 1)
            pool.memset(half[:, :], 0.5)
            pool.wait_ge(s_job, plan.number("ffn1", 15))
            pool.memset(w_f1, 0.0).then_inc(s_f1zero, 1)
            pool.wait_ge(s_l1w, 14 * 16)
            pool.tensor_scalar(w_o1s[32:64], w_o1s[32:64], 3.0 ** -0.5, None, ALU.mult).then_inc(s_is3, 1)
            pool.wait_ge(s_u_out, 16)
            for t in range(NT):
                if t >= 12:
                    pool.wait_ge(s_u_used[t // 4 % 3], t // 12)
                pool.indirect_dma_start(out=ringu[:, t % 12, :], out_offset=None, in_=u_d,
                                        in_offset=bass.IndirectOffsetOnAxis(ap=dstx[:, t:t + 1], axis=0)).then_inc(s_u_in[t % 12], 16)
            for l in range(2):
                if l == 0:
                    pool.wait_ge(s_free, 1)
                    pool.wait_ge(s_mean, 2)
                halves = a[f"L3_gnn_basis{l + 1}"].rearrange("b (c k p) n -> b c p k n", c=2, p=P)
                with pool.Fori(0, NBASE // 3) as i:
                    for u in range(6):
                        pool.wait_ge(s_bas_used[u % 3], i * 2 + (l * 2 * NBASE // 3 + u // 3 + 1))
                        pool.dma_start(bas[u % 3].rearrange("p (o k n) -> p o k n", o=1, k=2),
                                       halves[bass.ds(i * 3 + u // 2, 1), u % 2].rearrange("o p k n -> p o k n")).then_inc(s_bas_in[u % 3], 16)
                if l == 0:
                    pool.wait_ge(s_rel, 1)
                    pool.dma_start(rel_d, acc).then_inc(s_rel_out, 16)
            pool.wait_ge(s_norm, 6)
            pool.wait_ge(s_l3par, 8 * 16)
            pool.tensor_tensor(xs[:, :, :], xs[:, :, :], rows[:, 1, :].unsqueeze(1).to_broadcast([P, NC, D]), ALU.add).then_inc(s_xb, 1)

        @block.scalar
        def _(act):
            step = Chain(act, s_act)

            def norm(turn, dst, src, func):
                act.wait_ge(s_var, turn + 1)
                act.activation(std[:, :], var[:, :], ACT.Sqrt).then_inc(s_std, 1)
                act.wait_ge(s_stat, turn + 1)
                for m in range(NC):
                    last = act.activation(dst[:, m, :], src[:, m, :], func, bias=nmr[:, m:m + 1], scale=rstd[:, m:m + 1])
                last.then_inc(s_norm, 1)

            def take_turned(name, dst, count=K4, scale=None, shift=None):
                for k in range(count):
                    act.wait_ge(s_job, plan.number(name, k))
                    o = plan.slot(ps, name, k)[:, 0:NP]
                    if scale is None:
                        act.activation(dst[:, k, :], o, ACT.Copy).then_inc(s_by_act, 1)
                    else:
                        act.activation(dst[:, k, :], o, ACT.Identity, bias=shift[:, k:k + 1], scale=scale[:, k:k + 1]).then_inc(s_by_act, 1)

            norm(0, hn, xs, ACT.Relu)
            norm(1, nrm, hn, ACT.Identity)
            act.wait_ge(s_par, 7 * 16)
            take_turned("ln1T", hT, scale=lng[:, 0, 0, :], shift=lng[:, 0, 1, :])
            act.wait_ge(s_by_dve, 2 * NC)
            act.activation(kH, kf, ACT.Copy).then_inc(s_kH, 1)
            with act.Fori(0, NB4) as i:
                act.wait_ge(s_turned, i + 1)
                act.activation(hotT, ps[:, 0:4 * P], ACT.Copy).then_inc(s_hotT, 1)
            act.wait_ge(s_akT, 1)
            act.activation(aT, ps[0:112, 0:768], ACT.Copy).then_inc(s_ak, 1)
            act.wait_ge(s_akT, 2)
            act.activation(kT, ps[0:112, 1024:1024 + 768], ACT.Copy).then_inc(s_ak, 1)
            act.wait_ge(s_shift, 1)
            act.activation(lg[:, :, :], lga[:, :, :], ACT.Exp).then_inc(s_prob, 1)

            def widen():
                with act.Fori(0, NB4 // 3) as i:
                    for k in range(3):
                        act.wait_ge(s_hot4_used[k], i + 1)
                        act.activation(hot4[:, k, :].rearrange("p (t d) -> p t d", d=P),
                                       hot[:, bass.ds(i * 12 + 4 * k, 4), :], ACT.Copy).then_inc(s_hot4, 1)

            widen()
            take_turned("aggT", hT)
            norm(2, nrm, hn, ACT.Identity)
            take_turned("ln2T", hT, scale=lng[:, 1, 0, :], shift=lng[:, 1, 1, :])
            for j in range(16):
                act.wait_ge(s_job, plan.number("ffn1", j))
                act.activation(g1T[:, j, :], plan.slot(ps, "ffn1", j)[:, 0:NP], ACT.Gelu, bias=b1c[:, j:j + 1]).then_inc(s_by_act, 1)

            def take(name, j, dst, width=D, func=ACT.Copy, **how):
                act.wait_ge(s_job, plan.number(name, j))
                act.activation(dst, plan.slot(ps, name, j)[:, 0:width], func, **how).then_inc(s_by_act, 1)

            def softplus(z, t):
                step(act.activation(t, z, ACT.Abs))
                step(act.activation(t, t, ACT.Exp, scale=-1.0))
                act.activation(t, t, ACT.Ln, scale=0.5, bias=half[:, :]).then_inc(s_z, 1)

            norm(3, hn, xs, ACT.Relu)
            take_turned("h1T", hT)
            for m in range(NC):
                take("in2f", m, uS[:, m, :], P, scale=float(B1) ** -0.5)
            for g in range(NB4):
                act.wait_ge(s_job, plan.number("attT", g))
                act.activation(attT[:, g, :], plan.slot(ps, "attT", g)[0:FEAT, 0:4 * P], ACT.Copy).then_inc(s_by_act, 1)
            for g in range(7):
                take("hid", g, zf[:, 3 * P * g:3 * P * (g + 1)], 3 * P)
            act.wait_ge(s_by_act, plan.by[:plan.number("hid", 6)].count("act"))
            act.wait_ge(s_is3, 1)
            softplus(zf, tf)
            with act.Fori(0, NB4 // 3) as i:
                for k in range(3):
                    act.wait_ge(s_feat_full, i * 3 + (k + 1))
                    act.activation(featH[:, 4 * k:4 * k + 4, :], feat[:, 4 * k:4 * k + 4, :], ACT.Copy).then_inc(s_featH, 1)
            act.wait_ge(s_agg, 2)
            act.activation(agg1, ps[:, 0:NC * 512].rearrange("p (m n) -> p m n", n=512)[:, :, 0:NF], ACT.Copy).then_inc(s_agg1, 1)
            take_turned("f2T", hT, 2)
            for k in range(4):
                take("o1", k, oT[:, k, :], NP, scale=0.125)
            act.wait_ge(s_by_act, plan.by[:plan.number("o1", 3)].count("act"))
            softplus(oT[:, 0, :], tz)
            for r in range(2):
                act.wait_ge(s_counts, r + 1)
                act.activation(adj[r][:, :, 0:D], ps[:, 0:NC * D].rearrange("p (c n) -> p c n", n=D), ACT.Copy)
                act.activation(adj[r][:, :, D:NP], ps[:, NC * D:NC * D + NP].rearrange("p (c n) -> p c n", n=P), ACT.Copy).then_inc(s_adj, 1)
            for c in range(NC):
                take("meanT", c, meanf[:, c, :], NP)
            norm(4, hn, xs, ACT.Relu)
            for k in range(K4):
                take("wi", k, wsT[:, k, :])
            take_turned("h2T", hT)
            for m in range(NC):
                take("h0", m, hn[:, m, :], func=ACT.Relu)
            take_turned("hT", hT)
            act.wait_ge(s_mean, 2)
            for l in range(LAYERS):
                for name, dst in (("ws", wsT), ("sf", sfT), ("cf", cf), ("sb", sfT), ("cb", cb)):
                    for k in range(K4):
                        take(f"{name}{l}", k, dst[:, k, :])
                take_turned(f"F{l}", fTv)
                take_turned(f"B{l}", bTv)
                for m in range(NC):
                    take(f"L{l}", m, hn[:, m, :], func=ACT.Relu)
                if l < LAYERS - 1:
                    take_turned(f"hT{l}", hT)
            norm(5, hn, xs, ACT.Relu)
            for l in range(2):
                take_turned(f"T{l}", hT)
                for m in range(NC):
                    take(f"gate{l}", m, gate[:, m, :], 2, ACT.Sigmoid)
                act.wait_ge(s_by_act, plan.by[:plan.number(f"gate{l}", NC - 1)].count("act"))
                for r in range(2):
                    for m in range(NC):
                        last = act.activation(gx[:, r, m, :], hn[:, m, :], ACT.Copy, scale=gate[:, m, r:r + 1])
                    last.then_inc(s_gx, 1)
                take_turned(f"P{l}0", fTv)
                take_turned(f"P{l}1", bTv)

        @block.vector
        def _(dve):
            step = Chain(dve, s_dve)

            def rank(turn, bins):
                oh = onehot[:, 0:bins * P].rearrange("p (b t) -> p b t", t=P)
                pre = prefix[:, 0:bins * P].rearrange("p (b t) -> p b t", t=P)
                end, cnt, tot, excl, off, incl = (small[:, j, 0:bins] for j in range(6))
                step(dve.tensor_tensor(oh, key[:, :].unsqueeze(1).to_broadcast([ER, bins, P]),
                                       iota[0:ER, 0:bins].unsqueeze(2).to_broadcast([ER, bins, P]), ALU.is_equal))
                step(dve.tensor_tensor_scan(prefix[:, 0:bins * P], onehot[:, 0:bins * P], onehot[:, 0:bins * P],
                                            0.0, ALU.add, ALU.max))
                step(dve.tensor_copy(end, pre[:, :, P - 1]))
                step(dve.tensor_copy(cnt, end))
                dve.tensor_tensor(cnt[:, 1:bins], end[:, 1:bins], end[:, 0:bins - 1], ALU.subtract).then_inc(s_count, 1)
                dve.wait_ge(s_count, turn + 1)
                dve.wait_ge(s_prefix, turn + 1)
                above, every = ps[0:ER, 0:bins], ps[0:ER, 64:64 + bins]
                step(dve.tensor_copy(tot, every))
                step(dve.tensor_tensor_scan(incl, tot, tot, 0.0, ALU.add, ALU.max))
                step(dve.tensor_tensor(excl, incl, tot, ALU.subtract))
                step(dve.scalar_tensor_tensor(off, above, -1.0, cnt, ALU.add, ALU.add))
                step(dve.tensor_tensor(off, off, end, ALU.subtract))
                step(dve.tensor_tensor(off, off, excl, ALU.add))
                if turn == 1:
                    nch = bins // 4
                    ctot, cincl, cexcl = (small[:, 6, 8 * j:8 * j + nch] for j in range(3))
                    step(dve.tensor_reduce(ctot, tot.rearrange("p (c b) -> p c b", b=4), AX.X, ALU.add))
                    ci = chi[:, 0:nch]
                    step(dve.tensor_scalar(ci, ctot, float(P - 1), None, ALU.add))
                    step(dve.tensor_scalar(ci, ci, 7, 7, ALU.arith_shift_right, ALU.arith_shift_left))
                    step(dve.tensor_copy(ctot, ci))
                    step(dve.tensor_tensor_scan(cincl, ctot, ctot, 0.0, ALU.add, ALU.max))
                    step(dve.tensor_tensor(cexcl, cincl, ctot, ALU.subtract))
                    off4 = off.rearrange("p (c b) -> p c b", b=4)
                    first = excl.rearrange("p (c b) -> p c b", b=4)[:, :, 0]
                    step(dve.tensor_tensor(cincl, cexcl, first, ALU.subtract))
                    step(dve.tensor_tensor(off4, off4, cincl.unsqueeze(2).to_broadcast([ER, nch, 4]), ALU.add))
                    step(dve.tensor_scalar(cexcl, cexcl, 1.0 / P, None, ALU.mult))
                    step(dve.tensor_tensor(tch[:, :, :], iota[0:ER, 0:NT].unsqueeze(1).to_broadcast([ER, 4, NT]),
                                           cexcl[:, 1:NC].unsqueeze(2).to_broadcast([ER, NC - 1, NT]), ALU.is_ge))
                    step(dve.tensor_reduce(key[:, 0:NT], tch[:, :, :].rearrange("p c t -> p t c"), AX.X, ALU.add))
                    of4 = key[:, 0:NT].rearrange("p (g j) -> p g j", j=4)
                    packed = small[:, 7, 0:NT // 4]
                    step(dve.tensor_copy(packed, of4[:, :, 3]))
                    for j in (2, 1, 0):
                        step(dve.scalar_tensor_tensor(packed, packed, float(NC), of4[:, :, j], ALU.mult, ALU.add))
                    step(dve.tensor_copy(tchunk[:, :], packed))
                step(dve.tensor_tensor(pre, pre, off.unsqueeze(2).to_broadcast([ER, bins, P]), ALU.add))
                step(dve.tensor_tensor(pre, pre, oh, ALU.mult))
                step(dve.tensor_reduce(pos[:, :], pre.rearrange("p b t -> p t b"), AX.X, ALU.add))
                step(dve.tensor_copy(posi[:, :], pos[:, :]))
                step(dve.tensor_scalar(digi[:, 0, :], posi[:, :], 7, None, ALU.arith_shift_right))
                step(dve.tensor_scalar(digi[:, 1, :], posi[:, :], P - 1, None, ALU.bitwise_and))
                dve.tensor_copy(dig[:, :, :], digi[:, :, :]).then_inc(s_ranked, 1)
                dve.wait_ge(s_ranked, turn + 1)

            def write_hots(by, turn, rows, cols):
                with dve.Fori(0, P // 8) as i:
                    for half in range(2):
                        dve.wait_ge(s_hot_read[half], i + (turn * (P // 8) + 1))
                        four = slice(4 * half, 4 * half + 4)
                        dve.tensor_tensor(rowhot[:, four, 0:rows], iota[0:ER, 0:rows].unsqueeze(1).to_broadcast([ER, 4, rows]),
                                          dig[:, by, bass.ds(i * 8 + 4 * half, 4)].unsqueeze(2).to_broadcast([ER, 4, rows]), ALU.is_equal)
                        for j in range(4):
                            at = bass.ds(i * 8 + (4 * half + j), 1)
                            last = dve.tensor_scalar(colhot[:, 4 * half + j, 0:cols], iota[0:ER, 0:cols], dig[:, 1 - by, at],
                                                     load[:, at], ALU.is_equal, ALU.mult)
                        last.then_inc(s_hots[half], 1)

            dve.wait_ge(s_edges_in, 32)
            dve.wait_ge(s_const, 1)
            step(dve.tensor_scalar(loadi[:, :], dsti[:, :], 5, None, ALU.arith_shift_right))
            step(dve.scalar_tensor_tensor(load[:, :], dsti[:, :], float(NP), enum[:, :], ALU.is_lt, ALU.mult))
            step(dve.scalar_tensor_tensor(load[:, :], load[:, :], 32.0, loadi[:, :], ALU.mult, ALU.add))
            step(dve.tensor_scalar(keyi[:, :], dsti[:, :], LO_BINS - 1, None, ALU.bitwise_and))
            step(dve.tensor_copy(key[:, :], keyi[:, :]))
            rank(0, LO_BINS)
            write_hots(0, 0, ER, P)
            dve.wait_ge(s_permuted, 1)
            step(dve.tensor_copy(load[:, :], ps[0:ER, 512:512 + P]))
            step(dve.tensor_copy(loadi[:, :], ps[0:ER, 512:512 + P]))
            step(dve.tensor_scalar(keyi[:, :], loadi[:, :], 31, None, ALU.bitwise_and))
            step(dve.tensor_copy(key[:, :], keyi[:, :]))
            rank(1, HI_BINS)
            write_hots(1, 1, P, NT)
            dve.wait_ge(s_permuted, 2)
            step(dve.tensor_copy(reli[:, :], ps[:, 1024:1024 + NT]))
            step(dve.tensor_scalar(reli[:, :], reli[:, :], 5, None, ALU.arith_shift_right))
            dve.tensor_scalar(real[:, :], reli[:, :], 0.0, None, ALU.is_gt)
            dve.tensor_scalar(eidx[:, :], reli[:, :], -1.0, 0.0, ALU.add, ALU.max).then_inc(s_sorted, 1)

            def stats(turn, src):
                for m in range(NC):
                    last = dve.bn_stats(bst[:, m, :], src[:, m, :])
                step(last)
                for m in range(NC):
                    last = dve.bn_aggr(mv[:, m, :], bst[:, m, :])
                step(last)
                dve.tensor_scalar(var[:, :], mv[:, :, 1], 1e-5, None, ALU.add).then_inc(s_var, 1)
                dve.wait_ge(s_std, turn + 1)
                step(dve.reciprocal(rstd[:, :], std[:, :]))
                dve.scalar_tensor_tensor(nmr[:, :], mv[:, :, 0], -1.0, rstd[:, :], ALU.mult, ALU.mult).then_inc(s_stat, 1)

            dve.wait_ge(s_x, 32)
            stats(0, xs)
            dve.wait_ge(s_norm, 1)
            stats(1, hn)
            dve.wait_ge(s_wqkv, 32)
            for n, dst in enumerate((qv[:, 0], kf, qv[:, 1])):
                for m in range(NC):
                    dve.wait_ge(s_job, plan.number("qkv", n * NC + m))
                    dve.tensor_tensor(dst[:, m, :], plan.slot(ps, "qkv", n * NC + m)[:, 0:D], bqkv[:, n * D:(n + 1) * D],
                                      ALU.add).then_inc(s_by_dve, 1)
            dve.wait_ge(s_kH, 1)
            dve.tensor_tensor(kL, kf, kH, ALU.subtract).then_inc(s_kL, 1)
            dve.wait_ge(s_q_out, 16)
            dve.wait_ge(s_v_out, 16)
            for n in range(3):
                dve.wait_ge(s_att[n], 16 * PIECE)
                at = slice(n * PIECE, (n + 1) * PIECE)
                step(dve.tensor_copy(srcx[:, at], attr[:, at, 34]))
                dve.tensor_copy(dstx[:, at], attr[:, at, 35]).then_inc(s_ids, 1)
                dve.wait_ge(s_ids, n + 1)
                step(dve.tensor_scalar(reli[:, at], dstx[:, at], P - 1, None, ALU.bitwise_and))
                step(dve.scalar_tensor_tensor(rel[:, at], reli[:, at], 1.0, real[:, at], ALU.add, ALU.mult))
                step(dve.tensor_scalar(rel[:, at], rel[:, at], -1.0, None, ALU.add))
                dve.tensor_tensor(hot[:, at, :], iota[:, 0:P].unsqueeze(1).to_broadcast([P, PIECE, P]),
                                  rel[:, at].unsqueeze(2).to_broadcast([P, PIECE, P]), ALU.is_equal).then_inc(s_hot, 1)
            step(dve.scalar_tensor_tensor(segk[:, :], dstx[:, :], 1.0, real[:, :], ALU.add, ALU.mult))
            for j in range(4):
                dve.nop().then_inc(s_q_used[j], 1)
            with dve.Fori(0, NB4) as i:
                step.enter(i, 1)
                for j in range(4):
                    dve.wait_ge(s_q_in[j], i * 16 + 16)
                    dve.wait_ge(s_kg, i * 4 + (j + 1))
                    last = dve.tensor_tensor(msg[:, j, :], ring[:, j, :], ps[:, 512 * (4 + j):512 * (5 + j)], ALU.mult)
                    last.then_inc(s_q_used[j], 1)
                dve.wait_ge(s_q_used[3], i + 2)
                step(dve.tensor_reduce(lg[:, bass.ds(i * 4, 4), :], msg.rearrange("p s (h d) -> p (s h) d", d=DH), AX.X, ALU.add))
            step.leave(NB4)
            step(dve.scalar_tensor_tensor(lg[:, :, :], lg[:, :, :], float(D) ** -0.5, attr[:, :, 24:32], ALU.mult, ALU.add))
            dve.tensor_copy(lgp.rearrange("p g t h -> p t g h"), lg[:, :, :].rearrange("p (t g) h -> p t g h", g=TG))
            dve.tensor_copy(kp.rearrange("p g t h -> p t g h"),
                            segk[:, :].rearrange("p (t g) -> p t g", g=TG).unsqueeze(3).to_broadcast([P, TT, TG, H])).then_inc(s_soft, 1)
            dve.wait_ge(s_ak, 2)
            step(dve.memset(pen[:, :], 0.0))
            step(dve.tensor_tensor(pen[:, 1:768], kT[:, 1:768], kT[:, 0:767], ALU.not_equal))
            step(dve.tensor_scalar(pen[:, 1:768], pen[:, 1:768], -BIG, None, ALU.mult))

            def scans(start_f, start_b):
                dve.tensor_tensor_scan(fwd[:, :], pen[:, 0:768], aT[:, :], start_f, ALU.add, ALU.max)
                step(dve.tensor_tensor_scan(bwd[:, ::-1], pen[:, 768:0:-1], aT[:, ::-1], start_b, ALU.add, ALU.max))

            scans(-BIG, -BIG)
            dve.tensor_copy(ends[:, 0:1], fwd[:, 767:768])
            dve.tensor_copy(ends[:, 1:2], bwd[:, 0:1])
            dve.tensor_copy(ends[:, 2:3], kT[:, 0:1])
            dve.tensor_copy(ends[:, 3:4], kT[:, 767:768])
            dve.tensor_reduce(ends[:, 4:5], pen[:, 0:768], AX.X, ALU.min).then_inc(s_ends, 1)
            dve.wait_ge(s_ends_in, 16)
            seam, hop, run_f, run_b = (chd[:, j, :] for j in range(4))
            step(dve.memset(chd[:, :, :], 0.0))
            step(dve.memset(carh[:, :, :], -BIG))
            step(dve.tensor_tensor(seam[:, 1:TT], endh[:, 1:TT, 2], endh[:, 0:TT - 1, 3], ALU.not_equal))
            step(dve.tensor_scalar(seam, seam, -BIG, None, ALU.mult))
            step(dve.tensor_tensor(hop, seam, endh[:, :, 4], ALU.add))
            step(dve.tensor_tensor_scan(run_f, hop, endh[:, :, 0], -BIG, ALU.add, ALU.max))
            step(dve.tensor_tensor(carh[:, 1:TT, 0], run_f[:, 0:TT - 1], seam[:, 1:TT], ALU.add))
            step(dve.tensor_copy(hop, endh[:, :, 4]))
            step(dve.tensor_tensor(hop[:, 0:TT - 1], hop[:, 0:TT - 1], seam[:, 1:TT], ALU.add))
            step(dve.tensor_tensor_scan(run_b[:, ::-1], hop[:, ::-1], endh[:, ::-1, 1], -BIG, ALU.add, ALU.max))
            step(dve.tensor_tensor(carh[:, 0:TT - 1, 1], run_b[:, 1:TT], seam[:, 1:TT], ALU.add))
            step(dve.tensor_scalar(carh[:, :, :], carh[:, :, :], -BIG, None, ALU.max))
            dve.nop().then_inc(s_carry, 1)
            dve.wait_ge(s_carry_in, 16)
            scans(carry[:, 0:1], carry[:, 1:2])
            dve.tensor_tensor(aT[:, :], fwd[:, :], bwd[:, :], ALU.max).then_inc(s_max, 1)
            dve.wait_ge(s_maxT, 1)
            top = ps[:, 2048:2048 + TG * P].rearrange("p (g q) -> p g q", q=P)[:, :, 0:112]
            dve.tensor_tensor(lga[:, :, :].rearrange("p (t g) h -> p t g h", g=TG), lg[:, :, :].rearrange("p (t g) h -> p t g h", g=TG),
                              top.rearrange("p g (t h) -> p t g h", h=H), ALU.subtract).then_inc(s_shift, 1)
            dve.wait_ge(s_prob, 1)
            with dve.Fori(0, NB4) as i:
                for j in range(4):
                    dve.wait_ge(s_v_in[j], i * 16 + 16)
                    dve.wait_ge(s_msg_used[j], i + 1)
                    dve.tensor_tensor(msg[:, j, :].rearrange("p (h d) -> p h d", d=DH), ring[:, j, :].rearrange("p (h d) -> p h d", d=DH),
                                      lg[:, bass.ds(i * 4 + j, 1), :].rearrange("p o h -> p (o h)").unsqueeze(2).to_broadcast([P, H, DH]), ALU.mult).then_inc(s_msg[j], 1)
            dve.wait_ge(s_agg, 1)
            step(dve.tensor_scalar(sums[:, :, :], ps[:, 2560:2560 + NC * H].rearrange("p (m h) -> p m h", h=H), 0.5, None, ALU.max))
            step(dve.reciprocal(sums[:, :, :], sums[:, :, :]))
            for m in range(NC):
                last = dve.tensor_tensor(agg[:, m, :].rearrange("p (h d) -> p h d", d=DH), ps[:, 512 * m:512 * (m + 1)].rearrange("p (h d) -> p h d", d=DH),
                                         sums[:, m, :].unsqueeze(2).to_broadcast([P, H, DH]), ALU.mult)
            last.then_inc(s_aggn, 1)
            dve.wait_ge(s_h1b, 1)
            for m in range(NC):
                dve.wait_ge(s_job, plan.number("wo", m))
                dve.tensor_tensor(hn[:, m, :], plan.slot(ps, "wo", m)[:, 0:D], hn[:, m, :], ALU.add).then_inc(s_by_dve, 1)
            dve.wait_ge(s_by_dve, plan.by[:plan.number("wo", NC - 1)].count("dve"))
            stats(2, hn)
            dve.wait_ge(s_resid, 1)
            for m in range(NC):
                dve.wait_ge(s_job, plan.number("ffn2", m))
                dve.tensor_tensor(xs[:, m, :], plan.slot(ps, "ffn2", m)[:, 0:D], xs[:, m, :], ALU.add).then_inc(s_by_dve, 1)
            dve.wait_ge(s_by_dve, plan.by[:plan.number("ffn2", NC - 1)].count("dve"))
            stats(3, xs)
            dve.wait_ge(s_is3, 1)
            step(dve.memset(small_w[:, 1152:1664], 0.0))
            for j in range(4):
                lanes = slice(F1 * j, F1 * (j + 1))
                step(dve.tensor_copy(w_bd[lanes, j, :].rearrange("p (c f) -> p c f", f=F1),
                                     w_f2[lanes].rearrange("p (f c) -> p c f", c=6)[:, 0:4, :]))
            dve.wait_ge(s_z, 1)
            dve.scalar_tensor_tensor(zf, zf, 0.0, tf, ALU.max, ALU.add).then_inc(s_ssp, 1)
            step(dve.tensor_copy(b_fc.rearrange("p (c f) -> p c f", f=F1), b_f2.rearrange("p (f c) -> p c f", c=6)[:, 0:4, :]))
            for g in range(NB4):
                dve.wait_ge(s_job, plan.number("filt", g))
                dve.tensor_tensor(filt[:, g:g + 63 + 1:21, :], plan.slot(ps, "filt", g)[:, 0:4 * P].rearrange("p (j n) -> p j n", n=P),
                                  b_fc.unsqueeze(1).to_broadcast([P, 4, P]), ALU.add).then_inc(s_by_dve, 1)
            dve.wait_ge(s_by_dve, plan.by[:plan.number("filt", NB4 - 1)].count("dve"))
            step(dve.scalar_tensor_tensor(srcf[:, :], srcx[:, :], 1.0, real[:, :], ALU.add, ALU.mult))
            step(dve.tensor_scalar(srcf[:, :], srcf[:, :], -1.0, None, ALU.add))
            with dve.Fori(0, NB4 // 3) as i:
                step.enter(i, 6)
                for k in range(3):
                    for j in range(4):
                        dve.wait_ge(s_u_in[4 * k + j], i * 16 + 16)
                    dve.wait_ge(s_feat_used[k], i + 1)
                    u = ringu[:, 4 * k:4 * k + 4, :]
                    s = u[:, :, 0:F1]
                    v = u[:, :, F1:P].rearrange("p s (c f) -> p s c f", c=3)
                    w = filt[:, bass.ds(i * 12 + 4 * k, 4), :]
                    y = attr[:, bass.ds(i * 12 + 4 * k, 4), 20:24]
                    ys = y[:, :, 0:1].to_broadcast([P, 4, F1])
                    yv = y[:, :, 1:4].unsqueeze(3).to_broadcast([P, 4, 3, F1])
                    f = feat[:, 4 * k:4 * k + 4, :]
                    fv = f[:, :, 2 * F1:NF].rearrange("p s (c w f) -> p s c w f", c=3, w=2)
                    dve.tensor_tensor(t1, w[:, :, 0:F1], ys, ALU.mult)
                    dve.tensor_tensor(t2, w[:, :, 2 * F1:3 * F1], s, ALU.mult)
                    dve.tensor_tensor(t3, w[:, :, 3 * F1:4 * F1], ys, ALU.mult)
                    step(dve.tensor_tensor(t4, v, yv, ALU.mult))
                    dve.tensor_tensor(f[:, :, 0:F1], t1, s, ALU.mult)
                    dve.tensor_tensor(fv[:, :, :, 0, :], t2.unsqueeze(2).to_broadcast([P, 4, 3, F1]), yv, ALU.mult)
                    dve.tensor_tensor(fv[:, :, :, 1, :], t3.unsqueeze(2).to_broadcast([P, 4, 3, F1]), v, ALU.mult).then_inc(s_u_used[k], 1)
                    step(dve.tensor_reduce(t5, t4.rearrange("p s c f -> p s f c"), AX.X, ALU.add))
                    dve.tensor_tensor(f[:, :, F1:2 * F1], t5, w[:, :, F1:2 * F1], ALU.mult).then_inc(s_feat_full, 1)
                    for j in range(4):
                        dve.tensor_scalar(hotL[k][:, j, :], iota[:, :], srcf[:, bass.ds(i * 12 + (4 * k + j), 1)], None, ALU.is_equal)
                    dve.wait_ge(s_featH, i * 3 + (k + 1))
                    dve.tensor_tensor(featL[:, 4 * k:4 * k + 4, :], f, featH[:, 4 * k:4 * k + 4, :], ALU.subtract).then_inc(s_feat, 1)
            step.leave(NB4 // 3)
            dve.wait_ge(s_z, 2)
            dve.scalar_tensor_tensor(oT[:, 0, :], oT[:, 0, :], 0.0, tz, ALU.max, ALU.add).then_inc(s_ssp, 1)
            for m in range(NC):
                dve.wait_ge(s_job, plan.number("o2", m))
                o = plan.slot(ps, "o2", m)
                dve.scalar_tensor_tensor(xs[:, m, 0:B1], o[:, 0:B1], float(B1) ** -0.5, xs[:, m, 0:B1], ALU.mult, ALU.add)
                xv = xs[:, m, B1:D].rearrange("p (d c) -> p c d", c=3)
                dve.scalar_tensor_tensor(xv, o[:, B1:D].rearrange("p (c d) -> p c d", c=3), float(B1) ** -0.5, xv, ALU.mult, ALU.add).then_inc(s_by_dve, 1)
            step(dve.tensor_scalar(tmask[:, 0, :], attr[:, :, 32], 0.0, None, ALU.is_equal))
            step(dve.tensor_scalar(tmask[:, 1, :], attr[:, :, 32], 0.0, None, ALU.not_equal))
            dve.nop().then_inc(s_free, 1)
            for r in range(2):
                with dve.Fori(0, NB4) as i:
                    for j in range(4):
                        dve.wait_ge(s_hs_used[j], i + (r * NB4 + 1))
                        at = bass.ds(i * 4 + j, 1)
                        dve.tensor_scalar(hotS[:, j, :], iota16[:, :], srcf[:, at], None, ALU.is_equal)
                        dve.tensor_scalar(hotD[:, j, :], iota16[:, 0:P], rel[:, at], tmask[:, r, at], ALU.is_equal, ALU.mult).then_inc(s_hs[j], 1)
            dve.wait_ge(s_adj, 2)
            step(dve.tensor_tensor(both, adj[0], adj[1], ALU.add))
            step(dve.tensor_reduce(deg[:, :], both, AX.X, ALU.add))
            step(dve.tensor_scalar(deg[:, :], deg[:, :], 1.0, None, ALU.max))
            step(dve.reciprocal(deg[:, :], deg[:, :]))
            dve.tensor_tensor(bymean, both, deg[:, :].unsqueeze(2).to_broadcast([P, NC, NP]), ALU.mult).then_inc(s_mean, 1)
            dve.wait_ge(s_job, plan.number("deg", 0))
            dve.tensor_scalar(degd, plan.slot(ps, "deg", 0)[:, 0:NP], 1.0, None, ALU.max).then_inc(s_by_dve, 1)
            dve.wait_ge(s_by_dve, plan.by[:plan.number("deg", 0)].count("dve"))
            step(dve.reciprocal(degd, degd))
            dve.tensor_tensor(meanb, both, degd.unsqueeze(1).to_broadcast([P, NC, NP]), ALU.mult).then_inc(s_mean, 1)
            stats(4, xs)

            def combine(l):
                step(dve.memset(acc, 0.0))
                with dve.Fori(0, NBASE // 3) as i:
                    step.enter(i, 6)
                    for u in range(6):
                        dve.wait_ge(s_bas_in[u % 3], i * 32 + (16 * (l * 2 * NBASE // 3 + u // 3) + 16))
                        part = slice(u % 2 * 1024, u % 2 * 1024 + 1024)
                        for r in range(2):
                            last = dve.scalar_tensor_tensor(acc[:, r, part], bas[u % 3], attb[:, l, bass.ds(i * 3 + (u // 2 + r * NBASE), 1)],
                                                            acc[:, r, part], ALU.mult, ALU.add)
                            if r == 0:
                                step(last)
                        last.then_inc(s_bas_used[u % 3], 1)
                        dve.wait_ge(s_bas_used[u % 3], i * 2 + (l * 2 * NBASE // 3 + u // 3 + 2))
                step.leave(NBASE // 3)
                dve.nop().then_inc(s_rel, 1)

            dve.wait_ge(s_l3par, 8 * 16)
            for j in range(3):
                dve.nop().then_inc(s_bas_used[j], 1)
            combine(0)
            dve.wait_ge(s_rel_out, 16)
            combine(1)
            dve.wait_ge(s_by_act, plan.by[:plan.number(f"L{LAYERS - 1}", NC - 1)].count("act"))
            step(dve.tensor_tensor(xs[:, :, :], xs[:, :, :], hn[:, :, :], ALU.add))
            stats(5, xs)
            for m in range(NC):
                dve.wait_ge(s_job, plan.number("O0", m))
                dve.tensor_tensor(hn[:, m, :], plan.slot(ps, "O0", m)[:, 0:D], rows[:, 0, :], ALU.add).then_inc(s_by_dve, 1)
            dve.wait_ge(s_by_dve, plan.by[:plan.number("O0", NC - 1)].count("dve"))
            dve.tensor_scalar(hn[:, :, :], hn[:, :, :], 0.0, None, ALU.max).then_inc(s_h3, 1)
            dve.wait_ge(s_xb, 1)
            for m in range(NC):
                dve.wait_ge(s_job, plan.number("O1", m))
                dve.tensor_tensor(xs[:, m, :], plan.slot(ps, "O1", m)[:, 0:D], xs[:, m, :], ALU.add).then_inc(s_by_dve, 1)

        @block.tensor
        def _(pe):
            def counts(turn, bins):
                pe.wait_ge(s_count, turn + 1)
                cnt = small[:, 1, 0:bins]
                pe.matmul(ps[0:ER, 0:bins], below[0:ER, 0:ER], cnt, start=True, stop=True)
                pe.matmul(ps[0:ER, 64:64 + bins], ones[0:ER, 0:ER], cnt, start=True, stop=True).then_inc(s_prefix, 1)

            def permute(turn, rows, cols):
                bank = ps[0:rows, 512 * (turn + 1):512 * (turn + 1) + cols]
                pe.matmul(bank, zeros[0:ER, 0:rows], zeros[0:ER, 0:cols], start=True, stop=False)
                with pe.Fori(0, P // 8) as i:
                    for half in range(2):
                        pe.wait_ge(s_hots[half], i + (turn * (P // 8) + 1))
                        for j in range(4 * half, 4 * half + 4):
                            last = pe.matmul(bank, rowhot[:, j, 0:rows], colhot[:, j, 0:cols], start=False, stop=False)
                        last.then_inc(s_hot_read[half], 1)
                pe.matmul(bank, zeros[0:ER, 0:rows], zeros[0:ER, 0:cols], start=False, stop=True).then_inc(s_permuted, 1)

            for half in range(2):
                pe.nop().then_inc(s_hot_read[half], 1)
            pe.wait_ge(s_const, 1)
            counts(0, LO_BINS)
            permute(0, ER, P)
            counts(1, HI_BINS)
            permute(1, P, NT)

            def turn_nodes(name, src, count=K4, cols=lambda k: slice(k * P, (k + 1) * P)):
                for k in range(count):
                    plan.open(pe, name, k)
                    o = plan.slot(ps, name, k)
                    for m in range(NC):
                        last = pe.transpose(o[:, m * P:(m + 1) * P], src[:, m, cols(k)], ident[:, :])
                    last.then_inc(s_job, 1)

            def product(name, j, width, pairs):
                plan.open(pe, name, j)
                o = plan.slot(ps, name, j)
                for at in range(0, width, D):
                    to = min(at + D, width)
                    for n, (lhsT, rhs) in enumerate(pairs):
                        last = pe.matmul(o[:, at:to], lhsT, rhs[:, at:to], start=n == 0, stop=n == len(pairs) - 1)
                last.then_inc(s_job, 1)

            def node(t, k, m):
                return t[:, k, m * P:(m + 1) * P]

            pe.wait_ge(s_norm, 2)
            turn_nodes("ln1T", nrm)
            pe.wait_ge(s_wqkv, 32)
            for n in range(3):
                for m in range(NC):
                    if m == 0 and n == 0:
                        plan.wait_taken(pe, plan.number("ln1T", K4 - 1) - 1)
                    product("qkv", n * NC + m, D, [(node(hT, k, m), wqkv[:, k, n * D:(n + 1) * D]) for k in range(K4)])
            plan.wait_taken(pe, plan.number("qkv", 3 * NC - 1) - 1)
            pe.wait_ge(s_hot, 3)
            pe.wait_ge(s_kL, 1)

            def tile_chunks(g):
                four = pe.value_load(tchunk[0:1, bass.ds(g, 1)], min_val=0, max_val=NC ** 4 - 1)
                return [four // NC ** j % NC for j in range(4)]

            with pe.Fori(0, NB4) as i:
                for j in range(4):
                    last = pe.matmul(ps[:, j * P:(j + 1) * P], hot[:, bass.ds(i * 4 + j, 1), :].rearrange("p o d -> p (o d)"), identb[:, :], start=True, stop=True)
                last.then_inc(s_turned, 1)
                chunks = tile_chunks(i * 1)
                pe.wait_ge(s_hotT, i + 1)
                for j, c in enumerate(chunks):
                    pe.wait_ge(s_q_used[j], i + 1)
                    for n, k in enumerate((kH, kL)):
                        last = pe.matmul(ps[:, 512 * (4 + j):512 * (5 + j)], hotT[:, j * P:(j + 1) * P],
                                         k[:, bass.ds(c, 1), :].rearrange("p o n -> p (o n)"), start=n == 0, stop=n == 1)
                    last.then_inc(s_kg, 1)
            pe.wait_ge(s_soft, 1)
            for n, src in enumerate((lgp, kp)):
                for g in range(TG):
                    last = pe.transpose(ps[0:112, 1024 * n + g * P:1024 * n + (g + 1) * P], src[:, g].rearrange("p t h -> p (t h)"), ident[:, :])
                last.then_inc(s_akT, 1)
            pe.wait_ge(s_max, 1)
            for g in range(TG):
                last = pe.transpose(ps[:, 2048 + g * P:2048 + g * P + 112], aT[:, g * P:(g + 1) * P], ident[0:112, 0:112])
            last.then_inc(s_maxT, 1)

            def open_sums(width, banks=NC):
                for m in range(banks):
                    pe.matmul(ps[:, 512 * m:512 * m + width], zeros[:, 0:P], iota[:, 0:width], start=True, stop=False)

            def close_sums(width, banks=NC):
                for m in range(banks):
                    last = pe.matmul(ps[:, 512 * m:512 * m + width], zeros[:, 0:P], iota[:, 0:width], start=False, stop=True)
                return last

            pe.wait_ge(s_prob, 1)
            pe.wait_ge(s_const, 1)
            for used in s_msg_used + s_hot4_used:
                pe.nop().then_inc(used, 1)
            open_sums(D)
            pe.matmul(ps[:, 2560:2560 + NC * H], zeros[:, 0:P], iota[:, 0:NC * H], start=True, stop=False)
            with pe.Fori(0, NB4 // 3) as i:
                for k in range(3):
                    chunks = tile_chunks(i * 3 + k)
                    pe.wait_ge(s_hot4, i * 3 + (k + 1))
                    for j, c in enumerate(chunks):
                        pe.wait_ge(s_msg[j], i * 3 + (k + 1))
                        one = hot4[:, k, j * P:(j + 1) * P]
                        pe.matmul(ps[:, bass.ds(c * 512, D)], one, msg[:, j, :], start=False, stop=False, skip_group_check=True)\
                          .then_inc(s_msg_used[j], 1)
                        last = pe.matmul(ps[:, bass.ds(c * H + 2560, H)], one, lg[:, bass.ds(i * 12 + (4 * k + j), 1), :].rearrange("p o h -> p (o h)"),
                                         start=False, stop=False, skip_group_check=True)
                    last.then_inc(s_hot4_used[k], 1)
            close_sums(D)
            pe.matmul(ps[:, 2560:2560 + NC * H], zeros[:, 0:P], iota[:, 0:NC * H], start=False, stop=True).then_inc(s_agg, 1)
            pe.wait_ge(s_aggn, 1)
            turn_nodes("aggT", agg)
            pe.wait_ge(s_wo, 16)
            plan.wait_taken(pe, plan.number("aggT", K4 - 1) - 1)
            for m in range(NC):
                product("wo", m, D, [(node(hT, k, m), wo[:, k, :]) for k in range(K4)])
            pe.wait_ge(s_norm, 3)
            turn_nodes("ln2T", nrm)
            pe.wait_ge(s_w1, 16)
            plan.wait_taken(pe, plan.number("ln2T", K4 - 1) - 1)
            for j in range(16):
                product("ffn1", j, NP, [(w1s[:, k, j * P:(j + 1) * P], hT[:, k, :]) for k in range(K4)])
            pe.wait_ge(s_w2, 16)
            plan.wait_taken(pe, plan.number("ffn1", 15) - 1)
            for m in range(NC):
                product("ffn2", m, D, [(node(g1T, j, m), w2s[:, j, :]) for j in range(16)])

            def taken(name, j):
                plan.wait_taken(pe, plan.number(name, j) - 1)

            pe.wait_ge(s_norm, 4)
            turn_nodes("h1T", hn, cols=lambda k: slice(0, P) if k == 0 else slice(P + k - 1, D, 3))
            pe.wait_ge(s_is3, 1)
            taken("h1T", K4 - 1)
            for m in range(NC):
                plan.open(pe, "in2f", m)
                for k in range(K4):
                    last = pe.matmul(plan.slot(ps, "in2f", m)[:, F1 * k:F1 * (k + 1)], node(hT, k, m), w_in[:, min(k, 1)], start=True, stop=True)
                last.then_inc(s_job, 1)
            for g in range(NB4):
                plan.open(pe, "attT", g)
                for j in range(4):
                    last = pe.transpose(plan.slot(ps, "attT", g)[0:FEAT, j * P:(j + 1) * P], attr[:, j * NB4 + g, :], ident[:, :])
                last.then_inc(s_job, 1)
            taken("attT", NB4 - 1)
            for g3 in range(7):
                plan.open(pe, "hid", g3)
                for g in range(3):
                    for j in range(4):
                        last = pe.matmul(plan.slot(ps, "hid", g3)[F1 * j:F1 * (j + 1), g * P:(g + 1) * P], w_f1,
                                         attT[:, 3 * g3 + g, j * P:(j + 1) * P], start=True, stop=True)
                last.then_inc(s_job, 1)
            pe.wait_ge(s_ssp, 1)
            for g in range(NB4):
                plan.open(pe, "filt", g)
                pe.matmul(plan.slot(ps, "filt", g)[:, 0:4 * P], zf[:, g * P:(g + 1) * P], small_w[:, 1152:1664], start=True, stop=True).then_inc(s_job, 1)
            for j in range(4):
                taken("filt", NB4 - 1 - j)
            for used in s_feat_used:
                pe.nop().then_inc(used, 1)
            open_sums(NF)
            with pe.Fori(0, NB4 // 3) as i:
                for k in range(3):
                    pe.wait_ge(s_feat, i * 3 + (k + 1))
                    for j in range(4):
                        for m in range(NC):
                            for part in (featH, featL):
                                last = pe.matmul(ps[:, 512 * m:512 * m + NF], hotL[k][:, j, m * P:(m + 1) * P], part[:, 4 * k + j, :],
                                                 start=False, stop=False)
                    last.then_inc(s_feat_used[k], 1)
            close_sums(NF).then_inc(s_agg, 1)
            pe.wait_ge(s_agg1, 1)
            turn_nodes("f2T", agg1, 2)
            taken("f2T", 1)
            product("o1", 0, NP, [(w_o1s, hT[0:64, 0, :])])
            for c in range(3):
                lanes = slice(64, 128) if c % 2 == 0 else slice(0, 64)
                product("o1", 1 + c, NP, [(w_o1v[lanes], hT[lanes, (c + 1) // 2, :])])
            pe.wait_ge(s_ssp, 2)
            taken("o1", 3)
            for m in range(NC):
                plan.open(pe, "o2", m)
                for k in range(4):
                    last = pe.matmul(plan.slot(ps, "o2", m)[:, k * P:(k + 1) * P], node(oT, k, m), w_o2[:, min(k, 1)], start=True, stop=True)
                last.then_inc(s_job, 1)
            for j in range(4):
                taken("o2", NC - 1 - j)
            for used in s_hs_used:
                pe.nop().then_inc(used, 1)
            for r in range(2):
                if r:
                    pe.wait_ge(s_adj, 1)
                open_sums(D, 7)
                with pe.Fori(0, NB4) as i:
                    chunks = tile_chunks(i * 1)
                    for j, c in enumerate(chunks):
                        pe.wait_ge(s_hs[j], i + (r * NB4 + 1))
                        pe.matmul(ps[:, bass.ds(c * D, D)], hotD[:, j, :], hotS[:, j, 0:D], start=False, stop=False, skip_group_check=True)
                        pe.matmul(ps[:, bass.ds(c * P + NC * D, P)], hotD[:, j, :], hotS[:, j, D:NP],
                                  start=False, stop=False, skip_group_check=True).then_inc(s_hs_used[j], 1)
                close_sums(D, 7).then_inc(s_counts, 1)
            pe.wait_ge(s_mean, 1)
            product("deg", 0, NP, [(ones[:, :], both[:, i, :]) for i in range(NC)])
            for c in range(NC):
                plan.open(pe, "meanT", c)
                for i in range(NC):
                    last = pe.transpose(plan.slot(ps, "meanT", c)[:, i * P:(i + 1) * P], bymean[:, i, c * P:(c + 1) * P], ident[:, :])
                last.then_inc(s_job, 1)

            def turn_weights(name, n):
                pe.wait_ge(s_rawin, 16 * n)
                for k in range(K4):
                    plan.open(pe, name, k)
                    for o in range(K4):
                        last = pe.transpose(plan.slot(ps, name, k)[:, o * P:(o + 1) * P], raw[:, o, k * P:(k + 1) * P], ident[:, :])
                    last.then_inc(s_job, 1)

            pe.wait_ge(s_norm, 5)
            turn_weights("wi", 1)
            turn_nodes("h2T", hn)
            taken("h2T", K4 - 1)
            for m in range(NC):
                product("h0", m, D, [(node(hT, k, m), wsT[:, k, :]) for k in range(K4)])
            taken("h0", NC - 1)
            turn_nodes("hT", hn)
            for l in range(LAYERS):
                turn_weights(f"ws{l}", 3 * l + 2)
                for p, (s, c) in enumerate((("sf", "cf"), ("sb", "cb"))):
                    turn_weights(f"{s}{l}", 3 * l + 3 + p)
                    pe.wait_ge(s_wnin, 16 * (2 * l + p + 1))
                    taken(f"{s}{l}", K4 - 1)
                    for k in range(K4):
                        product(f"{c}{l}", k, D, [(wn[:, o, k * P:(k + 1) * P], sfT[:, o, :]) for o in range(K4)])
                for name, mean in (("F", meanf), ("B", meanb)):
                    for k in range(K4):
                        product(f"{name}{l}", k, NP, [(hn[:, i, k * P:(k + 1) * P], mean[:, i, :]) for i in range(NC)])
                taken(f"B{l}", K4 - 1)
                for m in range(NC):
                    product(f"L{l}", m, D, [(node(t, k, m), w[:, k, :]) for t, w in ((hT, wsT), (fTv, cf), (bTv, cb)) for k in range(K4)])
                if l < LAYERS - 1:
                    taken(f"L{l}", NC - 1)
                    turn_nodes(f"hT{l}", hn)
            for l in range(2):
                if l == 0:
                    pe.wait_ge(s_norm, 6)
                    pe.wait_ge(s_root, 32)
                    pe.wait_ge(s_l3par, 8 * 16)
                else:
                    pe.wait_ge(s_h3, 1)
                turn_nodes(f"T{l}", hn)
                taken(f"T{l}", K4 - 1)
                for m in range(NC):
                    product(f"gate{l}", m, 2, [(node(hT, k, m), gw[:, l, :, k]) for k in range(K4)])
                for r in range(2):
                    pe.wait_ge(s_gx, 2 * l + r + 1)
                    for k in range(K4):
                        product(f"P{l}{r}", k, NP, [(gx[:, r, i, k * P:(k + 1) * P], adj[r][:, i, :]) for i in range(NC)])
                taken(f"P{l}1", K4 - 1)
                pe.wait_ge(s_rel_in, 16) if l == 0 else pe.wait_ge(s_rel, 2)
                wr = [rel_w[l][:, r].rearrange("p (k n) -> p k n", n=D) for r in range(2)]
                for m in range(NC):
                    product(f"O{l}", m, D, [(node(t, k, m), w[:, k, :]) for t, w in ((hT, root[l]), (fTv, wr[0]), (bTv, wr[1])) for k in range(K4)])


_INS = ['x', 'src', 'dst', 'edge_attr_20', 'edge_attr_4', 'edge_attr_8', 'edge_attr_8_n2', 'edge_type_2',
        'edge_weight', 'L0_gnn_Wqkv', 'L0_gnn_bqkv', 'L0_gnn_Wo', 'L0_gnn_bo', 'L0_gnn_ln1_g', 'L0_gnn_ln1_b',
        'L0_gnn_W1', 'L0_gnn_b1', 'L0_gnn_W2', 'L0_gnn_b2', 'L0_gnn_ln2_g', 'L0_gnn_ln2_b', 'L1_gnn_w_in2f_s',
        'L1_gnn_w_in2f_v', 'L1_gnn_W1', 'L1_gnn_b1', 'L1_gnn_W2', 'L1_gnn_b2', 'L1_gnn_w_f2o1_s',
        'L1_gnn_w_f2o1_v', 'L1_gnn_w_f2o2_s', 'L1_gnn_w_f2o2_v', 'L2_gnn_W_init', 'L2_gnn_W_fwd', 'L2_gnn_W_bwd',
        'L2_gnn_W_self', 'L3_gnn_basis1', 'L3_gnn_att1', 'L3_gnn_gate_w1', 'L3_gnn_root1', 'L3_gnn_bias1',
        'L3_gnn_basis2', 'L3_gnn_att2', 'L3_gnn_gate_w2', 'L3_gnn_root2', 'L3_gnn_bias2']


def kernel(**inputs):
    import numpy as _np
    import concourse.bacc as _bacc
    from concourse import mybir as _mybir
    from concourse.bass_utils import run_bass_kernel_spmd as _run

    nc = _bacc.Bacc("TRN2", target_bir_lowering=False, num_devices=1)
    arrays, args = {}, {}
    for name in _INS:
        a = _np.ascontiguousarray(inputs[name])
        arrays[f"in_{name}"] = a
        args[name] = nc.dram_tensor(f"in_{name}", a.shape, _mybir.dt.from_np(a.dtype), kind="ExternalInput").ap()
    out = nc.dram_tensor("out_x", (N, D), F32, kind="ExternalOutput").ap()
    build(nc, args, out)
    r = _run(nc, [arrays], core_ids=[0])
    return r.results[0]["out_x"]
```

```python
import concourse.bass as bass
from concourse import mybir
from contextlib import ExitStack

F32 = mybir.dt.float32
F32R = mybir.dt.float32r
BF16 = mybir.dt.bfloat16
F16 = mybir.dt.float16
I32 = mybir.dt.int32
ALU = mybir.AluOpType
ACT = mybir.ActivationFunctionType
AX = mybir.AxisListType

P = 128
N = 625
E = 10000
D = 512
H = 8
DH = D // H
NC = (N + P - 1) // P
NP = NC * P
LAST = N - (NC - 1) * P
ER = (E + P - 1) // P
ETAIL = E - (ER - 1) * P
NT = (E + NC * (P - 1)) // P + 1
LO_BINS = 32
HI_BINS = 24
BIG = 1.0e30
FEAT = 36
K4 = D // P


EARLY = [(_n, _l) for _l in range(3) for _n in ("ws", "sf", "cf", "sb", "cb")]
EARLY_IN = (0, 1, 2, 0, 1, 2, 0, 1, 0, 1, 3, 4, 5, 3, 4)
SORTING = 10


class Chain:

    def __init__(self, eng, sem):
        self.eng, self.sem, self.n, self.turn, self.per = eng, sem, 0, None, 0

    def __call__(self, ins):
        self.n += 1
        ins.then_inc(self.sem, 1)
        self.eng.wait_ge(self.sem, self.n if self.turn is None else self.turn * self.per + self.n)

    def enter(self, turn, per):
        self.turn, self.per, self.at = turn, per, self.n

    def leave(self, turns):
        assert self.n - self.at == self.per
        self.n = self.at + turns * self.per
        self.turn = None


class Plan:

    def __init__(self, stages, taken):
        self.taken, self.first, self.by = taken, {}, []
        for name, count, engine in stages:
            self.first[name] = len(self.by)
            self.by += [engine] * count

    def slot(self, ps, name, i):
        j = self.first[name] + i
        return ps[:, 1024 * (j % 4):1024 * (j % 4) + 1024]

    def wait_taken(self, pe, j):
        engine = self.by[j]
        pe.wait_ge(self.taken[engine], self.by[:j + 1].count(engine))

    def open(self, pe, name, i):
        j = self.first[name] + i
        if j >= 4:
            self.wait_taken(pe, j - 4)

    def number(self, name, i):
        return self.first[name] + i + 1


ATT1 = 14
LATER = [("attA", ATT1, "act"), ("h1T", K4, "act"), ("in2f", NC, "act"), ("attB", NT // 4 - ATT1, "act"), ("hid", 7, "act"), ("filt", NT // 4, "dve"),
         ("f2T", 2, "act"), ("o1", 4, "act"), ("o2", NC, "dve"),
         ("wi", K4, "act"), ("h2T", K4, "act"), ("h0", NC, "act"), ("hT", K4, "act"),
         ("deg", 1, "dve"), ("meanT", NC, "act")]
for _l in range(3):
    LATER += [(f"F{_l}", K4, "act"), (f"B{_l}", K4, "act"), (f"L{_l}", NC, "act")]
    if _l < 2:
        LATER.append((f"hT{_l}", K4, "act"))
for _l in range(2):
    LATER += [(f"T{_l}", K4, "act"), (f"gate{_l}", NC, "act"), (f"P{_l}0", K4, "act"), (f"P{_l}1", K4, "act"), (f"O{_l}", NC, "dve")]


def build(nc, a, out):
    with ExitStack() as ctx:
        def sb(name, shape, dt=F32):
            return ctx.enter_context(nc.sbuf_tensor(name, shape, dt))

        def sb_twice(name, shape):
            with nc.sbuf_tensor(name + "_r", shape, F32R) as rounded:
                pass
            return sb(name, shape), rounded

        def sem(name):
            return ctx.enter_context(nc.semaphore(name))

        iota = sb("iota", [P, NP])
        iota16 = sb("iota16", [P, NP], F16)
        ident = sb("ident", [P, P])
        identb = sb("identb", [P, P], BF16)
        ones = sb("ones", [P, P])
        below = sb("below", [P, P])
        zeros = sb("zeros", [P, 2 * P])
        work, work_r = sb_twice("work", [P, 12288])
        fT, fT_r = sb_twice("fT", [P, K4 * NP])
        sort = fT[0:ER, :].rearrange("p (j t) -> p j t", t=P)
        dsti = sort[:, 0].bitcast(I32)
        enum = sort[:, 2]
        load = sort[:, 3]
        loadi = sort[:, 4].bitcast(I32)
        key = sort[:, 6]
        keyi = sort[:, 7].bitcast(I32)
        pos = sort[:, 8]
        posi = sort[:, 9].bitcast(I32)
        digi = sort[:, 10:12].bitcast(I32)
        dig = sort[:, 12:14]
        small = sb("small", [ER, 8, LO_BINS])
        chi = sb("chi", [ER, 8], I32)
        onehot = work[0:ER, 0:2048].bitcast(BF16)
        prefix = work[0:ER, 2048:2048 + LO_BINS * P]
        rowhot, colhot = (work[0:ER, 6144 + 1024 * j:7168 + 1024 * j].rearrange("p (s w) -> p s w", w=P) for j in range(2))
        eidx = sb("eidx", [P, NT], I32)
        srcx = sb("srcx", [P, NT], I32)
        dstx = sb("dstx", [P, NT], I32)
        reli = sb("reli", [P, NT], I32)
        real = sb("real", [P, NT])
        rel = sb("rel", [P, NT])
        segk = sb("segk", [P, NT])
        tchunk = sb("tchunk", [ER, NT // 4], I32)
        tch = sb("tch", [ER, 4, NT])
        ps = ctx.enter_context(nc.psum_tensor("ps", [P, 4096], F32))

        s_fill = sem("s_fill")
        s_const = sem("s_const")
        s_edges_in = sem("s_edges_in")
        s_dve = sem("s_dve")
        s_pool = sem("s_pool")
        s_count = sem("s_count")
        s_prefix = sem("s_prefix")
        s_ranked = sem("s_ranked")
        s_hots = [sem(f"s_hots{h}") for h in range(2)]
        s_hot_read = [sem(f"s_hot_read{h}") for h in range(2)]
        s_permuted = sem("s_permuted")
        s_sorted = sem("s_sorted")

        xs = sb("xs", [P, NC, D])
        hn = sb("hn", [P, NC, D])
        hT, hT_r = sb_twice("hT", [P, K4, NP])
        bT, bT_r = sb_twice("bT", [P, K4 * NP])
        aux, aux_r = sb_twice("aux", [P, 10752])
        early_out = bT[:, 0:K4 * D].rearrange("p (k n) -> p k n", n=D)
        early_d = nc.dram_tensor("early_d", (3, P, 3, K4, D), F32).ap()
        wA, wA_r = sb_twice("wA", [P, 4 * 4 * D])
        att, att_r = sb_twice("att", [P, NT * FEAT])
        early_in = [w.rearrange("p (k n) -> p k n", n=D) for w in (
            work[:, 8192:10240], work[:, 10240:12288], att[:, 0:2048], wA[:, 0:2048], wA[:, 2048:4096], wA[:, 4096:6144])]
        early_s = [w.rearrange("p (k n) -> p k n", n=D) for w in (hT[:, :, :].rearrange("p k n -> p (k n)")[:, 0:K4 * D], wA[:, 6144:8192])]

        def early_bank(n):
            bank = 3 + n % 5 if n < K4 * SORTING else 6 + n % 2
            return ps[:, 512 * bank:512 * (bank + 1)]

        def early_source(step):
            kind, l = EARLY[step]
            if kind[0] == "c":
                src = a["L2_gnn_W_" + {"cf": "fwd", "cb": "bwd"}[kind]][l]
            else:
                part = ("ws", "sf", "sb").index(kind)
                src = a["L2_gnn_W_self"][l, :, part * D:(part + 1) * D]
            return src.rearrange("(k p) n -> p k n", p=P)

        attr = att[:, :].rearrange("p (t f) -> p t f", f=FEAT)
        nrm = aux[:, 8192:8192 + NC * D].rearrange("p (m n) -> p m n", n=D)
        bst = sb("bst", [P, NC, 6])
        mv = sb("mv", [P, NC, 2])
        var = sb("var", [P, NC])
        std = sb("std", [P, NC])
        rstd = sb("rstd", [P, NC])
        nmr = sb("nmr", [P, NC])
        lng = sb("lng", [P, 2, 2, K4])
        b1c = sb("b1c", [P, 16])
        rows = sb("rows", [P, 2, D])
        bqkv = wA[:, 6144:6144 + 3 * D]
        wqkv = wA[:, 0:K4 * 3 * D].rearrange("p (k n) -> p k n", k=K4)
        ETP, ETJ = 125, E // 125
        etab = aux[0:ETP, 0:ETJ * FEAT].rearrange("p (j f) -> p j f", f=FEAT)
        raw20 = aux[0:ETP, 2880:2880 + 1600].rearrange("p (j f) -> p j f", f=20)
        raw4 = aux[0:ETP, 4480:4480 + 320].rearrange("p (j f) -> p j f", f=4)
        raw8 = aux[0:ETP, 4800:4800 + 640].rearrange("p (j f) -> p j f", f=8)
        raw8b = aux[0:ETP, 5440:5440 + 640].rearrange("p (j f) -> p j f", f=8)
        rawt = aux[0:ETP, 6080:6160].bitcast(I32)
        raww = aux[0:ETP, 6160:6240]
        rawsd = aux[0:ETP, 6240:6400].bitcast(I32).rearrange("p (c j) -> p c j", c=2)
        wo = aux[:, 4096:4096 + K4 * D].rearrange("p (k n) -> p k n", k=K4)
        etab_d = nc.dram_tensor("etab_d", (E, FEAT), F32).ap()
        q_d = nc.dram_tensor("q_d", (NP, D), F32).ap()
        v_d = nc.dram_tensor("v_d", (NP, D), F32).ap()
        ends_d = nc.dram_tensor("ends_d", (112, 5), F32).ap()
        carry_d = nc.dram_tensor("carry_d", (112, 2), F32).ap()
        kH = bT_r[:, :].rearrange("p (m n) -> p m n", n=D)
        kf = work[:, 8192:8192 + NC * D].rearrange("p (m n) -> p m n", n=D)
        kL = work_r[:, 8192:8192 + NC * D].rearrange("p (m n) -> p m n", n=D)
        qv = aux[:, 0:2 * NC * D].rearrange("p (w m n) -> p w m n", w=2, m=NC)
        NB4 = NT // 4
        hot = work[:, 0:(NT + 4) * P // 2].bitcast(BF16).rearrange("p (t d) -> p t d", d=P)
        hTf = hT[:, :, :].rearrange("p k n -> p (k n)")
        hot4 = hTf[:, 0:3 * 4 * P].rearrange("p (k n) -> p k n", k=3)
        hotT = hT_r[:, :, :].rearrange("p k n -> p (k n)")[:, 0:3 * 4 * P].rearrange("p (k n) -> p k n", k=3)
        RING = 12
        ring = [buf[:, at:at + D] for buf, start in ((fT, 0), (aux, 6144), (aux, 8192)) for at in range(start, start + 4 * D, D)]
        msg = work[:, 5888:5888 + 4 * D].rearrange("p (s n) -> p s n", n=D)
        prod = [msg] + [aux[:, 2048 * j:2048 * (j + 1)].rearrange("p (s n) -> p s n", n=D) for j in range(2)]
        lg = sb("lg", [P, NT, H])
        lga = hTf[:, 1536:1536 + NT * H].rearrange("p (t h) -> p t h", h=H)
        TT, TG = 14, 6
        lgp, kp = (work[:, 5888 + 672 * j:5888 + 672 * (j + 1)].rearrange("p (g t h) -> p g t h", g=TG, t=TT) for j in range(2))
        aT = work[0:112, 7936:7936 + 768]
        kT = work[0:112, 8704:8704 + 768]
        pen = work[0:112, 9472:9472 + 769]
        fwd = work[0:112, 10496:10496 + 768]
        bwd = work[0:112, 11264:11264 + 768]
        ends = sb("ends", [112, 5])
        endh = sb("endh", [H, TT, 5])
        carh = sb("carh", [H, TT, 2])
        chd = sb("chd", [H, 4, TT])
        carry = sb("carry", [112, 2])
        agg = nrm
        sums = sb("sums", [P, NC, H])
        g1T = aux[:, 0:16 * NP].rearrange("p (j n) -> p j n", n=NP)
        w1s, w1_rest = (w[:, :].rearrange("p (k n) -> p k n", k=K4) for w in (wA, wA_r))
        w1_ring = [buf[:, at:at + K4 * P].rearrange("p (k n) -> p k n", n=P) for buf, first, count in ((work_r, 8192, 8), (fT_r, 0, 5))
                   for at in range(first, first + count * K4 * P, K4 * P)]
        h2_all, h2_rest = (t[:, :].rearrange("p (k n) -> p k n", n=NP) for t in (bT, bT_r))
        w2s = work[:, 0:16 * D].rearrange("p (k n) -> p k n", k=16)

        s_early_in = [sem(f"s_early_in{j}") for j in range(6)]
        s_early_job = sem("s_early_job")
        s_early_taken = sem("s_early_taken")
        s_early_out = sem("s_early_out")
        s_x = sem("s_x")
        s_xpad = sem("s_xpad")
        s_raw = sem("s_raw")
        s_table = sem("s_table")
        s_etab = sem("s_etab")
        s_par = sem("s_par")
        s_wqkv = sem("s_wqkv")
        s_var = sem("s_var")
        s_std = sem("s_std")
        s_stat = sem("s_stat")
        s_norm = sem("s_norm")
        s_job = sem("s_job")
        s_act = sem("s_act")
        s_by_act = sem("s_by_act")
        s_by_dve = sem("s_by_dve")
        s_q_out = sem("s_q_out")
        s_v_out = sem("s_v_out")
        PIECE = NT // 3
        s_att = [sem(f"s_att{j}") for j in range(3)]
        s_ids = sem("s_ids")
        s_hot = sem("s_hot")
        s_row_in = [sem(f"s_row_in{j}") for j in range(RING)]
        TURNS = NT // RING
        s_q_used = [sem(f"s_q_used{j}") for j in range(4)]
        s_hot4 = sem("s_hot4")
        s_hot4_used = [sem(f"s_hot4_used{k}") for k in range(3)]
        s_soft = sem("s_soft")
        s_h1b = sem("s_h1b")
        s_turned = sem("s_turned")
        s_hotT = sem("s_hotT")
        s_kg = sem("s_kg")
        s_reduced = sem("s_reduced")
        s_kH = sem("s_kH")
        s_kL = sem("s_kL")
        s_ak = sem("s_ak")
        s_akT = sem("s_akT")
        s_ends = sem("s_ends")
        s_ends_out = sem("s_ends_out")
        s_ends_in = sem("s_ends_in")
        s_carry = sem("s_carry")
        s_carry_out = sem("s_carry_out")
        s_carry_in = sem("s_carry_in")
        s_max = sem("s_max")
        s_maxT = sem("s_maxT")
        s_shift = sem("s_shift")
        s_prob = sem("s_prob")
        s_msg = [sem(f"s_msg{j}") for j in range(4)]
        s_msg_used = [sem(f"s_msg_used{j}") for j in range(4)]
        s_agg = sem("s_agg")
        s_aggn = sem("s_aggn")
        s_wo = sem("s_wo")
        s_w1 = sem("s_w1")
        s_w1_upper = sem("s_w1_upper")
        s_w1_rest = sem("s_w1_rest")
        s_h2_rest = sem("s_h2_rest")
        s_w2 = sem("s_w2")
        s_resid = sem("s_resid")
        plan = Plan([("ln1T", K4, "act"), ("qkv", 3 * NC, "dve"), ("aggT", K4, "act"), ("wo", NC, "dve"),
                     ("ln2T", K4, "act"), ("ffn1", 16, "act"), ("ffn2", NC, "dve")] + LATER,
                    {"act": s_by_act, "dve": s_by_dve})
        B1, F1, NF = 128, 32, 8 * 32
        half = sb("half", [P, 1])
        zf = wA[:, 0:21 * P]
        tf = wA[:, 21 * P:42 * P]
        ZPARTS = (slice(0, 12 * P), slice(12 * P, 21 * P))
        small_w = wA[:, 5376:8192]
        w_in = small_w[:, 0:64].rearrange("p (w f) -> p w f", w=2)
        w_f1 = small_w[0:FEAT, 64:96]
        w_f2 = small_w[:, 96:288]
        b_f2 = small_w[:, 288:480]
        w_bd = small_w[:, 1152:1664].rearrange("p (j n) -> p j n", n=P)
        b_fc = small_w[:, 1024:1152]
        w_o1s = small_w[0:64, 480:608]
        w_o1v = small_w[:, 608:736]
        w_o2 = small_w[:, 736:992].rearrange("p (w n) -> p w n", w=2)
        attT = work[0:FEAT, 0:NB4 * 4 * P].rearrange("p (g n) -> p g n", n=4 * P)
        filt = aux[:, :].rearrange("p (t n) -> p t n", n=P)
        uS = bT[:, 0:NC * P].rearrange("p (m n) -> p m n", n=P)
        u_d = nc.dram_tensor("u_d", (NP, P), F32).ap()
        ringu = fT[:, 0:12 * P].rearrange("p (s n) -> p s n", n=P)
        feat = work[:, 5120:5120 + 12 * NF].rearrange("p (s n) -> p s n", n=NF)
        featH = work_r[:, 9088:9088 + 12 * NF].rearrange("p (s n) -> p s n", n=NF)
        featL = wA_r[:, 0:12 * NF].rearrange("p (s n) -> p s n", n=NF)
        t1, t2, t3 = (work[:, 8192 + 128 * j:8192 + 128 * (j + 1)].rearrange("p (s f) -> p s f", f=F1) for j in range(3))
        t4 = work[:, 8576:8576 + 384].rearrange("p (s c f) -> p s c f", c=3, f=F1)
        t5 = work[:, 8960:8960 + 128].rearrange("p (s f) -> p s f", f=F1)
        agg1 = bT[:, 0:NC * NF].rearrange("p (m n) -> p m n", n=NF)
        oT = bT[:, :].rearrange("p (k n) -> p k n", n=NP)
        tz = fT[:, 0:NP]
        relr = bT[:, 0:2 * NT].rearrange("p (r t) -> p r t", r=2)
        srcf = sb("srcf", [P, NT])
        hotL = [work_r[:, 0:2560], work_r[:, 2560:5120], hT_r[:, :, :].rearrange("p k n -> p (k n)")]
        hotL = [h.rearrange("p (j n) -> p j n", n=NP) for h in hotL]
        hotS = work[:, 6400:6400 + 12 * NP // 2].bitcast(BF16).rearrange("p (s n) -> p s n", n=NP)
        hotD = fT[:, 0:12 * P // 2].bitcast(BF16).rearrange("p (s n) -> p s n", n=P)
        both, bymean = (work[:, 3200 * r:3200 * (r + 1)].rearrange("p (i n) -> p i n", n=NP) for r in range(2))
        adj = [aux[:, 3200 * r:3200 * (r + 1)].rearrange("p (i n) -> p i n", n=NP) for r in range(2)]
        deg = sb("deg", [P, NC])
        degd = fT[:, 0:NP]
        meanf = wA[:, 0:3200].rearrange("p (i n) -> p i n", n=NP)
        meanb = wA[:, 3200:6400].rearrange("p (i n) -> p i n", n=NP)
        LAYERS = 3

        def square(at):
            return work[:, at:at + K4 * D].rearrange("p (k n) -> p k n", n=D)
        w_all = [square(2048 * j) for j in range(3)]
        w_rest, w_upper = ([work_r[:, at + 2048 * j:at + 2048 * (j + 1)].rearrange("p (k n) -> p k n", n=D) for j in range(3)] for at in (0, 6144))

        def rests(aux, att, wA):
            at = [aux[:, NP * j:NP * (j + 1)] for j in range(10)] + [att[:, 2048:2048 + NP], wA[:, 7424:7424 + NP]]
            return [at[0:4], at[4:8], at[8:12]]

        t_all, t_rest = rests(aux, att, wA), rests(aux_r, att_r, wA_r)
        t_upper = [hT_r] + [t[:, :].rearrange("p (k n) -> p k n", n=NP) for t in (fT_r, bT_r)]
        adj_d = nc.dram_tensor("adj_d", (P, 6400), F32).ap()
        wsT, raw = square(8192), square(10240)
        NBASE = 30
        attb = sb("attb", [P, 2, 2 * NBASE])
        gw = sb("gw", [P, 2, 2, K4])
        gate = sb("gate", [P, NC, 2])
        root = [square(0), square(2048)]
        acc = aux[:, 6400:6400 + 4096].rearrange("p (r n) -> p r n", r=2)
        rel_w = [work[:, 4096:8192].rearrange("p (r n) -> p r n", r=2), acc]
        rel_d = nc.dram_tensor("rel_d", (P, 2, 4 * D), F32).ap()
        rel_r = [work_r[:, 4096:8192].rearrange("p (r n) -> p r n", r=2), aux_r[:, 6400:10496].rearrange("p (r n) -> p r n", r=2)]
        rel_upper = work_r[:, 8192:12288].rearrange("p (r n) -> p r n", r=2)

        def p_rests(att, wA):
            first = [wA[:, 5120:5760], wA[:, 5760:6400], wA[:, 7424:8064], att[:, 2048:2688]]
            return [first, [wA[:, NP * j:NP * (j + 1)] for j in range(4)]]

        p_all, p_rest = p_rests(att, wA), p_rests(att_r, wA_r)
        bas = [att[:, 0:1024], att[:, 1024:2048], wA[:, 6400:7424]]
        gx = wA[:, 0:2 * NC * D].rearrange("p (r m n) -> p r m n", r=2, m=NC)

        s_f1zero = sem("s_f1zero")
        s_l1w = sem("s_l1w")
        s_is3 = sem("s_is3")
        s_z = sem("s_z")
        s_ssp = sem("s_ssp")
        s_u_out = sem("s_u_out")
        s_u_used = [sem(f"s_u_used{k}") for k in range(3)]
        s_feat = sem("s_feat")
        s_feat_full = sem("s_feat_full")
        s_featH = sem("s_featH")
        s_feat_used = [sem(f"s_feat_used{k}") for k in range(3)]
        s_agg1 = sem("s_agg1")
        s_hs = [sem(f"s_hs{k}") for k in range(3)]
        s_hs_used = [sem(f"s_hs_used{k}") for k in range(3)]
        s_counts = sem("s_counts")
        s_adj = sem("s_adj")
        s_mean = sem("s_mean")
        s_rawin = sem("s_rawin")
        s_layer_in = sem("s_layer_in")
        s_w_upper = sem("s_w_upper")
        s_rest = sem("s_rest")
        s_adj_out = sem("s_adj_out")
        s_adj_in = sem("s_adj_in")
        s_free = sem("s_free")
        s_bas_in = [sem(f"s_bas_in{j}") for j in range(3)]
        s_bas_used = [sem(f"s_bas_used{j}") for j in range(3)]
        s_rel = sem("s_rel")
        s_rel_out = sem("s_rel_out")
        s_rel_in = sem("s_rel_in")
        s_l3par = sem("s_l3par")
        s_root = sem("s_root")
        s_gx = sem("s_gx")
        s_h3 = sem("s_h3")
        s_xb = sem("s_xb")
        s_x3 = sem("s_x3")
        s_out = sem("s_out")

        block = ctx.enter_context(nc.Block())

        @block.sync
        def _(sp):
            sp.wait_ge(s_fill, 1)
            sp.dma_start(dsti[0:ER - 1, :], a["dst"][0:(ER - 1) * P].rearrange("(p t) -> p t", t=P)).then_inc(s_edges_in, 16)
            sp.dma_start(dsti[ER - 1:ER, 0:ETAIL], a["dst"][(ER - 1) * P:E].rearrange("(p t) -> p t", p=1)).then_inc(s_edges_in, 16)

            def load_early(step):
                j = EARLY_IN[step]
                if j in EARLY_IN[:step]:
                    last = max(n for n in range(step) if EARLY_IN[n] == j)
                    sp.wait_ge(s_early_job, K4 * (last + 1))
                sp.dma_start(early_in[j], early_source(step)).then_inc(s_early_in[j], 16)

            def store_early(step):
                kind, l = EARLY[step]
                if kind in ("ws", "cf", "cb"):
                    sp.wait_ge(s_early_taken, K4 * (step + 1))
                    sp.dma_start(early_d[l, :, ("ws", "cf", "cb").index(kind)], early_out).then_inc(s_early_out, 16)

            for step in range(3):
                load_early(step)
            sp.wait_ge(s_xpad, 1)
            sp.dma_start(xs[:, 0:NC - 1, :], a["x"][0:(NC - 1) * P].rearrange("(m p) n -> p m n", p=P)).then_inc(s_x, 16)
            sp.dma_start(xs[0:LAST, NC - 1, :], a["x"][(NC - 1) * P:N]).then_inc(s_x, 16)
            for t, name in ((raw20, "edge_attr_20"), (raw4, "edge_attr_4"), (raw8, "edge_attr_8"), (raw8b, "edge_attr_8_n2")):
                sp.dma_start(t, a[name].rearrange("(p j) f -> p j f", p=ETP)).then_inc(s_raw, 16)
            sp.dma_start(rawt, a["edge_type_2"].rearrange("(p j) -> p j", p=ETP)).then_inc(s_raw, 16)
            sp.dma_start(raww, a["edge_weight"].rearrange("(p j) -> p j", p=ETP)).then_inc(s_raw, 16)
            sp.dma_start(rawsd[:, 0], a["src"].rearrange("(p j) -> p j", p=ETP)).then_inc(s_raw, 16)
            sp.dma_start(rawsd[:, 1], a["dst"].rearrange("(p j) -> p j", p=ETP)).then_inc(s_raw, 16)

            def load_qkv():
                sp.dma_start(wqkv, a["L0_gnn_Wqkv"].rearrange("(k p) n -> p k n", p=P)).then_inc(s_wqkv, 16)
                sp.dma_start(bqkv, a["L0_gnn_bqkv"].rearrange("(o n) -> o n", o=1).to_broadcast([P, 3 * D])).then_inc(s_wqkv, 16)

            with nc.allow_non_contiguous_dma(reason="a few columns of parameters"):
                for j, name in enumerate(("L0_gnn_ln1_g", "L0_gnn_ln1_b", "L0_gnn_ln2_g", "L0_gnn_ln2_b")):
                    sp.dma_start(lng[:, j // 2, j % 2, :], a[name].rearrange("(k p) -> p k", p=P)).then_inc(s_par, 16)
                sp.dma_start(b1c[:, :], a["L0_gnn_b1"].rearrange("(k p) -> p k", p=P)).then_inc(s_par, 16)
            for j, name in enumerate(("L0_gnn_bo", "L0_gnn_b2")):
                sp.dma_start(rows[:, j, :], a[name].rearrange("(o n) -> o n", o=1).to_broadcast([P, D])).then_inc(s_par, 16)
            sp.wait_ge(s_table, 1)
            sp.dma_start(etab_d.rearrange("(p j) f -> p j f", p=ETP), etab).then_inc(s_etab, 16)
            for step in range(SORTING):
                store_early(step)
                for n in range(3, SORTING):
                    if max(m for m in range(n) if EARLY_IN[m] == EARLY_IN[n]) == step:
                        load_early(n)
                if step == 3:
                    load_qkv()
            sp.wait_ge(s_by_dve, NC)
            sp.dma_start(q_d.rearrange("(m p) n -> p m n", p=P), qv[:, 0]).then_inc(s_q_out, 16)
            sp.wait_ge(s_by_dve, 3 * NC)
            sp.dma_start(v_d.rearrange("(m p) n -> p m n", p=P), qv[:, 1]).then_inc(s_v_out, 16)
            sp.wait_ge(s_v_out, 16)
            sp.dma_start(wo, a["L0_gnn_Wo"].rearrange("(k p) n -> p k n", p=P)).then_inc(s_wo, 16)
            for step in range(SORTING, SORTING + 3):
                load_early(step)
            with nc.allow_non_contiguous_dma(reason="a few numbers a block"):
                sp.wait_ge(s_ends, 1)
                sp.dma_start(ends_d, ends[:, :]).then_inc(s_ends_out, 16)
                sp.wait_ge(s_ends_out, 16)
                sp.dma_start(endh[:, :, :], ends_d.rearrange("(t h) v -> h t v", h=H)).then_inc(s_ends_in, 16)
                sp.wait_ge(s_carry, 1)
                sp.dma_start(carry_d.rearrange("(t h) v -> h t v", h=H), carh[:, :, :]).then_inc(s_carry_out, 16)
                sp.wait_ge(s_carry_out, 16)
                sp.dma_start(carry[:, :], carry_d).then_inc(s_carry_in, 16)
            sp.wait_ge(s_early_job, K4 * len(EARLY))
            sp.dma_start(w1s, a["L0_gnn_W1"].rearrange("(k p) n -> p k n", p=P)).then_inc(s_w1, 16)
            sp.wait_ge(s_agg, 1)
            sp.dma_start(w2s, a["L0_gnn_W2"].rearrange("(k p) n -> p k n", p=P)).then_inc(s_w2, 16)
            sp.wait_ge(s_f1zero, 1)
            for w, name in ((w_in[:, 0], "w_in2f_s"), (w_in[:, 1], "w_in2f_v"), (w_f1[0:20], "W1"), (w_o1s, "w_f2o1_s"),
                            (w_o1v[0:64], "w_f2o1_v"), (w_o1v[64:128], "w_f2o1_v"), (w_o2[:, 0], "w_f2o2_s"), (w_o2[:, 1], "w_f2o2_v")):
                sp.dma_start(w, a["L1_gnn_" + name]).then_inc(s_l1w, 16)
            sp.dma_start(w_f1[33:34], a["L1_gnn_b1"].rearrange("(o n) -> o n", o=1)).then_inc(s_l1w, 16)
            for j in range(4):
                sp.dma_start(w_f2[F1 * j:F1 * (j + 1)], a["L1_gnn_W2"]).then_inc(s_l1w, 16)
            sp.dma_start(b_f2, a["L1_gnn_b2"].rearrange("(o n) -> o n", o=1).to_broadcast([P, 192])).then_inc(s_l1w, 16)
            sp.wait_ge(s_by_act, plan.by[:plan.number("in2f", NC - 1)].count("act"))
            sp.dma_start(u_d.rearrange("(m p) n -> p m n", p=P), uS).then_inc(s_u_out, 16)
            for l in range(2):
                sp.dma_start(attb[:, l, :], a[f"L3_gnn_att{l + 1}"].rearrange("r b -> (r b)").rearrange("(o n) -> o n", o=1).to_broadcast([P, 2 * NBASE])).then_inc(s_l3par, 16)
                sp.dma_start(rows[:, l, :], a[f"L3_gnn_bias{l + 1}"].rearrange("(o n) -> o n", o=1).to_broadcast([P, D])).then_inc(s_l3par, 16)
                with nc.allow_non_contiguous_dma(reason="a few columns of parameters"):
                    for r in range(2):
                        sp.dma_start(gw[:, l, r, :], a[f"L3_gnn_gate_w{l + 1}"][r, :, 0].rearrange("(k p) -> p k", p=P)).then_inc(s_l3par, 16)
            sp.wait_ge(s_job, plan.number("o2", NC - 1))
            sp.dma_start(raw, a["L2_gnn_W_init"].rearrange("(k p) n -> p k n", p=P)).then_inc(s_rawin, 16)
            sp.wait_ge(s_adj, 2)
            sp.dma_start(adj_d, aux[:, 0:6400]).then_inc(s_adj_out, 16)
            sp.wait_ge(s_free, 1)
            sp.wait_ge(s_mean, 2)
            for l in range(2):
                halves = a[f"L3_gnn_basis{l + 1}"].rearrange("b (c k p) n -> b c p k n", c=2, p=P)
                with sp.Fori(0, NBASE // 3) as i:
                    for u in range(6):
                        sp.wait_ge(s_bas_used[u % 3], i * 2 + (l * 2 * NBASE // 3 + u // 3 + 1))
                        sp.dma_start(bas[u % 3].rearrange("p (o k n) -> p o k n", o=1, k=2),
                                     halves[bass.ds(i * 3 + u // 2, 1), u % 2].rearrange("o p k n -> p o k n")).then_inc(s_bas_in[u % 3], 16)
                if l == 0:
                    sp.wait_ge(s_rel, 1)
                    sp.dma_start(rel_d, acc).then_inc(s_rel_out, 16)
            sp.wait_ge(s_by_dve, plan.by.count("dve"))
            sp.dma_start(out[0:(NC - 1) * P].rearrange("(m p) n -> p m n", p=P), xs[:, 0:NC - 1, :]).then_inc(s_out, 16)
            sp.dma_start(out[(NC - 1) * P:N], xs[0:LAST, NC - 1, :]).then_inc(s_out, 16)
            sp.wait_ge(s_out, 32)

        @block.gpsimd
        def _(pool):
            step = Chain(pool, s_pool)
            pool.memset(dsti[:, :], NP).then_inc(s_fill, 1)
            step(pool.iota(iota[:, :], pattern=[[1, NP]], base=0, channel_multiplier=0,
                           allow_small_or_imprecise_dtypes=True))
            step(pool.tensor_copy(iota16[:, :], iota[:, :]))
            step(pool.iota(enum[:, :], pattern=[[1, P]], base=1, channel_multiplier=P,
                           allow_small_or_imprecise_dtypes=True))
            step(pool.memset(ones[:, :], 1.0))
            step(pool.memset(zeros[:, :], 0.0))
            for m in (ident, identb):
                step(pool.memset(m[:, :], 0.0))
                step(pool.affine_select(out=m[:, :], in_=m[:, :], compare_op=ALU.not_equal, fill=1.0,
                                        base=0, pattern=[[-1, P]], channel_multiplier=1))
            pool.affine_select(out=below[:, :], in_=ones[:, :], compare_op=ALU.is_gt, fill=0.0,
                               base=0, pattern=[[1, P]], channel_multiplier=-1).then_inc(s_const, 1)

            pool.memset(xs[:, NC - 1, :], 0.0).then_inc(s_xpad, 1)
            pool.wait_ge(s_raw, 128)
            pool.tensor_copy(etab[:, :, 0:20], raw20)
            pool.tensor_tensor(etab[:, :, 20:24], raw4, raww.unsqueeze(2).to_broadcast([ETP, ETJ, 4]), ALU.mult)
            pool.tensor_tensor(etab[:, :, 24:32], raw8, raw8b, ALU.add)
            pool.tensor_copy(etab[:, :, 32], rawt)
            pool.memset(etab[:, :, 33:34], 1.0)
            pool.tensor_copy(etab[:, :, 34], rawsd[:, 0])
            pool.tensor_copy(etab[:, :, 35], rawsd[:, 1]).then_inc(s_table, 1)
            pool.wait_ge(s_sorted, 1)
            pool.wait_ge(s_etab, 16)
            for t in range(NT):
                pool.indirect_dma_start(out=attr[:, t, :], out_offset=None, in_=etab_d,
                                        in_offset=bass.IndirectOffsetOnAxis(ap=eidx[:, t:t + 1], axis=0)).then_inc(s_att[t // PIECE], 16)
            pool.wait_ge(s_norm, 2)
            pool.wait_ge(s_par, 7 * 16)
            pool.tensor_tensor(hn[:, :, :], hn[:, :, :], rows[:, 0, :].unsqueeze(1).to_broadcast([P, NC, D]), ALU.add).then_inc(s_h1b, 1)
            pool.wait_ge(s_q_out, 16)
            for t in range(NT):
                if t % PIECE == 0:
                    pool.wait_ge(s_ids, t // PIECE + 1)
                if t >= RING:
                    pool.wait_ge(s_q_used[t % 4], (t - RING) // 4 + 2)
                pool.indirect_dma_start(out=ring[t % RING], out_offset=None, in_=q_d,
                                        in_offset=bass.IndirectOffsetOnAxis(ap=srcx[:, t:t + 1], axis=0)).then_inc(s_row_in[t % RING], 16)
            pool.wait_ge(s_v_out, 16)
            for t in range(NT):
                if t >= RING:
                    pool.wait_ge(s_msg[t % 4], (t - RING) // 4 + 1)
                else:
                    pool.wait_ge(s_q_used[t % 4], (NT - RING + t) // 4 + 2)
                pool.indirect_dma_start(out=ring[t % RING], out_offset=None, in_=v_d,
                                        in_offset=bass.IndirectOffsetOnAxis(ap=srcx[:, t:t + 1], axis=0)).then_inc(s_row_in[t % RING], 16)
            pool.wait_ge(s_norm, 3)
            step(pool.tensor_tensor(xs[:, :, :], xs[:, :, :], hn[:, :, :], ALU.add))
            pool.tensor_tensor(xs[:, :, :], xs[:, :, :], rows[:, 1, :].unsqueeze(1).to_broadcast([P, NC, D]), ALU.add).then_inc(s_resid, 1)
            pool.memset(half[:, :], 0.5)
            pool.wait_ge(s_job, plan.number("ffn1", 15))
            pool.memset(w_f1, 0.0).then_inc(s_f1zero, 1)
            pool.wait_ge(s_l1w, 14 * 16)
            pool.tensor_scalar(w_o1s[32:64], w_o1s[32:64], 3.0 ** -0.5, None, ALU.mult).then_inc(s_is3, 1)
            pool.wait_ge(s_u_out, 16)
            for t in range(NT):
                if t >= 12:
                    pool.wait_ge(s_u_used[t // 4 % 3], t // 12)
                pool.indirect_dma_start(out=ringu[:, t % 12, :], out_offset=None, in_=u_d,
                                        in_offset=bass.IndirectOffsetOnAxis(ap=dstx[:, t:t + 1], axis=0)).then_inc(s_row_in[t % 12], 16)
            def rest_of(name, all_of, rest, upper):
                for k in range(K4):
                    pool.wait_ge(s_by_act, plan.by[:plan.number(name, k)].count("act"))
                    pool.tensor_tensor(rest[k], all_of[k], upper[:, k, :], ALU.subtract).then_inc(s_rest, 1)

            for l in range(LAYERS):
                rest_of(("hT", "hT0", "hT1")[l], t_all[0], t_rest[0], t_upper[0])
                rest_of(f"F{l}", t_all[1], t_rest[1], t_upper[1])
                for j in range(3):
                    pool.wait_ge(s_w_upper, 3 * l + j + 1)
                    pool.tensor_tensor(w_rest[j], w_all[j], w_upper[j], ALU.subtract).then_inc(s_rest, 1)
                rest_of(f"B{l}", t_all[2], t_rest[2], t_upper[2])
            pool.wait_ge(s_norm, 6)
            pool.wait_ge(s_l3par, 8 * 16)
            pool.tensor_tensor(xs[:, :, :], xs[:, :, :], rows[:, 1, :].unsqueeze(1).to_broadcast([P, NC, D]), ALU.add).then_inc(s_xb, 1)
            for l in range(2):
                pool.wait_ge(s_w_upper, 3 * LAYERS + l + 1)
                for r in range(2):
                    pool.tensor_tensor(rel_r[l][:, r], rel_w[l][:, r], rel_upper[:, r], ALU.subtract).then_inc(s_rest, 1)
                for r in range(2):
                    rest_of(f"P{l}{r}", p_all[r], p_rest[r], t_upper[r + 1])

        @block.scalar
        def _(act):
            step = Chain(act, s_act)

            def norm(turn, dst, src, func):
                act.wait_ge(s_var, turn + 1)
                act.activation(std[:, :], var[:, :], ACT.Sqrt).then_inc(s_std, 1)
                act.wait_ge(s_stat, turn + 1)
                for m in range(NC):
                    last = act.activation(dst[:, m, :], src[:, m, :], func, bias=nmr[:, m:m + 1], scale=rstd[:, m:m + 1])
                last.then_inc(s_norm, 1)

            def take_turned(name, dst, count=K4, scale=None, shift=None):
                for k in range(count):
                    act.wait_ge(s_job, plan.number(name, k))
                    o = plan.slot(ps, name, k)[:, 0:NP]
                    if scale is None:
                        act.activation(dst[:, k, :], o, ACT.Copy).then_inc(s_by_act, 1)
                    else:
                        act.activation(dst[:, k, :], o, ACT.Identity, bias=shift[:, k:k + 1], scale=scale[:, k:k + 1]).then_inc(s_by_act, 1)

            def take_early(part):
                kind = EARLY[part][0]
                if kind in ("ws", "cf", "cb"):
                    stored = sum(n in ("ws", "cf", "cb") for n, _ in EARLY[:part])
                    if stored:
                        act.wait_ge(s_early_out, 16 * stored)
                for k in range(K4):
                    n = K4 * part + k
                    act.wait_ge(s_early_job, n + 1)
                    dst = early_s[part >= SORTING] if kind in ("sf", "sb") else early_out
                    act.activation(dst[:, k, :], early_bank(n), ACT.Copy).then_inc(s_early_taken, 1)
                if part >= SORTING:
                    if kind in ("ws", "cf", "cb"):
                        act.wait_ge(s_early_taken, K4 * (part + 1))
                        act.dma_start(early_d[2, :, ("ws", "cf", "cb").index(kind)], early_out).then_inc(s_early_out, 16)
                    if part + 3 < len(EARLY):
                        act.dma_start(early_in[EARLY_IN[part + 3]], early_source(part + 3)).then_inc(s_early_in[EARLY_IN[part + 3]], 16)

            for part in range(6):
                take_early(part)
            norm(0, hn, xs, ACT.Relu)
            take_early(6)
            take_early(7)
            norm(1, nrm, hn, ACT.Identity)
            take_early(8)
            take_early(9)
            act.wait_ge(s_par, 7 * 16)
            take_turned("ln1T", hT, scale=lng[:, 0, 0, :], shift=lng[:, 0, 1, :])
            act.wait_ge(s_by_dve, 2 * NC)
            act.wait_ge(s_early_out, 16 * 6)
            act.activation(kH, kf, ACT.Copy).then_inc(s_kH, 1)
            act.wait_ge(s_turned, 1)
            act.activation(hotT[:, 0, :], ps[:, 0:4 * P], ACT.Copy).then_inc(s_hotT, 1)
            with act.Fori(0, NB4 // 3) as i:
                for n in range(3):
                    k = (n + 1) % 3
                    act.wait_ge(s_turned, i * 3 + (n + 2))
                    act.activation(hotT[:, k, :], ps[:, 512 * k:512 * (k + 1)], ACT.Copy).then_inc(s_hotT, 1)
            act.wait_ge(s_akT, 1)
            act.activation(aT, ps[0:112, 0:768], ACT.Copy).then_inc(s_ak, 1)
            act.wait_ge(s_akT, 2)
            act.activation(kT, ps[0:112, 1024:1024 + 768], ACT.Copy).then_inc(s_ak, 1)
            for part in range(SORTING, SORTING + 3):
                take_early(part)
            act.wait_ge(s_shift, 1)
            act.activation(lg[:, :, :], lga[:, :, :], ACT.Exp).then_inc(s_prob, 1)
            for part in range(SORTING + 3, len(EARLY)):
                take_early(part)

            def widen():
                with act.Fori(0, NB4 // 3) as i:
                    for k in range(3):
                        act.wait_ge(s_hot4_used[k], i + 1)
                        act.activation(hot4[:, k, :].rearrange("p (t d) -> p t d", d=P),
                                       hot[:, bass.ds(i * 12 + 4 * k, 4), :], ACT.Copy).then_inc(s_hot4, 1)

            widen()
            take_turned("aggT", hT)
            def w1_upper(j):
                if j >= len(w1_ring):
                    act.wait_ge(s_job, plan.number("ffn1", j - len(w1_ring)))
                act.activation(w1_ring[j % len(w1_ring)], w1s[:, :, j * P:(j + 1) * P], ACT.Copy).then_inc(s_w1_upper, 1)

            act.wait_ge(s_w1, 16)
            for j in range(8):
                w1_upper(j)
            norm(2, nrm, hn, ACT.Identity)
            act.wait_ge(s_early_out, 16 * 9)
            for k in range(K4):
                act.wait_ge(s_job, plan.number("ln2T", k))
                o = plan.slot(ps, "ln2T", k)[:, 0:NP]
                act.activation(h2_all[:, k, :], o, ACT.Identity, bias=lng[:, 1, 1, k:k + 1], scale=lng[:, 1, 0, k:k + 1])
                act.activation(hT_r[:, k, :], o, ACT.Identity, bias=lng[:, 1, 1, k:k + 1], scale=lng[:, 1, 0, k:k + 1]).then_inc(s_by_act, 1)
            for j in range(16):
                if j < 8:
                    w1_upper(j + 8)
                act.wait_ge(s_job, plan.number("ffn1", j))
                act.activation(g1T[:, j, :].rearrange("p (c n) -> p c n", c=2), plan.slot(ps, "ffn1", j).rearrange("p (c n) -> p c n", c=2)[:, :, 0:NP // 2],
                               ACT.Gelu, bias=b1c[:, j:j + 1]).then_inc(s_by_act, 1)

            def take(name, j, dst, width=D, func=ACT.Copy, **how):
                act.wait_ge(s_job, plan.number(name, j))
                act.activation(dst, plan.slot(ps, name, j)[:, 0:width], func, **how).then_inc(s_by_act, 1)

            def softplus(z, t):
                step(act.activation(t, z, ACT.Abs))
                step(act.activation(t, t, ACT.Exp, scale=-1.0))
                act.activation(t, t, ACT.Ln, scale=0.5, bias=half[:, :]).then_inc(s_z, 1)

            def take_table(name, groups):
                for n, g in enumerate(groups):
                    act.wait_ge(s_job, plan.number(name, n))
                    act.activation(attT[:, g, :], plan.slot(ps, name, n)[0:FEAT, 0:4 * P], ACT.Copy).then_inc(s_by_act, 1)

            take_table("attA", range(ATT1))
            norm(3, hn, xs, ACT.Relu)
            take_turned("h1T", hT)
            act.wait_ge(s_early_out, 16 * 9)
            for m in range(NC):
                take("in2f", m, uS[:, m, :], P, scale=float(B1) ** -0.5)
            take_table("attB", range(ATT1, NB4))
            for g in range(7):
                take("hid", g, zf[:, 3 * P * g:3 * P * (g + 1)], 3 * P)
            act.wait_ge(s_is3, 1)
            for part, last in zip(ZPARTS, (3, 6)):
                act.wait_ge(s_by_act, plan.by[:plan.number("hid", last)].count("act"))
                softplus(zf[:, part], tf[:, part])
            with act.Fori(0, NB4 // 3) as i:
                for k in range(3):
                    act.wait_ge(s_feat_full, i * 3 + (k + 1))
                    act.activation(featH[:, 4 * k:4 * k + 4, :], feat[:, 4 * k:4 * k + 4, :], ACT.Copy).then_inc(s_featH, 1)
            act.wait_ge(s_agg, 2)
            act.activation(agg1, ps[:, 0:NC * 512].rearrange("p (m n) -> p m n", n=512)[:, :, 0:NF], ACT.Copy).then_inc(s_agg1, 1)
            take_turned("f2T", hT, 2)
            for k in range(4):
                take("o1", k, oT[:, k, :], NP, scale=0.125)
            act.wait_ge(s_by_act, plan.by[:plan.number("o1", 3)].count("act"))
            softplus(oT[:, 0, :], tz)
            norm(4, hn, xs, ACT.Relu)
            for r in range(2):
                act.wait_ge(s_counts, r + 1)
                act.activation(adj[r][:, :, 0:D], ps[:, 0:NC * D].rearrange("p (c n) -> p c n", n=D), ACT.Copy)
                act.activation(adj[r][:, :, D:NP], ps[:, NC * D:NC * D + NP].rearrange("p (c n) -> p c n", n=P), ACT.Copy).then_inc(s_adj, 1)
            for k in range(K4):
                take("wi", k, wsT[:, k, :])
            take_turned("h2T", hT)
            for m in range(NC):
                take("h0", m, hn[:, m, :], func=ACT.Relu)
            def take_split(name, all_of, upper):
                for k in range(K4):
                    act.wait_ge(s_job, plan.number(name, k))
                    o = plan.slot(ps, name, k)[:, 0:NP]
                    act.activation(all_of[k], o, ACT.Copy)
                    act.activation(upper[:, k, :], o, ACT.Copy).then_inc(s_by_act, 1)

            def load_layer(l):
                for j in range(3):
                    act.dma_start(w_all[j], early_d[l, :, j]).then_inc(s_layer_in, 16)

            act.wait_ge(s_adj_out, 16)
            act.wait_ge(s_mean, 1)
            take_split("hT", t_all[0], t_upper[0])
            for c in range(NC):
                take("meanT", c, meanf[:, c, :], NP)
            act.wait_ge(s_mean, 2)
            load_layer(0)
            for l in range(LAYERS):
                take_split(f"F{l}", t_all[1], t_upper[1])
                act.wait_ge(s_layer_in, 48 * (l + 1))
                for j in range(3):
                    act.activation(w_upper[j], w_all[j], ACT.Copy).then_inc(s_w_upper, 1)
                take_split(f"B{l}", t_all[2], t_upper[2])
                for m in range(NC):
                    take(f"L{l}", m, hn[:, m, :], func=ACT.Relu)
                if l < LAYERS - 1:
                    load_layer(l + 1)
                    take_split(f"hT{l}", t_all[0], t_upper[0])
            for l in range(2):
                act.dma_start(root[l], a[f"L3_gnn_root{l + 1}"].rearrange("(k p) n -> p k n", p=P)).then_inc(s_root, 16)
            act.dma_start(aux[:, 0:6400], adj_d).then_inc(s_adj_in, 16)
            act.wait_ge(s_rel_out, 16)
            act.dma_start(rel_w[0], rel_d).then_inc(s_rel_in, 16)
            norm(5, hn, xs, ACT.Relu)
            for l in range(2):
                take_turned(f"T{l}", hT)
                for m in range(NC):
                    take(f"gate{l}", m, gate[:, m, :], 2, ACT.Sigmoid)
                act.wait_ge(s_by_act, plan.by[:plan.number(f"gate{l}", NC - 1)].count("act"))
                for r in range(2):
                    for m in range(NC):
                        last = act.activation(gx[:, r, m, :], hn[:, m, :], ACT.Copy, scale=gate[:, m, r:r + 1])
                    last.then_inc(s_gx, 1)
                if l == 0:
                    act.wait_ge(s_rel_in, 16)
                else:
                    act.wait_ge(s_rel, 2)
                act.activation(rel_upper, rel_w[l], ACT.Copy).then_inc(s_w_upper, 1)
                for r in range(2):
                    take_split(f"P{l}{r}", p_all[r], t_upper[r + 1])

        @block.vector
        def _(dve):
            step = Chain(dve, s_dve)

            def rank(turn, bins):
                oh = onehot[:, 0:bins * P].rearrange("p (b t) -> p b t", t=P)
                pre = prefix[:, 0:bins * P].rearrange("p (b t) -> p b t", t=P)
                end, cnt, tot, excl, off, incl = (small[:, j, 0:bins] for j in range(6))
                step(dve.tensor_tensor(oh, key[:, :].unsqueeze(1).to_broadcast([ER, bins, P]),
                                       iota[0:ER, 0:bins].unsqueeze(2).to_broadcast([ER, bins, P]), ALU.is_equal))
                step(dve.tensor_tensor_scan(prefix[:, 0:bins * P], onehot[:, 0:bins * P], onehot[:, 0:bins * P],
                                            0.0, ALU.add, ALU.max))
                step(dve.tensor_copy(end, pre[:, :, P - 1]))
                step(dve.tensor_copy(cnt, end))
                dve.tensor_tensor(cnt[:, 1:bins], end[:, 1:bins], end[:, 0:bins - 1], ALU.subtract).then_inc(s_count, 1)
                dve.wait_ge(s_count, turn + 1)
                dve.wait_ge(s_prefix, turn + 1)
                above, every = ps[0:ER, 0:bins], ps[0:ER, 64:64 + bins]
                step(dve.tensor_copy(tot, every))
                step(dve.tensor_tensor_scan(incl, tot, tot, 0.0, ALU.add, ALU.max))
                step(dve.tensor_tensor(excl, incl, tot, ALU.subtract))
                step(dve.scalar_tensor_tensor(off, above, -1.0, cnt, ALU.add, ALU.add))
                step(dve.tensor_tensor(off, off, end, ALU.subtract))
                step(dve.tensor_tensor(off, off, excl, ALU.add))
                if turn == 1:
                    nch = bins // 4
                    ctot, cincl, cexcl = (small[:, 6, 8 * j:8 * j + nch] for j in range(3))
                    step(dve.tensor_reduce(ctot, tot.rearrange("p (c b) -> p c b", b=4), AX.X, ALU.add))
                    ci = chi[:, 0:nch]
                    step(dve.tensor_scalar(ci, ctot, float(P - 1), None, ALU.add))
                    step(dve.tensor_scalar(ci, ci, 7, 7, ALU.arith_shift_right, ALU.arith_shift_left))
                    step(dve.tensor_copy(ctot, ci))
                    step(dve.tensor_tensor_scan(cincl, ctot, ctot, 0.0, ALU.add, ALU.max))
                    step(dve.tensor_tensor(cexcl, cincl, ctot, ALU.subtract))
                    off4 = off.rearrange("p (c b) -> p c b", b=4)
                    first = excl.rearrange("p (c b) -> p c b", b=4)[:, :, 0]
                    step(dve.tensor_tensor(cincl, cexcl, first, ALU.subtract))
                    step(dve.tensor_tensor(off4, off4, cincl.unsqueeze(2).to_broadcast([ER, nch, 4]), ALU.add))
                    step(dve.tensor_scalar(cexcl, cexcl, 1.0 / P, None, ALU.mult))
                    step(dve.tensor_tensor(tch[:, :, :], iota[0:ER, 0:NT].unsqueeze(1).to_broadcast([ER, 4, NT]),
                                           cexcl[:, 1:NC].unsqueeze(2).to_broadcast([ER, NC - 1, NT]), ALU.is_ge))
                    step(dve.tensor_reduce(key[:, 0:NT], tch[:, :, :].rearrange("p c t -> p t c"), AX.X, ALU.add))
                    of4 = key[:, 0:NT].rearrange("p (g j) -> p g j", j=4)
                    packed = small[:, 7, 0:NT // 4]
                    step(dve.tensor_copy(packed, of4[:, :, 3]))
                    for j in (2, 1, 0):
                        step(dve.scalar_tensor_tensor(packed, packed, float(NC), of4[:, :, j], ALU.mult, ALU.add))
                    step(dve.tensor_copy(tchunk[:, :], packed))
                step(dve.tensor_tensor(pre, pre, off.unsqueeze(2).to_broadcast([ER, bins, P]), ALU.add))
                step(dve.tensor_tensor(pre, pre, oh, ALU.mult))
                step(dve.tensor_reduce(pos[:, :], pre.rearrange("p b t -> p t b"), AX.X, ALU.add))
                step(dve.tensor_copy(posi[:, :], pos[:, :]))
                step(dve.tensor_scalar(digi[:, 0, :], posi[:, :], 7, None, ALU.arith_shift_right))
                step(dve.tensor_scalar(digi[:, 1, :], posi[:, :], P - 1, None, ALU.bitwise_and))
                dve.tensor_copy(dig[:, :, :], digi[:, :, :]).then_inc(s_ranked, 1)
                dve.wait_ge(s_ranked, turn + 1)

            def write_hots(by, turn, rows, cols):
                with dve.Fori(0, P // 8) as i:
                    for half in range(2):
                        dve.wait_ge(s_hot_read[half], i + (turn * (P // 8) + 1))
                        four = slice(4 * half, 4 * half + 4)
                        dve.tensor_tensor(rowhot[:, four, 0:rows], iota[0:ER, 0:rows].unsqueeze(1).to_broadcast([ER, 4, rows]),
                                          dig[:, by, bass.ds(i * 8 + 4 * half, 4)].unsqueeze(2).to_broadcast([ER, 4, rows]), ALU.is_equal)
                        for j in range(4):
                            at = bass.ds(i * 8 + (4 * half + j), 1)
                            last = dve.tensor_scalar(colhot[:, 4 * half + j, 0:cols], iota[0:ER, 0:cols], dig[:, 1 - by, at],
                                                     load[:, at], ALU.is_equal, ALU.mult)
                        last.then_inc(s_hots[half], 1)

            dve.wait_ge(s_edges_in, 32)
            dve.wait_ge(s_const, 1)
            step(dve.tensor_scalar(loadi[:, :], dsti[:, :], 5, None, ALU.arith_shift_right))
            step(dve.scalar_tensor_tensor(load[:, :], dsti[:, :], float(NP), enum[:, :], ALU.is_lt, ALU.mult))
            step(dve.scalar_tensor_tensor(load[:, :], load[:, :], 32.0, loadi[:, :], ALU.mult, ALU.add))
            step(dve.tensor_scalar(keyi[:, :], dsti[:, :], LO_BINS - 1, None, ALU.bitwise_and))
            step(dve.tensor_copy(key[:, :], keyi[:, :]))
            rank(0, LO_BINS)
            write_hots(0, 0, ER, P)
            dve.wait_ge(s_permuted, 1)
            step(dve.tensor_copy(load[:, :], ps[0:ER, 512:512 + P]))
            step(dve.tensor_copy(loadi[:, :], ps[0:ER, 512:512 + P]))
            step(dve.tensor_scalar(keyi[:, :], loadi[:, :], 31, None, ALU.bitwise_and))
            step(dve.tensor_copy(key[:, :], keyi[:, :]))
            rank(1, HI_BINS)
            write_hots(1, 1, P, NT)
            dve.wait_ge(s_permuted, 2)
            step(dve.tensor_copy(reli[:, :], ps[:, 1024:1024 + NT]))
            step(dve.tensor_scalar(reli[:, :], reli[:, :], 5, None, ALU.arith_shift_right))
            dve.tensor_scalar(real[:, :], reli[:, :], 0.0, None, ALU.is_gt)
            dve.tensor_scalar(eidx[:, :], reli[:, :], -1.0, 0.0, ALU.add, ALU.max).then_inc(s_sorted, 1)

            def stats(turn, src, write=None):
                written = []
                for m in range(NC + 1):
                    if write and m < NC:
                        written.append(write(m))
                    if m > 0:
                        if write:
                            dve.wait_ge(*written[m - 1])
                        last = dve.bn_stats(bst[:, m - 1, :], src[:, m - 1, :])
                step(last)
                for m in range(NC):
                    last = dve.bn_aggr(mv[:, m, :], bst[:, m, :])
                step(last)
                dve.tensor_scalar(var[:, :], mv[:, :, 1], 1e-5, None, ALU.add).then_inc(s_var, 1)
                dve.wait_ge(s_std, turn + 1)
                step(dve.reciprocal(rstd[:, :], std[:, :]))
                dve.scalar_tensor_tensor(nmr[:, :], mv[:, :, 0], -1.0, rstd[:, :], ALU.mult, ALU.mult).then_inc(s_stat, 1)

            dve.wait_ge(s_x, 32)
            stats(0, xs)
            dve.wait_ge(s_norm, 1)
            stats(1, hn)
            dve.wait_ge(s_wqkv, 32)
            dve.wait_ge(s_etab, 16)
            for n, dst in enumerate((qv[:, 0], kf, qv[:, 1])):
                for m in range(NC):
                    dve.wait_ge(s_job, plan.number("qkv", n * NC + m))
                    dve.tensor_tensor(dst[:, m, :], plan.slot(ps, "qkv", n * NC + m)[:, 0:D], bqkv[:, n * D:(n + 1) * D],
                                      ALU.add).then_inc(s_by_dve, 1)
                dve.wait_ge(s_att[n], 16 * PIECE)
                at = slice(n * PIECE, (n + 1) * PIECE)
                step(dve.tensor_copy(srcx[:, at], attr[:, at, 34]))
                dve.tensor_copy(dstx[:, at], attr[:, at, 35]).then_inc(s_ids, 1)
                dve.wait_ge(s_ids, n + 1)
                step(dve.tensor_scalar(reli[:, at], dstx[:, at], P - 1, None, ALU.bitwise_and))
                step(dve.scalar_tensor_tensor(rel[:, at], reli[:, at], 1.0, real[:, at], ALU.add, ALU.mult))
                step(dve.tensor_scalar(rel[:, at], rel[:, at], -1.0, None, ALU.add))
                if n == 0:
                    step(dve.memset(hot[:, NT:NT + 4, :], 0.0))
                dve.tensor_tensor(hot[:, at, :], iota[:, 0:P].unsqueeze(1).to_broadcast([P, PIECE, P]),
                                  rel[:, at].unsqueeze(2).to_broadcast([P, PIECE, P]), ALU.is_equal).then_inc(s_hot, 1)
                if n == 1:
                    dve.wait_ge(s_kH, 1)
                    dve.tensor_tensor(kL, kf, kH, ALU.subtract).then_inc(s_kL, 1)
            step(dve.scalar_tensor_tensor(segk[:, :], dstx[:, :], 1.0, real[:, :], ALU.add, ALU.mult))
            for j in range(4):
                dve.nop().then_inc(s_q_used[j], 1)
            dve.wait_ge(s_q_out, 16)
            dve.wait_ge(s_v_out, 16)
            with dve.Fori(0, NB4 // 3) as i:

                def multiply(k):
                    for j in range(4):
                        dve.wait_ge(s_row_in[4 * k + j], i * 16 + 16)
                        dve.wait_ge(s_kg, i * 12 + (4 * k + j + 1))
                        dve.tensor_tensor(prod[k][:, j, :], ring[4 * k + j], ps[:, 512 * (4 + j):512 * (5 + j)], ALU.mult).then_inc(s_q_used[j], 1)

                def reduce(k):
                    dve.wait_ge(s_q_used[3], i * 3 + (k + 2))
                    dve.tensor_reduce(lg[:, bass.ds(i * 12 + 4 * k, 4), :], prod[k].rearrange("p s (h d) -> p (s h) d", d=DH),
                                      AX.X, ALU.add).then_inc(s_reduced, 1)

                multiply(0)
                multiply(1)
                reduce(0)
                multiply(2)
                reduce(1)
                reduce(2)
                dve.wait_ge(s_reduced, i * 3 + 2)
            dve.wait_ge(s_reduced, NB4)
            step(dve.scalar_tensor_tensor(lg[:, :, :], lg[:, :, :], float(D) ** -0.5, attr[:, :, 24:32], ALU.mult, ALU.add))
            dve.tensor_copy(lgp.rearrange("p g t h -> p t g h"), lg[:, :, :].rearrange("p (t g) h -> p t g h", g=TG))
            dve.tensor_copy(kp.rearrange("p g t h -> p t g h"),
                            segk[:, :].rearrange("p (t g) -> p t g", g=TG).unsqueeze(3).to_broadcast([P, TT, TG, H])).then_inc(s_soft, 1)
            dve.wait_ge(s_ak, 2)
            step(dve.memset(pen[:, :], 0.0))
            step(dve.tensor_tensor(pen[:, 1:768], kT[:, 1:768], kT[:, 0:767], ALU.not_equal))
            step(dve.tensor_scalar(pen[:, 1:768], pen[:, 1:768], -BIG, None, ALU.mult))

            def scans(start_f, start_b):
                dve.tensor_tensor_scan(fwd[:, :], pen[:, 0:768], aT[:, :], start_f, ALU.add, ALU.max)
                step(dve.tensor_tensor_scan(bwd[:, ::-1], pen[:, 768:0:-1], aT[:, ::-1], start_b, ALU.add, ALU.max))

            scans(-BIG, -BIG)
            dve.tensor_copy(ends[:, 0:1], fwd[:, 767:768])
            dve.tensor_copy(ends[:, 1:2], bwd[:, 0:1])
            dve.tensor_copy(ends[:, 2:3], kT[:, 0:1])
            dve.tensor_copy(ends[:, 3:4], kT[:, 767:768])
            dve.tensor_reduce(ends[:, 4:5], pen[:, 0:768], AX.X, ALU.min).then_inc(s_ends, 1)
            dve.wait_ge(s_ends_in, 16)
            seam, hop, run_f, run_b = (chd[:, j, :] for j in range(4))
            step(dve.memset(chd[:, :, :], 0.0))
            step(dve.memset(carh[:, :, :], -BIG))
            step(dve.tensor_tensor(seam[:, 1:TT], endh[:, 1:TT, 2], endh[:, 0:TT - 1, 3], ALU.not_equal))
            step(dve.tensor_scalar(seam, seam, -BIG, None, ALU.mult))
            step(dve.tensor_tensor(hop, seam, endh[:, :, 4], ALU.add))
            step(dve.tensor_tensor_scan(run_f, hop, endh[:, :, 0], -BIG, ALU.add, ALU.max))
            step(dve.tensor_tensor(carh[:, 1:TT, 0], run_f[:, 0:TT - 1], seam[:, 1:TT], ALU.add))
            step(dve.tensor_copy(hop, endh[:, :, 4]))
            step(dve.tensor_tensor(hop[:, 0:TT - 1], hop[:, 0:TT - 1], seam[:, 1:TT], ALU.add))
            step(dve.tensor_tensor_scan(run_b[:, ::-1], hop[:, ::-1], endh[:, ::-1, 1], -BIG, ALU.add, ALU.max))
            step(dve.tensor_tensor(carh[:, 0:TT - 1, 1], run_b[:, 1:TT], seam[:, 1:TT], ALU.add))
            step(dve.tensor_scalar(carh[:, :, :], carh[:, :, :], -BIG, None, ALU.max))
            dve.nop().then_inc(s_carry, 1)
            dve.wait_ge(s_carry_in, 16)
            scans(carry[:, 0:1], carry[:, 1:2])
            dve.tensor_tensor(aT[:, :], fwd[:, :], bwd[:, :], ALU.max).then_inc(s_max, 1)
            dve.wait_ge(s_maxT, 1)
            top = ps[:, 2048:2048 + TG * P].rearrange("p (g q) -> p g q", q=P)[:, :, 0:112]
            dve.tensor_tensor(lga[:, :, :].rearrange("p (t g) h -> p t g h", g=TG), lg[:, :, :].rearrange("p (t g) h -> p t g h", g=TG),
                              top.rearrange("p g (t h) -> p t g h", h=H), ALU.subtract).then_inc(s_shift, 1)
            dve.wait_ge(s_prob, 1)
            with dve.Fori(0, NT // RING) as i:
                for t in range(RING):
                    j = t % 4
                    dve.wait_ge(s_row_in[t], i * 16 + 16 * (TURNS + 1))
                    dve.wait_ge(s_msg_used[j], i * 3 + (t // 4 + 1))
                    dve.tensor_tensor(msg[:, j, :].rearrange("p (h d) -> p h d", d=DH), ring[t].rearrange("p (h d) -> p h d", d=DH),
                                      lg[:, bass.ds(i * RING + t, 1), :].rearrange("p o h -> p (o h)").unsqueeze(2).to_broadcast([P, H, DH]), ALU.mult).then_inc(s_msg[j], 1)
            dve.wait_ge(s_agg, 1)
            step(dve.tensor_scalar(sums[:, :, :], ps[:, 2560:2560 + NC * H].rearrange("p (m h) -> p m h", h=H), 0.5, None, ALU.max))
            step(dve.reciprocal(sums[:, :, :], sums[:, :, :]))
            for m in range(NC):
                last = dve.tensor_tensor(agg[:, m, :].rearrange("p (h d) -> p h d", d=DH), ps[:, 512 * m:512 * (m + 1)].rearrange("p (h d) -> p h d", d=DH),
                                         sums[:, m, :].unsqueeze(2).to_broadcast([P, H, DH]), ALU.mult)
            last.then_inc(s_aggn, 1)
            def rest_of_w1(columns):
                for j in columns:
                    dve.wait_ge(s_w1_upper, j + 1)
                    w = slice(j * P, (j + 1) * P)
                    dve.tensor_tensor(w1_rest[:, :, w], w1s[:, :, w], w1_ring[j % len(w1_ring)], ALU.subtract).then_inc(s_w1_rest, 1)

            rest_of_w1(range(5))
            dve.wait_ge(s_h1b, 1)

            def add_sums(name, dst):
                def write(m):
                    dve.wait_ge(s_job, plan.number(name, m))
                    dve.tensor_tensor(dst[:, m, :], plan.slot(ps, name, m)[:, 0:D], dst[:, m, :], ALU.add).then_inc(s_by_dve, 1)
                    return s_by_dve, plan.by[:plan.number(name, m)].count("dve")
                return write

            stats(2, hn, add_sums("wo", hn))
            rest_of_w1(range(5, 8))
            for k in range(K4):
                dve.wait_ge(s_by_act, plan.by[:plan.number("ln2T", k)].count("act"))
                dve.tensor_tensor(h2_rest[:, k, :], h2_all[:, k, :], hT_r[:, k, :], ALU.subtract).then_inc(s_h2_rest, 1)
            rest_of_w1(range(8, 16))
            dve.wait_ge(s_resid, 1)
            stats(3, xs, add_sums("ffn2", xs))
            dve.wait_ge(s_is3, 1)
            step(dve.memset(small_w[:, 1152:1664], 0.0))
            for j in range(4):
                lanes = slice(F1 * j, F1 * (j + 1))
                step(dve.tensor_copy(w_bd[lanes, j, :].rearrange("p (c f) -> p c f", f=F1),
                                     w_f2[lanes].rearrange("p (f c) -> p c f", c=6)[:, 0:4, :]))
            for n, part in enumerate(ZPARTS):
                dve.wait_ge(s_z, n + 1)
                dve.scalar_tensor_tensor(zf[:, part], zf[:, part], 0.0, tf[:, part], ALU.max, ALU.add).then_inc(s_ssp, 1)
            step(dve.tensor_copy(b_fc.rearrange("p (c f) -> p c f", f=F1), b_f2.rearrange("p (f c) -> p c f", c=6)[:, 0:4, :]))
            for g in range(NB4):
                dve.wait_ge(s_job, plan.number("filt", g))
                dve.tensor_tensor(filt[:, g:g + 63 + 1:21, :], plan.slot(ps, "filt", g)[:, 0:4 * P].rearrange("p (j n) -> p j n", n=P),
                                  b_fc.unsqueeze(1).to_broadcast([P, 4, P]), ALU.add).then_inc(s_by_dve, 1)
            dve.wait_ge(s_by_dve, plan.by[:plan.number("filt", NB4 - 1)].count("dve"))
            step(dve.scalar_tensor_tensor(srcf[:, :], srcx[:, :], 1.0, real[:, :], ALU.add, ALU.mult))
            step(dve.tensor_scalar(srcf[:, :], srcf[:, :], -1.0, None, ALU.add))
            with dve.Fori(0, NB4 // 3) as i:
                step.enter(i, 6)
                for k in range(3):
                    for j in range(4):
                        dve.wait_ge(s_row_in[4 * k + j], i * 16 + 16 * (2 * TURNS + 1))
                    dve.wait_ge(s_feat_used[k], i + 1)
                    u = ringu[:, 4 * k:4 * k + 4, :]
                    s = u[:, :, 0:F1]
                    v = u[:, :, F1:P].rearrange("p s (c f) -> p s c f", c=3)
                    w = filt[:, bass.ds(i * 12 + 4 * k, 4), :]
                    y = attr[:, bass.ds(i * 12 + 4 * k, 4), 20:24]
                    ys = y[:, :, 0:1].to_broadcast([P, 4, F1])
                    yv = y[:, :, 1:4].unsqueeze(3).to_broadcast([P, 4, 3, F1])
                    f = feat[:, 4 * k:4 * k + 4, :]
                    fv = f[:, :, 2 * F1:NF].rearrange("p s (c w f) -> p s c w f", c=3, w=2)
                    dve.tensor_tensor(t1, w[:, :, 0:F1], ys, ALU.mult)
                    dve.tensor_tensor(t2, w[:, :, 2 * F1:3 * F1], s, ALU.mult)
                    dve.tensor_tensor(t3, w[:, :, 3 * F1:4 * F1], ys, ALU.mult)
                    step(dve.tensor_tensor(t4, v, yv, ALU.mult))
                    dve.tensor_tensor(f[:, :, 0:F1], t1, s, ALU.mult)
                    dve.tensor_tensor(fv[:, :, :, 0, :], t2.unsqueeze(2).to_broadcast([P, 4, 3, F1]), yv, ALU.mult)
                    dve.tensor_tensor(fv[:, :, :, 1, :], t3.unsqueeze(2).to_broadcast([P, 4, 3, F1]), v, ALU.mult).then_inc(s_u_used[k], 1)
                    step(dve.tensor_reduce(t5, t4.rearrange("p s c f -> p s f c"), AX.X, ALU.add))
                    dve.tensor_tensor(f[:, :, F1:2 * F1], t5, w[:, :, F1:2 * F1], ALU.mult).then_inc(s_feat_full, 1)
                    for j in range(4):
                        dve.tensor_scalar(hotL[k][:, j, :], iota[:, :], srcf[:, bass.ds(i * 12 + (4 * k + j), 1)], None, ALU.is_equal)
                    dve.wait_ge(s_featH, i * 3 + (k + 1))
                    dve.tensor_tensor(featL[:, 4 * k:4 * k + 4, :], f, featH[:, 4 * k:4 * k + 4, :], ALU.subtract).then_inc(s_feat, 1)
            step.leave(NB4 // 3)
            dve.wait_ge(s_z, 3)
            dve.scalar_tensor_tensor(oT[:, 0, :], oT[:, 0, :], 0.0, tz, ALU.max, ALU.add).then_inc(s_ssp, 1)
            for m in range(NC):
                dve.wait_ge(s_job, plan.number("o2", m))
                o = plan.slot(ps, "o2", m)
                dve.scalar_tensor_tensor(xs[:, m, 0:B1], o[:, 0:B1], float(B1) ** -0.5, xs[:, m, 0:B1], ALU.mult, ALU.add)
                xv = xs[:, m, B1:D].rearrange("p (d c) -> p c d", c=3)
                dve.scalar_tensor_tensor(xv, o[:, B1:D].rearrange("p (c d) -> p c d", c=3), float(B1) ** -0.5, xv, ALU.mult, ALU.add).then_inc(s_by_dve, 1)
            dve.wait_ge(s_by_dve, plan.by[:plan.number("o2", NC - 1)].count("dve"))
            stats(4, xs)
            step(dve.tensor_scalar(relr[:, 0, :], attr[:, :, 32], 0.0, None, ALU.is_equal))
            step(dve.tensor_scalar(relr[:, 1, :], attr[:, :, 32], 0.0, None, ALU.not_equal))
            for r in range(2):
                step(dve.scalar_tensor_tensor(relr[:, r, :], rel[:, :], 1.0, relr[:, r, :], ALU.add, ALU.mult))
                step(dve.tensor_scalar(relr[:, r, :], relr[:, r, :], -1.0, None, ALU.add))
            dve.nop().then_inc(s_free, 1)
            for r in range(2):
                with dve.Fori(0, NB4 // 3) as i:
                    for k in range(3):
                        dve.wait_ge(s_hs_used[k], i + (r * NB4 // 3 + 1))
                        for j in range(4 * k, 4 * k + 4):
                            at = bass.ds(i * 12 + j, 1)
                            dve.tensor_scalar(hotS[:, j, :], iota16[:, :], srcf[:, at], None, ALU.is_equal)
                            last = dve.tensor_scalar(hotD[:, j, :], iota16[:, 0:P], relr[:, r, at], None, ALU.is_equal)
                        last.then_inc(s_hs[k], 1)
            dve.wait_ge(s_adj, 2)
            step(dve.tensor_tensor(both, adj[0], adj[1], ALU.add))
            step(dve.tensor_reduce(deg[:, :], both, AX.X, ALU.add))
            step(dve.tensor_scalar(deg[:, :], deg[:, :], 1.0, None, ALU.max))
            step(dve.reciprocal(deg[:, :], deg[:, :]))
            dve.tensor_tensor(bymean, both, deg[:, :].unsqueeze(2).to_broadcast([P, NC, NP]), ALU.mult).then_inc(s_mean, 1)
            dve.wait_ge(s_job, plan.number("deg", 0))
            dve.tensor_scalar(degd, plan.slot(ps, "deg", 0)[:, 0:NP], 1.0, None, ALU.max).then_inc(s_by_dve, 1)
            dve.wait_ge(s_by_dve, plan.by[:plan.number("deg", 0)].count("dve"))
            step(dve.reciprocal(degd, degd))
            dve.tensor_tensor(meanb, both, degd.unsqueeze(1).to_broadcast([P, NC, NP]), ALU.mult).then_inc(s_mean, 1)

            def combine(l, first, turns):
                if first == 0:
                    step(dve.memset(acc, 0.0))
                done = step.n - 6 * first
                with dve.Fori(first, first + turns) as i:
                    for u in range(6):
                        part = slice(u % 2 * 1024, u % 2 * 1024 + 1024)
                        dve.wait_ge(s_bas_in[u % 3], i * 32 + (16 * (l * 2 * NBASE // 3 + u // 3) + 16))
                        for r in range(2):
                            if r == 0:
                                dve.wait_ge(s_dve, i * 6 + (done + u - 1))
                            else:
                                dve.wait_ge(s_bas_used[(u - 2) % 3], i * 2 + (l * 2 * NBASE // 3 + (u - 2) // 3 + 2))
                            dve.scalar_tensor_tensor(acc[:, r, part], bas[u % 3], attb[:, l, bass.ds(i * 3 + (u // 2 + r * NBASE), 1)],
                                                     acc[:, r, part], ALU.mult, ALU.add).then_inc((s_dve, s_bas_used[u % 3])[r], 1)
                step.n += 6 * turns
                dve.wait_ge(s_dve, step.n)
                for j in range(1, 3):
                    dve.wait_ge(s_bas_used[j], 2 * (first + turns) + l * 2 * NBASE // 3 + 1)
                if first + turns == NBASE // 3:
                    dve.nop().then_inc(s_rel, 1)

            dve.wait_ge(s_l3par, 8 * 16)
            for j in range(3):
                dve.nop().then_inc(s_bas_used[j], 1)
            combine(0, 0, NBASE // 3)
            dve.wait_ge(s_rel_out, 16)
            combine(1, 0, 4)
            def add_h(m):
                dve.wait_ge(s_by_act, plan.by[:plan.number(f"L{LAYERS - 1}", m)].count("act"))
                dve.tensor_tensor(xs[:, m, :], xs[:, m, :], hn[:, m, :], ALU.add).then_inc(s_x3, 1)
                return s_x3, m + 1

            stats(5, xs, add_h)
            combine(1, 4, NBASE // 3 - 4)
            for m in range(NC):
                dve.wait_ge(s_job, plan.number("O0", m))
                dve.tensor_tensor(hn[:, m, :], plan.slot(ps, "O0", m)[:, 0:D], rows[:, 0, :], ALU.add).then_inc(s_by_dve, 1)
            dve.wait_ge(s_by_dve, plan.by[:plan.number("O0", NC - 1)].count("dve"))
            dve.tensor_scalar(hn[:, :, :], hn[:, :, :], 0.0, None, ALU.max).then_inc(s_h3, 1)
            dve.wait_ge(s_xb, 1)
            for m in range(NC):
                dve.wait_ge(s_job, plan.number("O1", m))
                dve.tensor_tensor(xs[:, m, :], plan.slot(ps, "O1", m)[:, 0:D], xs[:, m, :], ALU.add).then_inc(s_by_dve, 1)

        @block.tensor
        def _(pe):
            def counts(turn, bins):
                pe.wait_ge(s_count, turn + 1)
                cnt = small[:, 1, 0:bins]
                pe.matmul(ps[0:ER, 0:bins], below[0:ER, 0:ER], cnt, start=True, stop=True)
                pe.matmul(ps[0:ER, 64:64 + bins], ones[0:ER, 0:ER], cnt, start=True, stop=True).then_inc(s_prefix, 1)

            def permute(turn, rows, cols):
                bank = ps[0:rows, 512 * (turn + 1):512 * (turn + 1) + cols]
                pe.matmul(bank, zeros[0:ER, 0:rows], zeros[0:ER, 0:cols], start=True, stop=False)
                with pe.Fori(0, P // 8) as i:
                    for half in range(2):
                        pe.wait_ge(s_hots[half], i + (turn * (P // 8) + 1))
                        for j in range(4 * half, 4 * half + 4):
                            last = pe.matmul(bank, rowhot[:, j, 0:rows], colhot[:, j, 0:cols], start=False, stop=False)
                        last.then_inc(s_hot_read[half], 1)
                pe.matmul(bank, zeros[0:ER, 0:rows], zeros[0:ER, 0:cols], start=False, stop=True).then_inc(s_permuted, 1)

            for half in range(2):
                pe.nop().then_inc(s_hot_read[half], 1)
            def prepare(steps):
                for step in steps:
                    kind, j = EARLY[step][0], EARLY_IN[step]
                    w = early_in[j]
                    pe.wait_ge(s_early_in[j], 16 * EARLY_IN[:step + 1].count(j))
                    if kind[0] == "c":
                        pe.wait_ge(s_early_taken, K4 * step)
                    for k in range(K4):
                        n = K4 * step + k
                        banks = 5 if step < SORTING else 2
                        if n >= banks:
                            pe.wait_ge(s_early_taken, n - banks + 1)
                        to = early_bank(n)
                        for o in range(K4):
                            if kind[0] == "c":
                                last = pe.matmul(to, w[:, o, k * P:(k + 1) * P], early_s[step >= SORTING][:, o, :], start=o == 0, stop=o == K4 - 1)
                            else:
                                last = pe.transpose(to[:, o * P:(o + 1) * P], w[:, o, k * P:(k + 1) * P], ident[:, :])
                        last.then_inc(s_early_job, 1)

            pe.wait_ge(s_const, 1)
            prepare(range(0, 2))
            counts(0, LO_BINS)
            prepare(range(2, 4))
            permute(0, ER, P)
            counts(1, HI_BINS)
            prepare(range(4, 6))
            permute(1, P, NT)
            prepare(range(6, 10))

            def turn_nodes(name, src, count=K4, cols=lambda k: slice(k * P, (k + 1) * P)):
                for k in range(count):
                    plan.open(pe, name, k)
                    o = plan.slot(ps, name, k)
                    for m in range(NC):
                        last = pe.transpose(o[:, m * P:(m + 1) * P], src[:, m, cols(k)], ident[:, :])
                    last.then_inc(s_job, 1)

            def product(name, j, width, pairs):
                plan.open(pe, name, j)
                o = plan.slot(ps, name, j)
                for at in range(0, width, D):
                    to = min(at + D, width)
                    for n, (lhsT, rhs) in enumerate(pairs):
                        last = pe.matmul(o[:, at:to], lhsT, rhs[:, at:to], start=n == 0, stop=n == len(pairs) - 1)
                last.then_inc(s_job, 1)

            def node(t, k, m):
                return t[:, k, m * P:(m + 1) * P]

            pe.wait_ge(s_norm, 2)
            pe.wait_ge(s_early_taken, K4 * SORTING)
            turn_nodes("ln1T", nrm)
            pe.wait_ge(s_wqkv, 32)
            for n in range(3):
                for m in range(NC):
                    if m == 0 and n == 0:
                        plan.wait_taken(pe, plan.number("ln1T", K4 - 1) - 1)
                    product("qkv", n * NC + m, D, [(node(hT, k, m), wqkv[:, k, n * D:(n + 1) * D]) for k in range(K4)])
            plan.wait_taken(pe, plan.number("qkv", 3 * NC - 1) - 1)
            pe.wait_ge(s_hot, 3)
            pe.wait_ge(s_kL, 1)

            def tile_chunks(g):
                four = pe.value_load(tchunk[0:1, bass.ds(g, 1)], min_val=0, max_val=NC ** 4 - 1)
                return [four // NC ** j % NC for j in range(4)]

            for j in range(4):
                last = pe.matmul(ps[:, j * P:(j + 1) * P], hot[:, j, :], identb[:, :], start=True, stop=True)
            last.then_inc(s_turned, 1)
            with pe.Fori(0, NB4 // 3) as i:
                for k in range(3):
                    to = (k + 1) % 3
                    for j in range(4):
                        last = pe.matmul(ps[:, 512 * to + j * P:512 * to + (j + 1) * P],
                                         hot[:, bass.ds(i * 12 + (4 * k + 4 + j), 1), :].rearrange("p o d -> p (o d)"), identb[:, :],
                                         start=True, stop=True)
                    last.then_inc(s_turned, 1)
                    chunks = tile_chunks(i * 3 + k)
                    pe.wait_ge(s_hotT, i * 3 + (k + 1))
                    for j, c in enumerate(chunks):
                        pe.wait_ge(s_q_used[j], i * 3 + (k + 1))
                        for n, part in enumerate((kH, kL)):
                            last = pe.matmul(ps[:, 512 * (4 + j):512 * (5 + j)], hotT[:, k, j * P:(j + 1) * P],
                                             part[:, bass.ds(c, 1), :].rearrange("p o n -> p (o n)"), start=n == 0, stop=n == 1)
                        last.then_inc(s_kg, 1)
            pe.wait_ge(s_soft, 1)
            pe.wait_ge(s_hotT, NB4 + 1)
            for n, src in enumerate((lgp, kp)):
                for g in range(TG):
                    last = pe.transpose(ps[0:112, 1024 * n + g * P:1024 * n + (g + 1) * P], src[:, g].rearrange("p t h -> p (t h)"), ident[:, :])
                last.then_inc(s_akT, 1)
            prepare(range(SORTING, SORTING + 3))
            pe.wait_ge(s_max, 1)
            for g in range(TG):
                last = pe.transpose(ps[:, 2048 + g * P:2048 + g * P + 112], aT[:, g * P:(g + 1) * P], ident[0:112, 0:112])
            last.then_inc(s_maxT, 1)

            def open_sums(width, banks=NC):
                for m in range(banks):
                    pe.matmul(ps[:, 512 * m:512 * m + width], zeros[:, 0:P], iota[:, 0:width], start=True, stop=False)

            def close_sums(width, banks=NC):
                for m in range(banks):
                    last = pe.matmul(ps[:, 512 * m:512 * m + width], zeros[:, 0:P], iota[:, 0:width], start=False, stop=True)
                return last

            prepare(range(SORTING + 3, len(EARLY)))
            pe.wait_ge(s_prob, 1)
            pe.wait_ge(s_const, 1)
            for used in s_msg_used + s_hot4_used:
                pe.nop().then_inc(used, 1)
            open_sums(D)
            pe.matmul(ps[:, 2560:2560 + NC * H], zeros[:, 0:P], iota[:, 0:NC * H], start=True, stop=False)
            with pe.Fori(0, NB4 // 3) as i:
                for k in range(3):
                    chunks = tile_chunks(i * 3 + k)
                    pe.wait_ge(s_hot4, i * 3 + (k + 1))
                    for j, c in enumerate(chunks):
                        pe.wait_ge(s_msg[j], i * 3 + (k + 1))
                        one = hot4[:, k, j * P:(j + 1) * P]
                        pe.matmul(ps[:, bass.ds(c * 512, D)], one, msg[:, j, :], start=False, stop=False, skip_group_check=True)\
                          .then_inc(s_msg_used[j], 1)
                        last = pe.matmul(ps[:, bass.ds(c * H + 2560, H)], one, lg[:, bass.ds(i * 12 + (4 * k + j), 1), :].rearrange("p o h -> p (o h)"),
                                         start=False, stop=False, skip_group_check=True)
                    last.then_inc(s_hot4_used[k], 1)
            close_sums(D)
            pe.matmul(ps[:, 2560:2560 + NC * H], zeros[:, 0:P], iota[:, 0:NC * H], start=False, stop=True).then_inc(s_agg, 1)
            pe.wait_ge(s_aggn, 1)
            turn_nodes("aggT", agg)
            pe.wait_ge(s_wo, 16)
            plan.wait_taken(pe, plan.number("aggT", K4 - 1) - 1)
            for m in range(NC):
                product("wo", m, D, [(node(hT, k, m), wo[:, k, :]) for k in range(K4)])
            pe.wait_ge(s_norm, 3)
            turn_nodes("ln2T", nrm)
            pe.wait_ge(s_w1, 16)
            pe.wait_ge(s_h2_rest, K4)
            for j in range(16):
                pe.wait_ge(s_w1_rest, j + 1)
                plan.open(pe, "ffn1", j)
                for c in range(2):
                    o = plan.slot(ps, "ffn1", j)[:, 512 * c:512 * c + NP // 2]
                    nodes = slice(c * NP // 2, (c + 1) * NP // 2)
                    for k in range(K4):
                        upper, rest = w1_ring[j % len(w1_ring)][:, k, :], w1_rest[:, k, j * P:(j + 1) * P]
                        for n, (w, h) in enumerate(((upper, hT_r), (upper, h2_rest), (rest, hT_r))):
                            last = pe.matmul(o, w, h[:, k, nodes], start=k == n == 0, stop=(k, n) == (K4 - 1, 2))
                last.then_inc(s_job, 1)
            pe.wait_ge(s_w2, 16)
            plan.wait_taken(pe, plan.number("ffn1", 15) - 1)
            for m in range(NC):
                product("ffn2", m, D, [(node(g1T, j, m), w2s[:, j, :]) for j in range(16)])

            def taken(name, j):
                plan.wait_taken(pe, plan.number(name, j) - 1)

            def turn_table(name, groups):
                for n, g in enumerate(groups):
                    plan.open(pe, name, n)
                    for j in range(4):
                        last = pe.transpose(plan.slot(ps, name, n)[0:FEAT, j * P:(j + 1) * P], attr[:, j * NB4 + g, :], ident[:, :])
                    last.then_inc(s_job, 1)

            turn_table("attA", range(ATT1))
            pe.wait_ge(s_norm, 4)
            turn_nodes("h1T", hn, cols=lambda k: slice(0, P) if k == 0 else slice(P + k - 1, D, 3))
            pe.wait_ge(s_is3, 1)
            taken("h1T", K4 - 1)
            for m in range(NC):
                plan.open(pe, "in2f", m)
                for k in range(K4):
                    last = pe.matmul(plan.slot(ps, "in2f", m)[:, F1 * k:F1 * (k + 1)], node(hT, k, m), w_in[:, min(k, 1)], start=True, stop=True)
                last.then_inc(s_job, 1)
            turn_table("attB", range(ATT1, NB4))
            taken("attB", NB4 - ATT1 - 1)
            for g3 in range(7):
                plan.open(pe, "hid", g3)
                for g in range(3):
                    for j in range(4):
                        last = pe.matmul(plan.slot(ps, "hid", g3)[F1 * j:F1 * (j + 1), g * P:(g + 1) * P], w_f1,
                                         attT[:, 3 * g3 + g, j * P:(j + 1) * P], start=True, stop=True)
                last.then_inc(s_job, 1)
            for g in range(NB4):
                if g in (0, 12):
                    pe.wait_ge(s_ssp, 1 + g // 12)
                plan.open(pe, "filt", g)
                pe.matmul(plan.slot(ps, "filt", g)[:, 0:4 * P], zf[:, g * P:(g + 1) * P], small_w[:, 1152:1664], start=True, stop=True).then_inc(s_job, 1)
            for j in range(4):
                taken("filt", NB4 - 1 - j)
            for used in s_feat_used:
                pe.nop().then_inc(used, 1)
            open_sums(NF)
            with pe.Fori(0, NB4 // 3) as i:
                for k in range(3):
                    pe.wait_ge(s_feat, i * 3 + (k + 1))
                    for j in range(4):
                        for m in range(NC):
                            for part in (featH, featL):
                                last = pe.matmul(ps[:, 512 * m:512 * m + NF], hotL[k][:, j, m * P:(m + 1) * P], part[:, 4 * k + j, :],
                                                 start=False, stop=False)
                    last.then_inc(s_feat_used[k], 1)
            close_sums(NF).then_inc(s_agg, 1)
            pe.wait_ge(s_agg1, 1)
            turn_nodes("f2T", agg1, 2)
            taken("f2T", 1)
            product("o1", 0, NP, [(w_o1s, hT[0:64, 0, :])])
            for c in range(3):
                lanes = slice(64, 128) if c % 2 == 0 else slice(0, 64)
                product("o1", 1 + c, NP, [(w_o1v[lanes], hT[lanes, (c + 1) // 2, :])])
            pe.wait_ge(s_ssp, 3)
            taken("o1", 3)
            for m in range(NC):
                plan.open(pe, "o2", m)
                for k in range(4):
                    last = pe.matmul(plan.slot(ps, "o2", m)[:, k * P:(k + 1) * P], node(oT, k, m), w_o2[:, min(k, 1)], start=True, stop=True)
                last.then_inc(s_job, 1)
            for j in range(4):
                taken("o2", NC - 1 - j)
            for used in s_hs_used:
                pe.nop().then_inc(used, 1)
            for r in range(2):
                if r:
                    pe.wait_ge(s_adj, 1)
                open_sums(D, 7)
                with pe.Fori(0, NB4 // 3) as i:
                    for k in range(3):
                        chunks = tile_chunks(i * 3 + k)
                        pe.wait_ge(s_hs[k], i + (r * NB4 // 3 + 1))
                        for j, c in enumerate(chunks):
                            pe.matmul(ps[:, bass.ds(c * D, D)], hotD[:, 4 * k + j, :], hotS[:, 4 * k + j, 0:D],
                                      start=False, stop=False, skip_group_check=True)
                            last = pe.matmul(ps[:, bass.ds(c * P + NC * D, P)], hotD[:, 4 * k + j, :], hotS[:, 4 * k + j, D:NP],
                                             start=False, stop=False, skip_group_check=True)
                        last.then_inc(s_hs_used[k], 1)
                close_sums(D, 7).then_inc(s_counts, 1)
            def turn_weights(name, n):
                pe.wait_ge(s_rawin, 16 * n)
                for k in range(K4):
                    plan.open(pe, name, k)
                    for o in range(K4):
                        last = pe.transpose(plan.slot(ps, name, k)[:, o * P:(o + 1) * P], raw[:, o, k * P:(k + 1) * P], ident[:, :])
                    last.then_inc(s_job, 1)

            pe.wait_ge(s_norm, 5)
            pe.wait_ge(s_adj, 2)
            turn_weights("wi", 1)
            turn_nodes("h2T", hn)
            taken("h2T", K4 - 1)
            for m in range(NC):
                product("h0", m, D, [(node(hT, k, m), wsT[:, k, :]) for k in range(K4)])
            taken("h0", NC - 1)
            turn_nodes("hT", hn)
            pe.wait_ge(s_mean, 1)
            product("deg", 0, NP, [(ones[:, :], both[:, i, :]) for i in range(NC)])
            for c in range(NC):
                plan.open(pe, "meanT", c)
                for i in range(NC):
                    last = pe.transpose(plan.slot(ps, "meanT", c)[:, i * P:(i + 1) * P], bymean[:, i, c * P:(c + 1) * P], ident[:, :])
                last.then_inc(s_job, 1)
            taken("meanT", NC - 1)
            pe.wait_ge(s_mean, 2)
            for l in range(LAYERS):
                for name, mean in (("F", meanf), ("B", meanb)):
                    for k in range(K4):
                        product(f"{name}{l}", k, NP, [(hn[:, i, k * P:(k + 1) * P], mean[:, i, :]) for i in range(NC)])
                pe.wait_ge(s_rest, 15 * l + 11)
                for m in range(NC):
                    plan.open(pe, f"L{l}", m)
                    o = plan.slot(ps, f"L{l}", m)[:, 0:D]
                    for j in range(3):
                        if m == 0 and j == 2:
                            pe.wait_ge(s_rest, 15 * l + 15)
                        for k in range(K4):
                            upper, rest = node(t_upper[j], k, m), t_rest[j][k][:, m * P:(m + 1) * P]
                            for n, (lhsT, rhs) in enumerate(((upper, w_upper[j]), (upper, w_rest[j]), (rest, w_upper[j]))):
                                last = pe.matmul(o, lhsT, rhs[:, k, :], start=j == k == n == 0, stop=(j, k, n) == (2, K4 - 1, 2))
                    last.then_inc(s_job, 1)
                if l < LAYERS - 1:
                    taken(f"L{l}", NC - 1)
                    turn_nodes(f"hT{l}", hn)
            for l in range(2):
                if l == 0:
                    pe.wait_ge(s_norm, 6)
                    pe.wait_ge(s_root, 32)
                    pe.wait_ge(s_l3par, 8 * 16)
                else:
                    pe.wait_ge(s_h3, 1)
                turn_nodes(f"T{l}", hn)
                taken(f"T{l}", K4 - 1)
                for m in range(NC):
                    product(f"gate{l}", m, 2, [(node(hT, k, m), gw[:, l, :, k]) for k in range(K4)])
                if l == 0:
                    pe.wait_ge(s_adj_in, 16)
                for r in range(2):
                    pe.wait_ge(s_gx, 2 * l + r + 1)
                    for k in range(K4):
                        product(f"P{l}{r}", k, NP, [(gx[:, r, i, k * P:(k + 1) * P], adj[r][:, i, :]) for i in range(NC)])
                for m in range(NC):
                    plan.open(pe, f"O{l}", m)
                    o = plan.slot(ps, f"O{l}", m)[:, 0:D]
                    for k in range(K4):
                        pe.matmul(o, node(hT, k, m), root[l][:, k, :], start=k == 0, stop=False)
                    for r in range(2):
                        if m == 0:
                            pe.wait_ge(s_rest, 15 * LAYERS + 10 * l + 4 * r + 6)
                        for k in range(K4):
                            upper, rest = node(t_upper[r + 1], k, m), p_rest[r][k][:, m * P:(m + 1) * P]
                            w = slice(k * D, (k + 1) * D)
                            for n, (lhsT, rhs) in enumerate(((upper, rel_upper), (upper, rel_r[l]), (rest, rel_upper))):
                                last = pe.matmul(o, lhsT, rhs[:, r, w], start=False, stop=(r, k, n) == (1, K4 - 1, 2))
                    last.then_inc(s_job, 1)


_INS = ['x', 'src', 'dst', 'edge_attr_20', 'edge_attr_4', 'edge_attr_8', 'edge_attr_8_n2', 'edge_type_2',
        'edge_weight', 'L0_gnn_Wqkv', 'L0_gnn_bqkv', 'L0_gnn_Wo', 'L0_gnn_bo', 'L0_gnn_ln1_g', 'L0_gnn_ln1_b',
        'L0_gnn_W1', 'L0_gnn_b1', 'L0_gnn_W2', 'L0_gnn_b2', 'L0_gnn_ln2_g', 'L0_gnn_ln2_b', 'L1_gnn_w_in2f_s',
        'L1_gnn_w_in2f_v', 'L1_gnn_W1', 'L1_gnn_b1', 'L1_gnn_W2', 'L1_gnn_b2', 'L1_gnn_w_f2o1_s',
        'L1_gnn_w_f2o1_v', 'L1_gnn_w_f2o2_s', 'L1_gnn_w_f2o2_v', 'L2_gnn_W_init', 'L2_gnn_W_fwd', 'L2_gnn_W_bwd',
        'L2_gnn_W_self', 'L3_gnn_basis1', 'L3_gnn_att1', 'L3_gnn_gate_w1', 'L3_gnn_root1', 'L3_gnn_bias1',
        'L3_gnn_basis2', 'L3_gnn_att2', 'L3_gnn_gate_w2', 'L3_gnn_root2', 'L3_gnn_bias2']


def kernel(**inputs):
    import numpy as _np
    import concourse.bacc as _bacc
    from concourse import mybir as _mybir
    from concourse.bass_utils import run_bass_kernel_spmd as _run

    nc = _bacc.Bacc("TRN2", target_bir_lowering=False, num_devices=1)
    arrays, args = {}, {}
    for name in _INS:
        a = _np.ascontiguousarray(inputs[name])
        arrays[f"in_{name}"] = a
        args[name] = nc.dram_tensor(f"in_{name}", a.shape, _mybir.dt.from_np(a.dtype), kind="ExternalInput").ap()
    out = nc.dram_tensor("out_x", (N, D), F32, kind="ExternalOutput").ap()
    build(nc, args, out)
    r = _run(nc, [arrays], core_ids=[0])
    return r.results[0]["out_x"]
```
